# Optimizing a Trainium2 kernel written in Bass

```python
import numpy as np
import jax
import jax.numpy as jnp

def _softmax(x, axis=-1):
    return jax.nn.softmax(x, axis=axis)

def _gelu(x):
    return jax.nn.gelu(x, approximate=True)

def _silu(x):
    return jax.nn.silu(x)

def _sigmoid(x):
    return jax.nn.sigmoid(x)

def _layernorm(x, axis=-1, eps=1e-05):
    m = jnp.mean(x, axis=axis, keepdims=True)
    v = jnp.var(x, axis=axis, keepdims=True)
    return (x - m) / jnp.sqrt(v + eps)

def _scatter_add(tgt, idx, src, axis=0):
    return tgt.at[idx].add(src)

def _segment_sum(src, seg, n):
    return jax.ops.segment_sum(src, seg, n)
kernel_name = 'mk_seq_postln_d2_jaxref_r8_2f73bf'

def setup_inputs(seed: int=0):
    np.random.seed(seed)
    _w = jnp.asarray

    def _L0_attn_setup():
        import jax, jax.numpy as jnp
        import numpy as np
        B, N, C, H = (4, 1024, 128, 16)
        D = C // H
        key = jax.random.key(seed)
        k1, k2, k3 = jax.random.split(key, 3)
        scale_in = 1.0 / np.sqrt(C)
        return {'x': jax.random.normal(k1, (B, N, C), dtype=jnp.float32), 'w_qkv': jax.random.normal(k2, (C, 3 * C), dtype=jnp.float32) * scale_in, 'b_qkv': jnp.zeros((3 * C,), dtype=jnp.float32), 'w_proj': jax.random.normal(k3, (C, C), dtype=jnp.float32) * scale_in, 'b_proj': jnp.zeros((C,), dtype=jnp.float32)}
    _L0_attn_in = _L0_attn_setup()

    def _L0_ffn_setup():
        import jax, jax.numpy as jnp
        import numpy as np
        import math
        E = 8
        K = 2
        CF = 1.2
        D = 128
        H = 512
        key = jax.random.key(seed)
        k0, k1, k2, k3 = jax.random.split(key, 4)
        B, T = (8, 256)
        x_btd = jax.random.normal(k0, (B, T, D), jnp.float32)
        Wr = jax.random.normal(k1, (D, E), jnp.float32) / np.sqrt(D)
        br = jnp.zeros((E,), jnp.float32)
        W1 = jax.random.normal(k2, (E, D, H), jnp.float32) / np.sqrt(D)
        b1 = jnp.zeros((E, H), jnp.float32)
        W2 = jax.random.normal(k3, (E, H, D), jnp.float32) / np.sqrt(H)
        b2 = jnp.zeros((E, D), jnp.float32)
        return dict(x_btd=x_btd, Wr=Wr, br=br, W1=W1, b1=b1, W2=W2, b2=b2)
    _L0_ffn_in = _L0_ffn_setup()

    def _L1_attn_setup():
        import math
        import jax, jax.numpy as jnp
        import numpy as np
        B, T, D, H = (2, 256, 128, 16)
        N_LAYERS = 24

        def get_slopes(n):

            def pow2(n):
                start = 2 ** (-2 ** (-(math.log2(n) - 3)))
                return [start * start ** i for i in range(n)]
            if math.log2(n).is_integer():
                return pow2(n)
            c = 2 ** math.floor(math.log2(n))
            return pow2(c) + get_slopes(2 * c)[0::2][:n - c]
        key = jax.random.key(seed)
        ks = jax.random.split(key, 5)
        x = jax.random.normal(ks[0], (B, T, D), dtype=jnp.float32)
        Wq = 0.02 * jax.random.normal(ks[1], (D, D), dtype=jnp.float32)
        Wk = 0.02 * jax.random.normal(ks[2], (D, D), dtype=jnp.float32)
        Wv = 0.02 * jax.random.normal(ks[3], (D, D), dtype=jnp.float32)
        Wo = 0.02 / math.sqrt(2 * N_LAYERS) * jax.random.normal(ks[4], (D, D), dtype=jnp.float32)
        z = jnp.zeros((D,), dtype=jnp.float32)
        return {'x': x, 'Wq': Wq, 'bq': z, 'Wk': Wk, 'bk': z, 'Wv': Wv, 'bv': z, 'Wo': Wo, 'bo': z}
    _L1_attn_in = _L1_attn_setup()

    def _L1_ffn_setup():
        import jax, jax.numpy as jnp
        import numpy as np
        TOPK = 4
        key = jax.random.key(seed)
        ks = jax.random.split(key, 9)
        B, T, D = (4, 256, 128)
        E, H = (32, 128)
        HS = H * TOPK
        s = lambda k, shape, fan: jax.random.normal(k, shape, dtype=jnp.float32) / np.sqrt(fan)
        return {'x': jax.random.normal(ks[0], (B, T, D), dtype=jnp.float32), 'router_w': s(ks[1], (E, D), D), 'router_bias': jnp.zeros((E,), dtype=jnp.float32), 'gate_w': s(ks[2], (E, H, D), D), 'up_w': s(ks[3], (E, H, D), D), 'down_w': s(ks[4], (E, D, H), H), 'sgate_w': s(ks[5], (HS, D), D), 'sup_w': s(ks[6], (HS, D), D), 'sdown_w': s(ks[7], (D, HS), HS)}
    _L1_ffn_in = _L1_ffn_setup()
    _d = {'L0_attn_x': _L0_attn_in['x'], 'L0_attn_w_qkv': _L0_attn_in['w_qkv'], 'L0_attn_b_qkv': _L0_attn_in['b_qkv'], 'L0_attn_w_proj': _L0_attn_in['w_proj'], 'L0_attn_b_proj': _L0_attn_in['b_proj'], 'L0_ffn_Wr': _L0_ffn_in['Wr'], 'L0_ffn_br': _L0_ffn_in['br'], 'L0_ffn_W1': _L0_ffn_in['W1'], 'L0_ffn_b1': _L0_ffn_in['b1'], 'L0_ffn_W2': _L0_ffn_in['W2'], 'L0_ffn_b2': _L0_ffn_in['b2'], 'L1_attn_Wq': _L1_attn_in['Wq'], 'L1_attn_bq': _L1_attn_in['bq'], 'L1_attn_Wk': _L1_attn_in['Wk'], 'L1_attn_bk': _L1_attn_in['bk'], 'L1_attn_Wv': _L1_attn_in['Wv'], 'L1_attn_bv': _L1_attn_in['bv'], 'L1_attn_Wo': _L1_attn_in['Wo'], 'L1_attn_bo': _L1_attn_in['bo'], 'L1_ffn_router_w': _L1_ffn_in['router_w'], 'L1_ffn_router_bias': _L1_ffn_in['router_bias'], 'L1_ffn_gate_w': _L1_ffn_in['gate_w'], 'L1_ffn_up_w': _L1_ffn_in['up_w'], 'L1_ffn_down_w': _L1_ffn_in['down_w'], 'L1_ffn_sgate_w': _L1_ffn_in['sgate_w'], 'L1_ffn_sup_w': _L1_ffn_in['sup_w'], 'L1_ffn_sdown_w': _L1_ffn_in['sdown_w']}
    _x0 = _d['L0_attn_x']
    _d['L0_attn_x'] = jax.random.normal(jax.random.fold_in(jax.random.key(seed), 1), (4, 1024, 128), dtype=_x0.dtype)
    del _x0
    return _d

def reference(L0_attn_x, L0_attn_w_qkv, L0_attn_b_qkv, L0_attn_w_proj, L0_attn_b_proj, L0_ffn_Wr, L0_ffn_br, L0_ffn_W1, L0_ffn_b1, L0_ffn_W2, L0_ffn_b2, L1_attn_Wq, L1_attn_bq, L1_attn_Wk, L1_attn_bk, L1_attn_Wv, L1_attn_bv, L1_attn_Wo, L1_attn_bo, L1_ffn_router_w, L1_ffn_router_bias, L1_ffn_gate_w, L1_ffn_up_w, L1_ffn_down_w, L1_ffn_sgate_w, L1_ffn_sup_w, L1_ffn_sdown_w):

    def _L0_attn_ref(x, w_qkv, b_qkv, w_proj, b_proj):
        import jax, jax.numpy as jnp
        import numpy as np
        B, N, C, H = (4, 1024, 128, 16)
        D = C // H
        Bx, Nx, Cx = x.shape
        qkv = x @ w_qkv + b_qkv
        qkv = qkv.reshape(Bx, Nx, 3, H, D)
        qkv = jnp.transpose(qkv, (2, 0, 3, 1, 4))
        q, k, v = (qkv[0], qkv[1], qkv[2])
        q = jax.nn.elu(q) + 1.0
        k = jax.nn.elu(k) + 1.0
        kv = jnp.einsum('bhnd,bhne->bhde', k, v)
        out = jnp.einsum('bhnd,bhde->bhne', q, kv)
        z = 1.0 / (jnp.einsum('bhnd,bhd->bhn', q, k.sum(axis=2)) + 1e-08)
        out = out * z[..., None]
        out = jnp.transpose(out, (0, 2, 1, 3)).reshape(Bx, Nx, Cx)
        out = out @ w_proj + b_proj
        return out

    def _L0_ffn_ref(x_btd, Wr, br, W1, b1, W2, b2):
        import jax, jax.numpy as jnp
        import numpy as np
        import math
        E = 8
        K = 2
        CF = 1.2
        D = 128
        H = 512
        B, T, Dm = x_btd.shape
        N = B * T
        x = x_btd.reshape(N, Dm)
        cap = int(math.ceil(CF * N / E))
        probs = jax.nn.softmax(x @ Wr + br, axis=-1)
        gates, ids = jax.lax.top_k(probs, K)
        flat_ids = ids.reshape(-1)
        flat_g = gates.reshape(-1)
        M = N * K
        order = jnp.lexsort((-flat_g, flat_ids))
        s_ids = flat_ids[order]
        s_tok = (order // K).astype(jnp.int32)
        s_g = flat_g[order]
        counts = jnp.bincount(flat_ids, length=E)
        starts = jnp.concatenate([jnp.zeros((1,), counts.dtype), jnp.cumsum(counts)[:-1]])
        rank = jnp.arange(M) - starts[s_ids]
        valid = rank < cap
        pos = jnp.where(valid, s_ids * cap + rank, E * cap)
        disp_tok = jnp.zeros((E * cap + 1,), jnp.int32).at[pos].set(s_tok)[:E * cap]
        disp_g = jnp.zeros((E * cap + 1,), x.dtype).at[pos].set(s_g)[:E * cap]
        xg = x[disp_tok].reshape(E, cap, Dm)
        h = jax.nn.silu(jnp.einsum('ecd,edh->ech', xg, W1) + b1[:, None, :])
        out = jnp.einsum('ech,ehd->ecd', h, W2) + b2[:, None, :]
        gated = out * disp_g.reshape(E, cap, 1)
        y = jnp.zeros((N, Dm), x.dtype).at[disp_tok].add(gated.reshape(E * cap, Dm))
        return y.reshape(B, T, Dm)

    def _L1_attn_ref(x, Wq, bq, Wk, bk, Wv, bv, Wo, bo):
        import math
        import jax, jax.numpy as jnp
        import numpy as np
        B, T, D, H = (2, 256, 128, 16)
        N_LAYERS = 24

        def get_slopes(n):

            def pow2(n):
                start = 2 ** (-2 ** (-(math.log2(n) - 3)))
                return [start * start ** i for i in range(n)]
            if math.log2(n).is_integer():
                return pow2(n)
            c = 2 ** math.floor(math.log2(n))
            return pow2(c) + get_slopes(2 * c)[0::2][:n - c]
        Bb, Tt, C = x.shape
        hd = C // H
        q = (x @ Wq + bq).reshape(Bb, Tt, H, hd).transpose(0, 2, 1, 3)
        k = (x @ Wk + bk).reshape(Bb, Tt, H, hd).transpose(0, 2, 1, 3)
        v = (x @ Wv + bv).reshape(Bb, Tt, H, hd).transpose(0, 2, 1, 3)
        attn = jnp.einsum('bhqd,bhkd->bhqk', q, k) / jnp.sqrt(jnp.asarray(hd, x.dtype))
        slopes = jnp.asarray(get_slopes(H), dtype=x.dtype)
        alibi = -slopes[None, :, None, None] * (Tt - 1 - jnp.arange(Tt, dtype=x.dtype))[None, None, None, :]
        attn = attn + alibi
        causal = jnp.tril(jnp.ones((Tt, Tt), dtype=bool))[None, None, :, :]
        attn = jnp.where(causal, attn, jnp.finfo(x.dtype).min)
        p = jax.nn.softmax(attn, axis=-1)
        out = jnp.einsum('bhqk,bhkd->bqhd', p, v).reshape(Bb, Tt, C)
        return out @ Wo + bo

    def _L1_ffn_ref(x, router_w, router_bias, gate_w, up_w, down_w, sgate_w, sup_w, sdown_w):
        import jax, jax.numpy as jnp
        import numpy as np
        TOPK = 4
        B, T, D = x.shape
        flat = x.reshape(B * T, D)
        logits = flat.astype(jnp.float32) @ router_w.T + router_bias
        scores = jax.nn.softmax(logits, axis=-1)
        topk_scores, topk_idx = jax.lax.top_k(scores, TOPK)
        topk_scores = topk_scores / jnp.clip(topk_scores.sum(axis=-1, keepdims=True), 1e-12, None)
        h = jax.nn.silu(jnp.einsum('nd,ehd->neh', flat, gate_w)) * jnp.einsum('nd,ehd->neh', flat, up_w)
        expert_out = jnp.einsum('neh,edh->ned', h, down_w)
        sel = jnp.take_along_axis(expert_out, topk_idx[:, :, None], axis=1)
        out = (sel * topk_scores.astype(flat.dtype)[:, :, None]).sum(axis=1)
        out = out + jax.nn.silu(flat @ sgate_w.T) * (flat @ sup_w.T) @ sdown_w.T
        return out.reshape(B, T, D)
    x = L0_attn_x
    x = _layernorm(x + _L0_attn_ref(x, L0_attn_w_qkv, L0_attn_b_qkv, L0_attn_w_proj, L0_attn_b_proj), axis=-1)
    x = _layernorm(x + _L0_ffn_ref(x, L0_ffn_Wr, L0_ffn_br, L0_ffn_W1, L0_ffn_b1, L0_ffn_W2, L0_ffn_b2), axis=-1)
    x = _layernorm(x + _L1_attn_ref(x, L1_attn_Wq, L1_attn_bq, L1_attn_Wk, L1_attn_bk, L1_attn_Wv, L1_attn_bv, L1_attn_Wo, L1_attn_bo), axis=-1)
    x = _layernorm(x + _L1_ffn_ref(x, L1_ffn_router_w, L1_ffn_router_bias, L1_ffn_gate_w, L1_ffn_up_w, L1_ffn_down_w, L1_ffn_sgate_w, L1_ffn_sup_w, L1_ffn_sdown_w), axis=-1)
    return x

_drawn_inputs = setup_inputs


def setup_inputs(seed=0):
    import zlib

    import numpy as np

    out = dict(_drawn_inputs(seed))
    spreads = {'L0_attn_b_qkv': (0.0, 0.1),
     'L0_attn_b_proj': (0.0, 0.1),
     'L0_ffn_br': (0.0, 0.1),
     'L0_ffn_b1': (0.0, 0.1),
     'L0_ffn_b2': (0.0, 0.1),
     'L1_attn_bq': (0.0, 0.8),
     'L1_attn_bk': (0.0, 0.8),
     'L1_attn_bv': (0.0, 0.651),
     'L1_attn_bo': (0.0, 0.1),
     'L1_ffn_router_bias': (0.0, 0.1)}
    factors = {'L1_attn_Wq': 8.0, 'L1_attn_Wk': 8.0, 'L1_attn_Wv': 6.086, 'L1_attn_Wo': 4.34}
    for name, (base, spread) in spreads.items():
        noise = np.random.default_rng([zlib.crc32(name.encode()), seed]).standard_normal(out[name].shape)
        drawn = base * np.exp(spread * noise) if base else spread * noise
        out[name] = jnp.asarray(drawn.astype(out[name].dtype))
    for name, factor in factors.items():
        out[name] = (out[name] * factor).astype(out[name].dtype)
    return out
```

```python
import numpy as np
from contextlib import ExitStack

import concourse.bass as bass
from concourse import mybir

fp32 = mybir.dt.float32
bf16 = mybir.dt.bfloat16
i32 = mybir.dt.int32
u32 = mybir.dt.uint32
ALU = mybir.AluOpType
ACT = mybir.ActivationFunctionType
AX = mybir.AxisListType

P = 128
BATCH, SEQ, C = 4, 1024, 128
N = BATCH * SEQ
TILES = N // P
TB = SEQ // P
HALF = 512
HEADS, HD = 16, 8
EPS = 1e-5

E0, H0, K0 = 8, 512, 2
CLEARS = E0 + (N * 4 // P + 32) * P // 640 + 8
CAP = int(np.ceil(1.2 * N / E0))
SLOTS0 = -(-CAP // P) * P
ROWS0 = E0 * SLOTS0

E1, H1, K1 = 32, 128, 4
TILES1 = N * K1 // P + E1
ROWS1 = TILES1 * P
HS = H1 * K1
WIDE = C + 1
OUT_OF_RANGE = 1.0e6

GH = 4
STEPS = BATCH * HEADS // GH
PROD = 3 * 3 * HD
ALIBI_AT, MAX_AT = PROD, PROD + 3
ROWS_MAX, ROWS_ALL = PROD + 3, PROD + 6
MASKED = -1.0e30


def slopes():
    start = 2.0 ** (-2.0 ** (-(np.log2(HEADS) - 3)))
    return np.array([start * start ** i for i in range(HEADS)], np.float32)


class Order:

    def __init__(self, engine, sem, base=0):
        self.engine, self.sem, self.base, self.count = engine, sem, base, 0

    def done(self, instruction):
        self.count += 1
        instruction.then_inc(self.sem, 1)
        self.engine.wait_ge(self.sem, self.base + self.count)


def repeat(engine, times):
    def run(body):
        body(0)
        with engine.Fori(1, times) as i:
            body(i)
    return run


def wait_past(engine, sem, count):
    if not isinstance(count, int) or count > 0:
        engine.wait_ge(sem, count)


class Mem:

    def __init__(self, nc, ctx):
        self.nc, self.ctx = nc, ctx

    def sb(self, name, shape, dt=fp32):
        return self.ctx.enter_context(self.nc.sbuf_tensor(name, shape, dt))

    def sem(self, name):
        return self.ctx.enter_context(self.nc.semaphore(name))


def tiles(i, n=TB):
    return bass.ds(i * n, n)


def stage_setup(nc, G, I):
    with ExitStack() as ctx:
        M = Mem(nc, ctx)
        filled, shaped, loaded = M.sem("filled"), M.sem("shaped"), M.sem("loaded")
        with nc.Block() as block:
            @block.sync
            def _(sp):
                for b in range(BATCH):
                    sp.dma_start(G.x_rows[:, b * TB:(b + 1) * TB, :],
                                 I["x"][b * SEQ:(b + 1) * SEQ, :].rearrange("(t p) c -> p t c", p=P)).then_inc(loaded, 16)
                sp.dma_start(G.head_mask[:], I["c_head_mask"]).then_inc(loaded, 16)
                sp.wait_ge(loaded, (BATCH + 1) * 16)
                sp.wait_ge(filled, 9)
                for r in range(0, ROWS0, SLOTS0):
                    sp.dma_start(G.sorted0[r:r + SLOTS0, :].rearrange("(s p) c -> p s c", p=P),
                                 G.blank[:, None, :].to_broadcast([P, SLOTS0 // P, WIDE])).then_inc(G.cleared, 16)
                for r in range(0, ROWS1, SLOTS0):
                    sp.dma_start(G.sorted1[r:r + SLOTS0, :].rearrange("(s p) c -> p s c", p=P),
                                 G.blank[:, None, :].to_broadcast([P, SLOTS0 // P, WIDE])).then_inc(G.cleared, 16)
                for r in range(0, K0 * N, SEQ):
                    sp.dma_start(G.expert_out0[r:r + SEQ, :].rearrange("(s p) c -> p s c", p=P),
                                 G.blank[:, None, 0:C].to_broadcast([P, TB, C])).then_inc(G.cleared, 16)

            @block.gpsimd
            def _(pool):
                pool.memset(G.ident[:], 0.0).then_inc(filled, 1)
                pool.memset(G.ones[:], 1.0).then_inc(filled, 1)
                pool.memset(G.before[:], 1.0).then_inc(filled, 1)
                pool.memset(G.minus_half[:], -0.5).then_inc(filled, 1)
                pool.memset(G.blank[:, 0:C], 0.0).then_inc(filled, 1)
                pool.memset(G.blank[:, C:WIDE], OUT_OF_RANGE).then_inc(filled, 1)
                pool.iota(G.place_of[:], pattern=[[N, K1], [P, TILES]], base=0, channel_multiplier=1,
                          allow_small_or_imprecise_dtypes=True).then_inc(filled, 1)
                pool.iota(G.iota_e[:], pattern=[[1, E1]], base=0, channel_multiplier=0,
                          allow_small_or_imprecise_dtypes=True).then_inc(filled, 1)
                pool.iota(G.iota_p[:], pattern=[[P, 2]], base=0, channel_multiplier=1,
                          allow_small_or_imprecise_dtypes=True).then_inc(filled, 1)
                pool.wait_ge(filled, 9)
                pool.affine_select(out=G.ident[:], in_=G.ident[:], compare_op=ALU.not_equal, fill=1.0,
                                   base=0, pattern=[[-1, P]], channel_multiplier=1).then_inc(shaped, 1)
                pool.affine_select(out=G.before[:], in_=G.before[:], compare_op=ALU.is_gt, fill=0.0,
                                   base=0, pattern=[[1, P]], channel_multiplier=-1).then_inc(shaped, 1)
                pool.wait_ge(shaped, 2)


def emit_norm_vector(dve, G, order, i, y, stats, mv, var_eps, rstd, out_tile):
    for t in range(TB - 1):
        dve.bn_stats(stats[:, t, :], y(t))
    order.done(dve.bn_stats(stats[:, TB - 1, :], y(TB - 1)))
    dve.memset(var_eps[:, 0:1], 0.0)
    for t in range(TB - 1):
        dve.bn_aggr(mv[:, t, :], stats[:, t, :])
    order.done(dve.bn_aggr(mv[:, TB - 1, :], stats[:, TB - 1, :]))
    dve.tensor_scalar(var_eps[:], mv[:, :, 1], EPS, None, ALU.add).then_inc(G.var_ready, 1)
    dve.wait_ge(G.rstd_ready, i + 1)
    last = None
    for t in range(TB):
        last = dve.tensor_scalar(out_tile(t), y(t), mv[:, t, 0:1], rstd[:, t:t + 1],
                                 ALU.subtract, ALU.mult)
    return last


def emit_norm_pool(pool, G, i, var_eps, rstd):
    pool.wait_ge(G.var_ready, i + 1)
    pool.tensor_tensor(rstd[:], var_eps[:], G.minus_half[:, 0:TB], ALU.pow).then_inc(G.rstd_ready, 1)


def emit_scatter(pool, G, to_row, choices, sorted_rows, last_row, placed, scattered):
    for k in range(choices):
        if k:
            pool.wait_ge(scattered, k * TILES * 16)
        pool.tensor_copy(G.x_wide[:, :, C], G.place_of[:, k, :]).then_inc(placed, 1)
        pool.wait_ge(placed, k + 1)
        for t in range(TILES):
            pool.indirect_dma_start(
                out=sorted_rows, out_offset=bass.IndirectOffsetOnAxis(ap=to_row[:, t, k:k + 1], axis=0),
                in_=G.x_wide[:, t, :], in_offset=None, bounds_check=last_row,
                oob_is_err=False).then_inc(scattered, 16)
    pool.wait_ge(scattered, choices * TILES * 16)


def stage_linear_attention(nc, G, I):
    KV = 2 * C
    NORMED = 0 * BATCH
    with ExitStack() as ctx:
        M = Mem(nc, ctx)
        w_qkv, w_proj = M.sb("wqkv_sb", [P, 3 * C]), M.sb("wproj_sb", [P, C])
        bq, bkv, bproj = M.sb("bq_sb", [P, 1]), M.sb("bkv_sb", [P, KV]), M.sb("bproj_sb", [P, C])
        w_r, b_r = M.sb("wr_sb", [P, E0]), M.sb("br_sb", [P, E0])
        xT = M.sb("xT_in", [P, SEQ])
        kv = M.sb("kv_rows", [P, TB, KV + 1])
        k_exp, k_relu = M.sb("k_exp", [P, TB, C]), M.sb("k_relu", [P, TB, C])
        qT, q_exp = M.sb("qT", [P, SEQ]), M.sb("q_exp", [P, SEQ])
        kv_heads, ksum_heads = M.sb("kv_heads", [P, C]), M.sb("ksum_heads", [P, C])
        den, attT = M.sb("den", [P, SEQ]), M.sb("attT", [P, SEQ])
        x_bias = M.sb("x_bias", [P, TB, C])
        y, x_new = M.sb("y_rows", [P, TB, C]), M.sb("x_new", [P, TB, C])
        xT_new = M.sb("xT_new", [P, SEQ])
        stats, mv = M.sb("stats", [P, TB, 6]), M.sb("mv", [P, TB, 2])
        var_eps, rstd = M.sb("var_eps", [P, TB]), M.sb("rstd", [P, TB])
        weights, xT_here = M.sem("weights"), M.sem("xT_here")
        q_done, kv_done = M.sem("q_done"), M.sem("kv_done")
        kv_taken, q_relu = M.sem("kv_taken"), M.sem("q_relu")
        qexp_done, kexp_done, qT_done, k_done = M.sem("qexp_done"), M.sem("kexp_done"), M.sem("qT_done"), M.sem("k_done")
        sums_done, heads_done, out_done, den_done = M.sem("sums_done"), M.sem("heads_done"), M.sem("out_done"), M.sem("den_done")
        att_done, y_done, y_taken = M.sem("att_done"), M.sem("y_done"), M.sem("y_taken")
        xb_done = M.sem("xb_done")
        norm_done, xT_psum, xT_copied = M.sem("norm_done"), M.sem("xT_psum"), M.sem("xT_copied")
        logits_psum, logits_done, x_kept, steps = M.sem("logits_psum"), M.sem("logits_done"), M.sem("x_kept"), M.sem("steps")
        ones_set = M.sem("ones_set")
        B = G.bank
        with nc.Block() as block:
            @block.sync
            def _(sp):
                sp.dma_start(w_qkv[:], I["w_qkv"]).then_inc(weights, 16)
                sp.dma_start(bq[:], I["b_q_col"]).then_inc(weights, 16)
                sp.dma_start(bkv[:], I["b_kv"].to_broadcast([P, KV])).then_inc(weights, 16)
                sp.dma_start(w_proj[:], I["w_proj"]).then_inc(weights, 16)
                sp.dma_start(bproj[:], I["b_proj"].to_broadcast([P, C])).then_inc(weights, 16)
                sp.dma_start(w_r[:], I["Wr"]).then_inc(weights, 16)
                sp.dma_start(b_r[:], I["br"].to_broadcast([P, E0])).then_inc(weights, 16)
                sp.dma_start(xT[:], I["xT"][:, 0:SEQ]).then_inc(xT_here, 16)
                @repeat(sp, BATCH - 1)
                def _(i):
                    sp.wait_ge(kv_done, i * 4 + 4)
                    sp.dma_start(xT[:], I["xT"][:, bass.ds(i * SEQ + SEQ, SEQ)]).then_inc(xT_here, 16)
                    sp.wait_ge(norm_done, i + 1)
                    sp.dma_start(G.x_rows[:, tiles(i), :], x_new[:]).then_inc(x_kept, 16)
                sp.wait_ge(norm_done, BATCH)
                sp.dma_start(G.x_rows[:, tiles(BATCH - 1), :], x_new[:]).then_inc(x_kept, 16)
                sp.wait_ge(x_kept, BATCH * 16)

            @block.tensor
            def _(pe):
                pe.wait_ge(weights, 7 * 16)
                @repeat(pe, BATCH)
                def _(i):
                    pe.wait_ge(xT_here, i * 16 + 16)
                    wait_past(pe, y_taken, i * 2)
                    for c in range(2):
                        pe.matmul(B[4 + c][:], w_qkv[:, 0:C], xT[:, c * HALF:(c + 1) * HALF],
                                  start=True, stop=True).then_inc(q_done, 1)
                    for t in range(TB):
                        if t == 0:
                            wait_past(pe, logits_done, i)
                        mm = pe.matmul(B[t // 2][:, (t % 2) * KV:(t % 2 + 1) * KV], xT[:, t * P:(t + 1) * P],
                                       w_qkv[:, C:3 * C], start=(t % 2 == 0), stop=True, skip_group_check=True)
                        if t % 2:
                            mm.then_inc(kv_done, 1)
                    pe.wait_ge(k_done, i + 1)
                    for t in range(TB):
                        mm = pe.matmul(B[6][:, 0:C + 1], kv[:, t, 0:C], kv[:, t, C:KV + 1],
                                       start=(t == 0), stop=(t == TB - 1))
                    mm.then_inc(sums_done, 1)
                    pe.wait_ge(heads_done, i * 2 + 2)
                    pe.wait_ge(qT_done, i * 2 + 2)
                    for c in range(2):
                        pe.matmul(B[c][:], kv_heads[:], qT[:, c * HALF:(c + 1) * HALF], start=True, stop=True)
                        mm = pe.matmul(B[2 + c][:], ksum_heads[:], qT[:, c * HALF:(c + 1) * HALF],
                                       start=True, stop=True)
                        mm.then_inc(out_done, 1)
                    pe.wait_ge(att_done, i + 1)
                    for t in range(TB):
                        mm = pe.matmul(B[4 + t // 4][:, (t % 4) * C:(t % 4 + 1) * C], attT[:, t * P:(t + 1) * P],
                                       w_proj[:], start=(t % 4 == 0), stop=True, skip_group_check=True)
                        if t % 4 == 3:
                            mm.then_inc(y_done, 1)
                    pe.wait_ge(norm_done, i + 1)
                    for t in range(TB):
                        mm = pe.transpose(B[6 + t // 4][:, (t % 4) * P:(t % 4 + 1) * P], x_new[:, t, :], G.ident[:])
                        if t % 4 == 3:
                            mm.then_inc(xT_psum, 1)
                    pe.wait_ge(xT_copied, i * 2 + 2)
                    for t in range(TB):
                        mm = pe.matmul(B[0][:, t * E0:(t + 1) * E0], xT_new[:, t * P:(t + 1) * P], w_r[:],
                                       start=(t == 0), stop=True, skip_group_check=True)
                    mm.then_inc(logits_psum, 1)

            @block.scalar
            def _(act):
                @repeat(act, BATCH)
                def _(i):
                    wait_past(act, qT_done, i * 2)
                    for c in range(2):
                        act.wait_ge(q_relu, i * 2 + c + 1)
                        act.activation(q_exp[:, c * HALF:(c + 1) * HALF], B[4 + c][:], ACT.Exp,
                                       bias=bq[:]).then_inc(qexp_done, 1)
                    act.wait_ge(kv_taken, i * 4 + 4)
                    act.activation(k_exp[:], kv[:, :, 0:C], ACT.Exp).then_inc(kexp_done, 1)
                    for c in range(2):
                        act.wait_ge(out_done, i * 2 + c + 1)
                        act.activation(den[:, c * HALF:(c + 1) * HALF], B[2 + c][:], ACT.Copy,
                                       bias=1e-8).then_inc(den_done, 1)
                    for c in range(2):
                        act.wait_ge(xT_psum, i * 2 + c + 1)
                        act.activation(xT_new[:, c * HALF:(c + 1) * HALF], B[6 + c][:], ACT.Copy).then_inc(xT_copied, 1)

            @block.gpsimd
            def _(pool):
                pool.memset(kv[:, :, KV:KV + 1], 1.0).then_inc(ones_set, 1)
                pool.wait_ge(weights, 7 * 16)
                @repeat(pool, BATCH)
                def _(i):
                    wait_past(pool, y_taken, i * 2)
                    pool.tensor_tensor(x_bias[:], G.x_rows[:, tiles(i), :],
                                       bproj[:, None, :].to_broadcast([P, TB, C]), ALU.add).then_inc(xb_done, 1)
                    emit_norm_pool(pool, G, NORMED + i, var_eps, rstd)

            @block.vector
            def _(dve):
                dve.wait_ge(weights, 7 * 16)
                dve.wait_ge(ones_set, 1)
                @repeat(dve, BATCH)
                def _(i):
                    order = Order(dve, steps, i * 6)
                    for c in range(2):
                        dve.wait_ge(q_done, i * 2 + c + 1)
                        dve.tensor_scalar(qT[:, c * HALF:(c + 1) * HALF], B[4 + c][:], bq[:], 0.0,
                                          ALU.add, ALU.max).then_inc(q_relu, 1)
                    for b in range(4):
                        dve.wait_ge(kv_done, i * 4 + b + 1)
                        dve.tensor_tensor(kv[:, 2 * b:2 * b + 2, 0:KV],
                                          B[b][:].rearrange("p (t n) -> p t n", t=2),
                                          bkv[:, None, :].to_broadcast([P, 2, KV]), ALU.add).then_inc(kv_taken, 1)
                    for c in range(2):
                        dve.wait_ge(qexp_done, i * 2 + c + 1)
                        dve.wait_ge(q_relu, i * 2 + c + 1)
                        s = slice(c * HALF, (c + 1) * HALF)
                        dve.scalar_tensor_tensor(out=qT[:, s], in0=q_exp[:, s], scalar=1.0, in1=qT[:, s],
                                                 op0=ALU.min, op1=ALU.add).then_inc(qT_done, 1)
                    dve.wait_ge(kv_taken, i * 4 + 4)
                    order.done(dve.tensor_scalar(k_relu[:], kv[:, :, 0:C], 0.0, None, ALU.max))
                    dve.wait_ge(kexp_done, i + 1)
                    dve.scalar_tensor_tensor(out=kv[:, :, 0:C], in0=k_exp[:], scalar=1.0, in1=k_relu[:],
                                             op0=ALU.min, op1=ALU.add).then_inc(k_done, 1)
                    dve.wait_ge(sums_done, i + 1)
                    dve.tensor_tensor(kv_heads[:], B[6][:, 0:C], G.head_mask[:], ALU.mult).then_inc(heads_done, 1)
                    dve.tensor_scalar(ksum_heads[:], G.head_mask[:], B[6][:, C:C + 1], None,
                                      ALU.mult).then_inc(heads_done, 1)
                    for c in range(2):
                        s = slice(c * HALF, (c + 1) * HALF)
                        dve.wait_ge(den_done, i * 2 + c + 1)
                        order.done(dve.reciprocal(den[:, s], den[:, s]))
                        last = dve.tensor_tensor(attT[:, s], B[c][:], den[:, s], ALU.mult)
                        if c == 0:
                            order.done(last)
                    last.then_inc(att_done, 1)
                    dve.wait_ge(xb_done, i + 1)
                    for c in range(2):
                        dve.wait_ge(y_done, i * 2 + c + 1)
                        dve.tensor_tensor(y[:, 4 * c:4 * c + 4, :], B[4 + c][:].rearrange("p (t n) -> p t n", t=4),
                                          x_bias[:, 4 * c:4 * c + 4, :], ALU.add).then_inc(y_taken, 1)
                    dve.wait_ge(y_taken, i * 2 + 2)
                    wait_past(dve, x_kept, i * 16)
                    last = emit_norm_vector(dve, G, order, NORMED + i, lambda t: y[:, t, :], stats, mv, var_eps, rstd, lambda t: x_new[:, t, :])
                    last.then_inc(norm_done, 1)
                    dve.wait_ge(logits_psum, i + 1)
                    last = dve.tensor_tensor(G.logits0[:, tiles(i), :],
                                             B[0][:, 0:TB * E0].rearrange("p (t e) -> p t e", e=E0),
                                             b_r[:, None, :].to_broadcast([P, TB, E0]), ALU.add)
                    last.then_inc(logits_done, 1)
                    assert order.count == 6



class Router:

    def __init__(self, M, G, experts, chosen, name):
        self.E, self.K, self.G = experts, chosen, G
        self.cols = TILES * experts
        self.prob = M.sb(name + "_prob", [P, TILES, experts])
        self.top = M.sb(name + "_top", [P, TILES, 8])
        self.top_at = M.sb(name + "_top_at", [P, TILES, 8], u32)
        self.top_at_f = M.sb(name + "_top_at_f", [P, TILES, chosen])
        self.total = M.sb(name + "_total", [P, TILES])
        self.onehot = M.sb(name + "_onehot", [P, chosen, TILES, experts])
        self.member = M.sb(name + "_member", [P, TILES, experts])
        self.position = M.sb(name + "_position", [P, TILES, experts])
        self.by_expert = M.sb(name + "_by_expert", [P, experts, TILES])
        self.scanned = M.sb(name + "_scanned", [P, experts, TILES])
        self.goes_on = M.sb(name + "_goes_on", [P, experts, TILES])
        self.picked = M.sb(name + "_picked", [P, TILES, experts])
        self.row = M.sb(name + "_row", [P, TILES])
        self.vec, self.exp_in, self.exp_out = M.sem(name + "_vec"), M.sem(name + "_exp_in"), M.sem(name + "_exp_out")
        self.to_count, self.counted = M.sem(name + "_to_count"), M.sem(name + "_counted")

    def across(self, per_tile):
        return per_tile[:, :, None].to_broadcast([P, TILES, self.E])


def emit_softmax_topk(dve, order, R, logits):
    order.done(dve.tensor_reduce(R.total[:], logits[:], AX.X, ALU.max))
    dve.tensor_tensor(R.prob[:], logits[:], R.across(R.total), ALU.subtract).then_inc(R.exp_in, 1)
    dve.wait_ge(R.exp_out, 1)
    order.done(dve.tensor_reduce(R.total[:], R.prob[:], AX.X, ALU.add))
    order.done(dve.reciprocal(R.total[:], R.total[:]))
    order.done(dve.tensor_tensor(R.prob[:], R.prob[:], R.across(R.total), ALU.mult))
    for t in range(TILES - 1):
        dve.max(R.top[:, t, :], R.prob[:, t, :])
    order.done(dve.max(R.top[:, TILES - 1, :], R.prob[:, TILES - 1, :]))
    for t in range(TILES - 1):
        dve.max_index(R.top_at[:, t, :], R.top[:, t, :], R.prob[:, t, :])
    order.done(dve.max_index(R.top_at[:, TILES - 1, :], R.top[:, TILES - 1, :], R.prob[:, TILES - 1, :]))
    order.done(dve.tensor_copy(R.top_at_f[:], R.top_at[:, :, 0:R.K]))
    for k in range(R.K):
        last = dve.tensor_tensor(R.onehot[:, k], R.G.iota_e[:, None, 0:R.E].to_broadcast([P, TILES, R.E]),
                                 R.across(R.top_at_f[:, :, k]), ALU.is_equal)
    order.done(last)
    order.done(dve.tensor_tensor(R.member[:], R.onehot[:, 0], R.onehot[:, 1], ALU.add))
    for k in range(2, R.K):
        order.done(dve.tensor_tensor(R.member[:], R.member[:], R.onehot[:, k], ALU.add))


def emit_exp(act, R):
    act.wait_ge(R.exp_in, 1)
    act.activation(R.prob[:], R.prob[:], ACT.Exp).then_inc(R.exp_out, 1)


def emit_count_tensor(pe, R, n, mask, before_bank, total_bank):
    pe.wait_ge(R.to_count, n)
    flat = mask[:].rearrange("p t e -> p (t e)")
    for banks, lhsT in ((before_bank, R.G.before), (total_bank, R.G.ones)):
        for c in range(-(-R.cols // HALF)):
            w = min(HALF, R.cols - c * HALF)
            mm = pe.matmul(banks[c][:, 0:w], lhsT[:], flat[:, c * HALF:c * HALF + w], start=True, stop=True)
    mm.then_inc(R.counted, 1)


def emit_positions(dve, order, R, n, before_bank, total_bank):
    dve.wait_ge(R.counted, n)
    per = HALF // R.E
    for c in range(-(-R.cols // HALF)):
        w = min(per, TILES - c * per)
        last = dve.tensor_copy(R.by_expert[:, :, c * per:c * per + w],
                               total_bank[c][:, 0:w * R.E].rearrange("p (t e) -> p e t", e=R.E))
    order.done(last)
    flat = lambda x: x[:].rearrange("p e t -> p (e t)")
    order.done(dve.tensor_tensor_scan(flat(R.scanned), flat(R.goes_on), flat(R.by_expert), 0.0, ALU.mult, ALU.add))
    order.done(dve.tensor_tensor(R.by_expert[:], R.scanned[:], R.by_expert[:], ALU.subtract))
    for c in range(-(-R.cols // HALF)):
        w = min(per, TILES - c * per)
        last = dve.tensor_tensor(R.position[:, c * per:c * per + w, :],
                                 before_bank[c][:, 0:w * R.E].rearrange("p (t e) -> p t e", e=R.E),
                                 R.by_expert[:, :, c * per:c * per + w].rearrange("p e t -> p t e"), ALU.add)
    order.done(last)


def emit_pick(dve, order, R, k, values, out):
    order.done(dve.tensor_tensor(R.picked[:], R.onehot[:, k], values[:], ALU.mult))
    order.done(dve.tensor_reduce(out, R.picked[:], AX.X, ALU.add))


def stage_route0(nc, G, I):
    BITS = 30
    with ExitStack() as ctx:
        M = Mem(nc, ctx)
        R = Router(M, G, E0, K0, "r0")
        gate = M.sb("gate_of", [P, TILES, E0])
        gateT = M.sb("gateT", [P, 2 * P])
        compared = M.sb("compared", [P, 2 * P])
        same_expert = M.sb("same_expert", [P, P])
        first_of = M.sb("first_of", [P, E0])
        count, tried, found, spread = M.sb("count", [P, 1]), M.sb("tried", [P, 1]), M.sb("found", [P, 1]), M.sb("spread", [P, E0])
        bit = M.sb("bit", [P, 1], u32)
        above, equal, taken = M.sb("above", [P, TILES, E0]), M.sb("equal", [P, TILES, E0]), M.sb("taken", [P, TILES, E0])
        limit, room = M.sb("limit", [P, E0]), M.sb("room", [P, E0])
        loaded, gateT_psum, cnt_in, cnt_out = M.sem("loaded"), M.sem("gateT_psum"), M.sem("cnt_in"), M.sem("cnt_out")
        gate_done, found_done, limit_psum, vec_loop = M.sem("gate_done"), M.sem("found_done"), M.sem("limit_psum"), M.sem("vec_loop")
        above_done, above_psum = M.sem("above_done"), M.sem("above_psum")
        B = G.bank
        over = lambda v: v[:, None, :].to_broadcast([P, TILES, E0])
        with nc.Block() as block:
            @block.sync
            def _(sp):
                sp.dma_start(same_expert[:], I["c_same_expert"]).then_inc(loaded, 16)
                sp.dma_start(first_of[:], I["c_first_of"]).then_inc(loaded, 16)
                sp.dma_start(R.goes_on[:].rearrange("p e t -> p (e t)"),
                             I["c_goes_on"][:, 0:E0 * TILES].to_broadcast([P, E0 * TILES])).then_inc(loaded, 16)

            @block.scalar
            def _(act):
                emit_exp(act, R)

            @block.tensor
            def _(pe):
                pe.wait_ge(loaded, 48)
                pe.wait_ge(gate_done, 1)
                flat = gate[:].rearrange("p t e -> p (t e)")
                for c in range(2):
                    mm = pe.transpose(B[0][:, c * P:(c + 1) * P], flat[:, c * P:(c + 1) * P], G.ident[:])
                mm.then_inc(gateT_psum, 1)
                with pe.Fori(0, BITS) as i:
                    pe.wait_ge(cnt_in, i + 1)
                    pe.matmul(B[1][:, 0:1], same_expert[:], count[:], start=True, stop=True).then_inc(cnt_out, 1)
                pe.wait_ge(found_done, 1)
                pe.matmul(B[1][:, 0:E0], G.ones[:], spread[:], start=True, stop=True).then_inc(limit_psum, 1)
                emit_count_tensor(pe, R, 1, equal, [B[2]], [B[3]])
                pe.matmul(B[4][:, 0:R.cols], G.ones[:], above[:].rearrange("p t e -> p (t e)"),
                          start=True, stop=True).then_inc(above_psum, 1)
                emit_count_tensor(pe, R, 2, taken, [B[5]], [B[6]])

            @block.vector
            def _(dve):
                order = Order(dve, R.vec)
                emit_softmax_topk(dve, order, R, G.logits0)
                order.done(dve.tensor_tensor(gate[:], R.prob[:], R.member[:], ALU.mult))
                order.done(dve.tensor_tensor(gate[:], gate[:], R.member[:], ALU.add))
                dve.tensor_scalar(gate[:], gate[:], 1.0, None, ALU.subtract).then_inc(gate_done, 1)
                dve.memset(found[:], 0.0)
                dve.memset(bit[:], 1 << (BITS - 1))
                order.done(dve.memset(tried[:].bitcast(u32), 1 << (BITS - 1)))
                dve.wait_ge(loaded, 48)
                dve.wait_ge(gateT_psum, 1)
                order.done(dve.tensor_copy(gateT[:], B[0][:, 0:2 * P]))
                with dve.Fori(0, BITS) as i:
                    inner = Order(dve, vec_loop, i * 4)
                    dve.tensor_scalar(compared[:], gateT[:], tried[:], None, ALU.is_ge, ALU.add,
                                      accum_out=count[:]).then_inc(cnt_in, 1)
                    inner.done(dve.tensor_scalar(bit[:], bit[:], 1, None, ALU.logical_shift_right))
                    dve.wait_ge(cnt_out, i + 1)
                    inner.done(dve.scalar_tensor_tensor(out=tried[:], in0=B[1][:, 0:1], scalar=float(CAP),
                                                        in1=tried[:], op0=ALU.is_ge, op1=ALU.mult))
                    inner.done(dve.tensor_tensor(found[:], found[:], tried[:], ALU.max))
                    inner.done(dve.tensor_tensor(tried[:].bitcast(u32), found[:].bitcast(u32), bit[:], ALU.bitwise_or))
                    assert inner.count == 4
                dve.tensor_scalar(spread[:], first_of[:], found[:], None, ALU.mult).then_inc(found_done, 1)
                dve.wait_ge(limit_psum, 1)
                order.done(dve.tensor_copy(limit[:], B[1][:, 0:E0]))
                dve.tensor_tensor(above[:], gate[:], over(limit), ALU.is_gt).then_inc(above_done, 1)
                dve.tensor_tensor(equal[:], gate[:], over(limit), ALU.is_equal).then_inc(R.to_count, 1)
                emit_positions(dve, order, R, 1, [B[2]], [B[3]])
                dve.wait_ge(above_psum, 1)
                order.done(dve.tensor_reduce(room[:], B[4][:, 0:R.cols].rearrange("p (t e) -> p e t", e=E0), AX.X, ALU.add))
                order.done(dve.tensor_scalar(room[:], room[:], -1.0, float(CAP), ALU.mult, ALU.add))
                order.done(dve.tensor_tensor(taken[:], R.position[:], over(room), ALU.is_lt))
                order.done(dve.tensor_tensor(taken[:], taken[:], equal[:], ALU.mult))
                dve.tensor_tensor(taken[:], taken[:], above[:], ALU.add).then_inc(R.to_count, 1)
                emit_positions(dve, order, R, 2, [B[5]], [B[6]])
                order.done(dve.tensor_scalar(limit[:], G.iota_e[:, 0:E0], float(SLOTS0), OUT_OF_RANGE, ALU.mult, ALU.add))
                order.done(dve.tensor_tensor(R.position[:], R.position[:], over(limit), ALU.add))
                order.done(dve.scalar_tensor_tensor(out=R.position[:], in0=taken[:], scalar=-OUT_OF_RANGE,
                                                    in1=R.position[:], op0=ALU.mult, op1=ALU.add))
                for k in range(K0):
                    emit_pick(dve, order, R, k, taken, R.row[:])
                    order.done(dve.tensor_tensor(G.gate0[:, :, k], R.row[:], R.top[:, :, k], ALU.mult))
                    emit_pick(dve, order, R, k, R.position, R.row[:])
                    order.done(dve.tensor_copy(G.to_row0[:, :, k], R.row[:]))


def stage_experts0(nc, G, I):
    HC = H0 // P
    ST = SLOTS0 // P
    FIRST = min(SLOTS0, HALF)
    PARTS = ((0, FIRST), (FIRST, SLOTS0))
    with ExitStack() as ctx:
        M = Mem(nc, ctx)
        two = range(2)
        w1 = [M.sb(f"w1_{u}", [P, H0]) for u in two]
        w2 = [M.sb(f"w2_{u}", [P, HC, C]) for u in two]
        b1 = [M.sb(f"b1_{u}", [P, HC]) for u in two]
        b2 = [M.sb(f"b2_{u}", [P, C]) for u in two]
        rows = [M.sb(f"rows_{u}", [P, ST, WIDE]) for u in two]
        place = [M.sb(f"place_{u}", [P, ST], u32) for u in two]
        placed, place_done = M.sem("placed"), M.sem("place_done")
        xT = [M.sb(f"exT_{u}", [P, SLOTS0]) for u in two]
        hT = M.sb("hT", [P, HC, SLOTS0])
        y = [M.sb(f"ey_{u}", [P, ST, C]) for u in two]
        scattered, w_here = M.sem("scattered"), [M.sem(f"w_here{u}") for u in two]
        rows_here, y_kept = [M.sem(f"rows_here{u}") for u in two], [M.sem(f"y_kept{u}") for u in two]
        xT_psum, xT_done, h_psum, h_done = M.sem("xT_psum"), M.sem("xT_done"), M.sem("h_psum"), M.sem("h_done")
        y_psum, y_done = M.sem("y_psum"), M.sem("y_done")
        B = G.bank
        with nc.Block() as block:
            @block.gpsimd
            def _(pool):
                pool.wait_ge(G.cleared, CLEARS * 16)
                emit_scatter(pool, G, G.to_row0, K0, G.sorted0, ROWS0 - 1, placed, scattered)
                for e in range(E0):
                    pool.wait_ge(y_done, e + 1)
                    for t in range(ST):
                        pool.indirect_dma_start(
                            out=G.expert_out0, out_offset=bass.IndirectOffsetOnAxis(ap=place[e % 2][:, t:t + 1], axis=0),
                            in_=y[e % 2][:, t, :], in_offset=None, bounds_check=K0 * N - 1,
                            oob_is_err=False).then_inc(y_kept[e % 2], 16)
                for u in two:
                    pool.wait_ge(y_kept[u], E0 // 2 * ST * 16)

            @block.sync
            def _(sp):
                @repeat(sp, E0 // 2)
                def _(i):
                    for u in two:
                        e = i * 2 + u
                        wait_past(sp, y_psum, i * 2 + u - 1)
                        sp.dma_start(w1[u][:], I["W1"][bass.ds(e, 1)].rearrange("o d h -> (o d) h")).then_inc(w_here[u], 16)
                        sp.dma_start(w2[u][:], I["W2"][bass.ds(e, 1)].rearrange("o p c d -> (o p) c d")).then_inc(w_here[u], 16)
                        sp.dma_start(b1[u][:], I["b1"][bass.ds(e, 1)].rearrange("o p c -> (o p) c")).then_inc(w_here[u], 16)
                        wait_past(sp, y_done, i * 2 + u - 1)
                        sp.dma_start(b2[u][:], I["b2"][bass.ds(e, 1), :].to_broadcast([P, C])).then_inc(w_here[u], 16)
                        sp.wait_ge(scattered, TILES * K0 * 16)
                        sp.dma_start(rows[u][:], G.sorted0[bass.ds(e * SLOTS0, SLOTS0), :]
                                     .rearrange("(s p) c -> p s c", p=P)).then_inc(rows_here[u], 16)

            @block.tensor
            def _(pe):
                @repeat(pe, E0 // 2)
                def _(i):
                    for u in two:
                        pe.wait_ge(rows_here[u], i * 16 + 16)
                        for s in range(ST):
                            c, at = divmod(s * P, HALF)
                            mm = pe.transpose(B[c][:, at:at + P], rows[u][:, s, 0:C], G.ident[:])
                        mm.then_inc(xT_psum, 1)
                        pe.wait_ge(xT_done, i * 2 + u + 1)
                        pe.wait_ge(w_here[u], i * 64 + 64)
                        for c in range(HC):
                            if c < 2:
                                wait_past(pe, h_done, i * 2 * HC + u * HC)
                            else:
                                wait_past(pe, h_done, i * 2 * HC + u * HC + c - 1)
                            for n, (a, b) in enumerate(PARTS):
                                mm = pe.matmul(B[2 + 2 * (c % 2) + n][:, 0:b - a], w1[u][:, c * P:(c + 1) * P],
                                               xT[u][:, a:b], start=True, stop=True)
                            mm.then_inc(h_psum, 1)
                        pe.wait_ge(h_done, i * 2 * HC + (u + 1) * HC)
                        wait_past(pe, y_done, i * 2 + u)
                        for s in range(ST):
                            n, at = divmod(s * C, HALF)
                            for c in range(HC):
                                mm = pe.matmul(B[6 + n][:, at:at + C], hT[:, c, s * P:(s + 1) * P], w2[u][:, c, :],
                                               start=(c == 0 and at == 0), stop=(c == HC - 1), skip_group_check=True)
                        mm.then_inc(y_psum, 1)

            @block.scalar
            def _(act):
                @repeat(act, E0 // 2)
                def _(i):
                    for u in two:
                        act.wait_ge(xT_psum, i * 2 + u + 1)
                        for n, (a, b) in enumerate(PARTS):
                            last = act.activation(xT[u][:, a:b], B[n][:, 0:b - a], ACT.Copy)
                        last.then_inc(xT_done, 1)
                        act.wait_ge(w_here[u], i * 64 + 64)
                        wait_past(act, y_psum, i * 2 + u)
                        for c in range(HC):
                            act.wait_ge(h_psum, i * 2 * HC + u * HC + c + 1)
                            for n, (a, b) in enumerate(PARTS):
                                last = act.activation(hT[:, c, a:b], B[2 + 2 * (c % 2) + n][:, 0:b - a], ACT.Silu,
                                                      bias=b1[u][:, c:c + 1])
                            last.then_inc(h_done, 1)

            @block.vector
            def _(dve):
                @repeat(dve, E0 // 2)
                def _(i):
                    for u in two:
                        dve.wait_ge(y_psum, i * 2 + u + 1)
                        wait_past(dve, y_kept[u], i * (ST * 16))
                        dve.wait_ge(rows_here[u], i * 16 + 16)
                        dve.tensor_copy(place[u][:], rows[u][:, :, C]).then_inc(place_done, 1)
                        for n, (a, b) in enumerate(PARTS):
                            k = (b - a) // P
                            last = dve.tensor_tensor(y[u][:, a // P:b // P, :], B[6 + n][:, 0:b - a].rearrange("p (s c) -> p s c", c=C),
                                                     b2[u][:, None, :].to_broadcast([P, k, C]), ALU.add)
                        last.then_inc(y_done, 1)


def emit_combine_load(sp, b, got, here, expert_out, choices):
    for k in range(choices):
        sp.dma_start(got[:, k], expert_out[bass.ds(b * SEQ + k * N, SEQ), :]
                     .rearrange("(t p) c -> p t c", p=P)).then_inc(here, 16)


def emit_combine(dve, order, b, got, gate, choices, x, y):
    for k in range(choices):
        last = dve.tensor_tensor(got[:, k], got[:, k], gate[:, tiles(b), k:k + 1].to_broadcast([P, TB, C]), ALU.mult)
    order.done(last)
    for k in range(1, choices):
        order.done(dve.tensor_tensor(got[:, 0], got[:, 0], got[:, k], ALU.add))
    order.done(dve.tensor_tensor(y, got[:, 0], x, ALU.add))


def emit_split(engine_a, order_a, x, parts, rest):
    order_a.done(engine_a.tensor_copy(parts[0], x))
    order_a.done(engine_a.tensor_tensor(rest, x, parts[0], ALU.subtract))
    order_a.done(engine_a.tensor_copy(parts[1], rest))
    return engine_a.tensor_tensor(parts[2], rest, parts[1], ALU.subtract)


def stage_qkv(nc, G, I):
    GROUPS = HEADS // GH
    NORMED = 1 * BATCH
    with ExitStack() as ctx:
        M = Mem(nc, ctx)
        w_q, w_k, w_v = M.sb("wq_sb", [P, C]), M.sb("wk_sb", [P, C]), M.sb("wv_sb", [P, C])
        b_q, b_k, b_v = M.sb("bq1_sb", [P, 1]), M.sb("bk1_sb", [P, 1]), M.sb("bv1_sb", [P, C])
        x_new, xT = M.sb("qx_new", [P, TB, C]), M.sb("qxT", [P, SEQ])
        got, y = M.sb("got", [P, K0, TB, C]), M.sb("combined", [P, TB, C])
        got_here = M.sem("got_here")
        stats, mv = M.sb("qstats", [P, TB, 6]), M.sb("qmv", [P, TB, 2])
        var_eps, rstd = M.sb("qvar_eps", [P, TB]), M.sb("qrstd", [P, TB])
        qk = [M.sb("q_full", [P, SEQ]), M.sb("k_full", [P, SEQ])]
        rest = [M.sb("q_rest", [P, SEQ]), M.sb("k_rest", [P, SEQ])]
        parts = [M.sb("q_parts", [P, 3, SEQ], bf16), M.sb("k_parts", [P, 3, SEQ], bf16)]
        v_rows = M.sb("v_rows", [P, GROUPS, TB, GH, HD + 1])
        weights, ones_set = M.sem("weights"), M.sem("ones_set")
        norm_done, xT_psum, xT_done, x_kept = M.sem("norm_done"), M.sem("xT_psum"), M.sem("xT_done"), M.sem("x_kept")
        proj, qk_full = [M.sem("q_psum"), M.sem("k_psum")], [M.sem("q_full_done"), M.sem("k_full_done")]
        v_psum, v_done, v_kept = M.sem("v_psum"), M.sem("v_done"), M.sem("v_kept")
        part_done, rest_done, parts_kept = [M.sem("q_part"), M.sem("k_part")], [M.sem("q_rest_s"), M.sem("k_rest_s")], M.sem("parts_kept")
        steps = M.sem("steps")
        B = G.bank
        with nc.Block() as block:
            @block.sync
            def _(sp):
                for dst, name in ((w_q, "Wq"), (w_k, "Wk"), (w_v, "Wv"), (b_q, "bq"), (b_k, "bk")):
                    sp.dma_start(dst[:], I[name]).then_inc(weights, 16)
                sp.dma_start(b_v[:], I["bv"].to_broadcast([P, C])).then_inc(weights, 16)
                emit_combine_load(sp, 0, got, got_here, G.expert_out0, K0)

                def body(i, more):
                    sp.wait_ge(norm_done, i + 1)
                    if more:
                        emit_combine_load(sp, i + 1, got, got_here, G.expert_out0, K0)
                    sp.dma_start(G.x_rows[:, tiles(i), :], x_new[:]).then_inc(x_kept, 16)
                    sp.wait_ge(v_done, i * TB + TB)
                    sp.dma_start(G.v_steps[bass.ds(i * GROUPS, GROUPS)].rearrange("g p n -> p g n"),
                                 v_rows[:].rearrange("p g t h e -> p g (t h e)")).then_inc(v_kept, 16)
                    for s, store in enumerate((G.q_steps, G.k_steps)):
                        for j in range(3):
                            sp.wait_ge(part_done[s], i * 3 + j + 1)
                            sp.dma_start(store[bass.ds(i * GROUPS, GROUPS), j], parts[s][:, j, :])\
                              .then_inc(parts_kept, 16)
                body(0, True)
                with sp.Fori(1, BATCH - 1) as i:
                    body(i, True)
                body(BATCH - 1, False)
                sp.wait_ge(x_kept, BATCH * 16)
                sp.wait_ge(v_kept, BATCH * 16)
                sp.wait_ge(parts_kept, BATCH * 6 * 16)

            @block.gpsimd
            def _(pool):
                pool.memset(v_rows[:], 1.0).then_inc(ones_set, 1)
                @repeat(pool, BATCH)
                def _(i):
                    emit_norm_pool(pool, G, NORMED + i, var_eps, rstd)

            @block.tensor
            def _(pe):
                pe.wait_ge(weights, 6 * 16)
                @repeat(pe, BATCH)
                def _(i):
                    pe.wait_ge(norm_done, i + 1)
                    for t in range(TB):
                        mm = pe.transpose(B[t // 4][:, (t % 4) * P:(t % 4 + 1) * P], x_new[:, t, :], G.ident[:])
                        if t % 4 == 3:
                            mm.then_inc(xT_psum, 1)
                    for s, w in enumerate((w_q, w_k)):
                        for c in range(2):
                            if s == 0:
                                pe.wait_ge(xT_done, i * 2 + c + 1)
                            wait_past(pe, qk_full[s], i * 2)
                            pe.matmul(B[2 + 2 * s + c][:], w[:], xT[:, c * HALF:(c + 1) * HALF],
                                      start=True, stop=True).then_inc(proj[s], 1)
                    wait_past(pe, v_done, i * TB)
                    for t in range(TB):
                        mm = pe.matmul(B[6 + t // 4][:, (t % 4) * P:(t % 4 + 1) * P], xT[:, t * P:(t + 1) * P], w_v[:],
                                       start=(t % 4 == 0), stop=True, skip_group_check=True)
                        if t % 4 == 3:
                            mm.then_inc(v_psum, 1)

            @block.scalar
            def _(act):
                @repeat(act, BATCH)
                def _(i):
                    wait_past(act, v_psum, i * 2)
                    for c in range(2):
                        act.wait_ge(xT_psum, i * 2 + c + 1)
                        act.activation(xT[:, c * HALF:(c + 1) * HALF], B[c][:], ACT.Copy).then_inc(xT_done, 1)
                    for s in range(2):
                        act.wait_ge(qk_full[s], i * 2 + 2)
                        wait_past(act, parts_kept, i * 96)
                        act.activation(parts[s][:, 0, :], qk[s][:], ACT.Copy).then_inc(part_done[s], 1)
                    for s in range(2):
                        act.wait_ge(rest_done[s], i + 1)
                        act.activation(parts[s][:, 1, :], rest[s][:], ACT.Copy).then_inc(part_done[s], 1)

            @block.vector
            def _(dve):
                dve.wait_ge(weights, 6 * 16)
                dve.wait_ge(ones_set, 1)
                @repeat(dve, BATCH)
                def _(i):
                    order = Order(dve, steps, i * (K0 + 3))
                    dve.wait_ge(got_here, i * (K0 * 16) + K0 * 16)
                    emit_combine(dve, order, i, got, G.gate0, K0, G.x_rows[:, tiles(i), :], y[:])
                    wait_past(dve, x_kept, i * 16)
                    last = emit_norm_vector(dve, G, order, NORMED + i, lambda t: y[:, t, :], stats, mv, var_eps, rstd,
                                            lambda t: x_new[:, t, :])
                    last.then_inc(norm_done, 1)
                    for s, (bias, scale) in enumerate(((b_q, float(1 / np.sqrt(np.float32(HD)))), (b_k, 1.0))):
                        for c in range(2):
                            dve.wait_ge(proj[s], i * 2 + c + 1)
                            dve.tensor_scalar(qk[s][:, c * HALF:(c + 1) * HALF], B[2 + 2 * s + c][:], bias[:], scale,
                                              ALU.add, ALU.mult).then_inc(qk_full[s], 1)
                    wait_past(dve, v_kept, i * 16)
                    for t in range(TB):
                        if t % 4 == 0:
                            dve.wait_ge(v_psum, i * 2 + t // 4 + 1)
                        dve.tensor_tensor(v_rows[:, :, t, :, 0:HD],
                                          B[6 + t // 4][:, (t % 4) * P:(t % 4 + 1) * P].rearrange("p (g h e) -> p g h e", g=GROUPS, h=GH),
                                          b_v[:].rearrange("p (g h e) -> p g h e", g=GROUPS, h=GH), ALU.add).then_inc(v_done, 1)
                    for s in range(2):
                        dve.wait_ge(part_done[s], i * 3 + 1)
                        dve.tensor_tensor(rest[s][:], qk[s][:], parts[s][:, 0, :], ALU.subtract).then_inc(rest_done[s], 1)
                    for s in range(2):
                        dve.wait_ge(part_done[s], i * 3 + 2)
                        dve.tensor_tensor(parts[s][:, 2, :], rest[s][:], parts[s][:, 1, :], ALU.subtract).then_inc(part_done[s], 1)
                    assert order.count == K0 + 3


def max_units():
    units = []
    for qt in range(TB):
        for seg in range(qt // 4 + 1):
            width = min(HALF, (qt + 1) * P - seg * HALF)
            heads = max(1, min(GH, HALF // width))
            if qt == 0:
                heads = 2
            units += [(qt, seg, h, heads, width) for h in range(0, GH, heads)]
    return units + ["maxima"]


EXP_UNITS = [(c, j) for c in range(2) for j in range(4 * c + 4)]
MAX_UNITS = max_units()
EARLY = 7
AT_SECOND, AT_FIRST = 2, 7
BUFS = 3
PRING = 3


class Step:

    def __init__(self, n, buf, used):
        self.n, self.buf, self.used = n, buf, used

    def next(self, by=1):
        b = self.buf + by
        return Step(self.n + by, b % BUFS, self.used + b // BUFS)


def schedule(first, more, more2):
    work = [("max", 1, u) for u in MAX_UNITS[EARLY:]] if more else []
    work2 = [("max", 2, u) for u in MAX_UNITS[:EARLY]] if more2 else []
    slots = []
    K = len(EXP_UNITS)
    for k in range(K):
        if k < K - 2:
            a, b = len(work) * k // (K - 2), len(work) * (k + 1) // (K - 2)
            slot = work[a:b]
        else:
            a, b = len(work2) * (k - K + 2) // 2, len(work2) * (k - K + 3) // 2
            slot = work2[a:b]
        if k == AT_SECOND and not first:
            slot = slot + [("out", -1, 1)]
        if k == AT_FIRST:
            slot = slot + [("out", 0, 0)]
        slots.append(slot)
    return slots


def step_plan():
    def flags(n):
        return n == 0, n + 1 < STEPS, n + 2 < STEPS
    count = lambda n: sum(map(len, schedule(*flags(n))))
    base = [len(MAX_UNITS) + EARLY]
    for n in range(STEPS):
        base.append(base[-1] + count(n))
    assert all(base[n] == base[1] + (n - 1) * (base[2] - base[1]) for n in range(1, STEPS - 1)), base
    assert (base[2] - base[1]) % 2 == 0
    return flags, base


def run_steps(engine, body):
    flags, base = step_plan()
    per = base[2] - base[1]
    body(Step(0, 0, 0), base[0], base[0] % 2, flags(0))
    rounds = (STEPS - 1 - 2) // BUFS
    with engine.Fori(0, rounds) as i:
        for r in range(BUFS):
            n = 1 + r
            body(Step(i * BUFS + n, n % BUFS, i + n // BUFS), i * (BUFS * per) + base[n], base[n] % 2, flags(n))
    for n in range(1 + rounds * BUFS, STEPS):
        body(Step(n, n % BUFS, n // BUFS), base[n], base[n] % 2, flags(n))
    return base[STEPS]


def stage_attention(nc, G, I):
    W4 = GH * SEQ
    with ExitStack() as ctx:
        M = Mem(nc, ctx)
        qa = [M.sb(f"qa{b}", [P, GH, SEQ], bf16) for b in range(BUFS)]
        ka = [M.sb(f"ka{b}", [P, GH, SEQ], bf16) for b in range(BUFS)]
        va = [M.sb(f"va{b}", [P, TB, GH, HD + 1]) for b in range(BUFS)]
        probs = [M.sb(f"probs{b}", [P, GH, HALF]) for b in range(PRING)]
        outT = [M.sb(f"outT{c}", [P, HALF]) for c in range(2)]
        maxima, neg_max = M.sb("maxima", [P, 2, GH, TB]), M.sb("neg_max", [P, TB * GH])
        max_parts, max_rest = M.sb("max_parts", [TB * GH, 3, P], bf16), M.sb("max_rest", [TB * GH, P])
        recip = [M.sb(f"recip{c}", [P, 4, GH]) for c in range(2)]
        mark = M.sb("mark", [P, 1])
        ident_b, mask_q, mask_k = M.sb("ident_b", [P, P], bf16), M.sb("mask_q", [P, P], bf16), M.sb("mask_k", [P, P], bf16)
        here = [M.sem(f"operands_here{b}") for b in range(BUFS)]
        max_here = [M.sem(f"max_rows_here{b}") for b in range(BUFS)]
        preset, masks, ones_here = M.sem("preset"), M.sem("masks"), M.sem("ones_here")
        scores, exps, pv = M.sem("scores"), M.sem("exps"), M.sem("pv")
        small, small_read, out_read, split = M.sem("small"), M.sem("small_read"), M.sem("out_read"), M.sem("split")
        order_sem, rows_done, neg_done = M.sem("order"), M.sem("rows_done"), M.sem("neg_done")
        PS, B = G.psum, G.bank
        SMALL, OUT = (4, 5), (6, 7)
        Q = len(EXP_UNITS)
        flags_of, base_of = step_plan()

        def emit_load(sp, s):
            def sl(store):
                return store[bass.ds(s.n, 1)] if not isinstance(s.n, int) else store[s.n:s.n + 1]
            q = sl(G.q_steps)
            k = sl(G.k_steps)
            for j in range(3):
                sp.dma_start(qa[s.buf][j * HD * 3:(j + 1) * HD * 3].rearrange("r h n -> r (h n)"),
                             q.rearrange("o i (d h) n -> (o d) i (h n)", d=HD)).then_inc(here[s.buf], 16)
            sp.dma_start(ka[s.buf][0:PROD].rearrange("r h n -> r (h n)"),
                         k.rearrange("o j (d h) n -> (o j d) (h n)", d=HD)[:, None, :].to_broadcast([3 * HD, 3, W4])
                         ).then_inc(here[s.buf], 16)
            sp.dma_start(va[s.buf][:].rearrange("p t h e -> p (t h e)"),
                         sl(G.v_steps).rearrange("o p n -> (o p) n")).then_inc(here[s.buf], 16)
            al = I["c_alibi"]
            al = al[bass.ds(s.n, 1)] if not isinstance(s.n, int) else al[s.n:s.n + 1]
            sp.dma_start(ka[s.buf][ALIBI_AT:ALIBI_AT + 6].rearrange("r h n -> r (h n)"),
                         al.rearrange("o r n -> (o r) n")).then_inc(here[s.buf], 16)
        LOADS = 6 * 16

        def emit_max_rows(sp, s):
            sp.wait_ge(split, s.n + 1)
            for r in range(3):
                sp.dma_start(qa[s.buf][MAX_AT + r:MAX_AT + r + 1].rearrange("o h (t q) -> o (h t) q", q=P),
                             max_parts[:, r, :]).then_inc(max_here[s.buf], 16)

        with nc.Block() as block:
            @block.gpsimd
            def _(pool):
                pool.memset(ident_b[:], 0.0).then_inc(preset, 1)
                pool.memset(mask_q[:], 0.0).then_inc(preset, 1)
                pool.memset(mask_k[:], 0.0).then_inc(preset, 1)
                pool.memset(maxima[:], -3.0e38).then_inc(preset, 1)
                pool.wait_ge(preset, 4)
                pool.affine_select(out=ident_b[:], in_=ident_b[:], compare_op=ALU.not_equal, fill=1.0,
                                   base=0, pattern=[[-1, P]], channel_multiplier=1).then_inc(masks, 1)
                pool.affine_select(out=mask_q[:], in_=mask_q[:], compare_op=ALU.is_ge, fill=MASKED,
                                   base=0, pattern=[[-1, P]], channel_multiplier=1).then_inc(masks, 1)
                pool.affine_select(out=mask_k[:], in_=mask_k[:], compare_op=ALU.is_ge, fill=MASKED,
                                   base=0, pattern=[[1, P]], channel_multiplier=-1).then_inc(masks, 1)

            @block.sync
            def _(sp):
                for b in range(BUFS):
                    sp.dma_start(qa[b][ALIBI_AT:ALIBI_AT + 3].rearrange("r h n -> r (h n)"),
                                 I["c_alibi"][0, 3:6, :]).then_inc(ones_here, 16)
                emit_load(sp, Step(0, 0, 0))
                emit_load(sp, Step(1, 1, 0))
                emit_max_rows(sp, Step(0, 0, 0))

                def body(s, base, odd, flags):
                    first, more, more2 = flags
                    if more2:
                        if not first:
                            sp.wait_ge(pv, s.n * Q)
                            sp.wait_ge(ones_here, BUFS * 16)
                        emit_load(sp, s.next(2))
                    if more:
                        emit_max_rows(sp, s.next())
                run_steps(sp, body)

            @block.tensor
            def _(pe):
                pe.wait_ge(masks, 3)
                pe.wait_ge(ones_here, BUFS * 16)
                pe.wait_ge(rows_done, 1)

                def emit_small(number, odd, s, what):
                    kind, ahead, u = what
                    bank = B[SMALL[odd]]
                    if not isinstance(number, int) or number >= 2:
                        pe.wait_ge(small_read, number - 1)
                    if kind == "out":
                        pe.wait_ge(out_read, (s.n + ahead) * 2 + u + 1)
                        for t in range(4):
                            mm = pe.transpose(bank[:, t * P:(t + 1) * P], outT[u][:, t * P:(t + 1) * P], G.ident[:])
                    elif u == "maxima":
                        pe.wait_ge(small_read, number)
                        pe.wait_ge(neg_done, s.n + ahead + 1)
                        mm = pe.transpose(bank[0:TB * GH, 0:P], neg_max[:], G.ident[:])
                    else:
                        b = (s.buf + ahead) % BUFS
                        qt, seg, h0, heads, width = u
                        if u == MAX_UNITS[0]:
                            t = s.next(ahead) if ahead else s
                            pe.wait_ge(here[b], t.used * LOADS + LOADS)
                        for h in range(heads):
                            mm = pe.matmul(bank[:, h * width:(h + 1) * width], qa[b][0:ROWS_MAX, h0 + h, qt * P:(qt + 1) * P],
                                           ka[b][0:ROWS_MAX, h0 + h, seg * HALF:seg * HALF + width],
                                           start=(h == 0), stop=True, skip_group_check=True)
                        if seg * HALF + width == (qt + 1) * P:
                            for h in range(heads):
                                mm = pe.matmul(bank[:, (h + 1) * width - P:(h + 1) * width], ident_b[:], mask_q[:],
                                               start=False, stop=True, skip_group_check=True)
                    mm.then_inc(small, 1)

                def emit_scores(s, k, pair):
                    c, j = EXP_UNITS[k]
                    q0 = max(c * HALF, j * P)
                    if k or not isinstance(s.n, int) or s.n:
                        pe.wait_ge(exps, s.n * (2 * Q) + 2 * k + pair - 1)
                    for h in (2 * pair, 2 * pair + 1):
                        out = B[h][:, 0:(c + 1) * HALF - q0]
                        mm = pe.matmul(out, ka[s.buf][0:ROWS_ALL, h, j * P:(j + 1) * P],
                                       qa[s.buf][0:ROWS_ALL, h, q0:(c + 1) * HALF], start=True, stop=True,
                                       skip_group_check=True)
                        if q0 == j * P:
                            mm = pe.matmul(out[:, 0:P], ident_b[:], mask_k[:], start=False, stop=True,
                                           skip_group_check=True)
                    mm.then_inc(scores, 1)

                def emit_pv(s, k):
                    c, j = EXP_UNITS[k]
                    q0 = max(c * HALF, j * P)
                    pe.wait_ge(exps, s.n * (2 * Q) + 2 * k + 2)
                    if j == 0 and (not isinstance(s.n, int) or s.n):
                        pe.wait_ge(out_read, s.n * 2 - 1 + c)
                    for h in range(GH):
                        mm = pe.matmul(B[OUT[c]][32 * h:32 * h + HD + 1, q0 - c * HALF:HALF],
                                       va[s.buf][:, j, h, :], probs[k % PRING][:, h, 0:(c + 1) * HALF - q0],
                                       start=(j == 0), stop=(j == 4 * c + 3), skip_group_check=True)
                    mm.then_inc(pv, 1)

                number = 0
                for s, units in ((Step(0, 0, 0), MAX_UNITS), (Step(1, 1, 0), MAX_UNITS[:EARLY])):
                    for u in units:
                        emit_small(number, number % 2, s, ("max", 0, u))
                        number += 1

                def body(s, base, odd, flags):
                    pe.wait_ge(max_here[s.buf], s.used * 48 + 48)
                    n = 0
                    for k, slot in enumerate(schedule(*flags)):
                        apart = [slot[:len(slot) // 3], slot[len(slot) // 3:2 * len(slot) // 3], slot[2 * len(slot) // 3:]]
                        for part, pair in zip(apart, (0, 1, None)):
                            for what in part:
                                emit_small(base + n, (odd + n) % 2, s, what)
                                n += 1
                            if pair is not None:
                                emit_scores(s, k, pair)
                        if k:
                            emit_pv(s, k - 1)
                        elif not flags[0]:
                            before = Step(s.n - 1, (s.buf - 1) % BUFS, 0)
                            emit_pv(before, Q - 1)
                base = run_steps(pe, body)
                last = Step(STEPS - 1, (STEPS - 1) % BUFS, 0)
                emit_pv(last, Q - 1)
                emit_small(base, base % 2, last, ("out", 0, 1))

            @block.scalar
            def _(act):
                def emit_out(s, c, before):
                    act.wait_ge(pv, s.n * Q + (4 if c == 0 else Q))
                    if before is not None:
                        act.wait_ge(small, before)
                    act.activation(outT[c][:], B[OUT[c]], ACT.Copy).then_inc(out_read, 1)

                def at_out(flags, c):
                    n = 0
                    for slot in schedule(*flags):
                        for what in slot:
                            n += 1
                            if what[0] == "out" and what[2] == c:
                                return n

                def body(s, base, odd, flags):
                    for k in range(Q):
                        c, j = EXP_UNITS[k]
                        q0 = max(c * HALF, j * P)
                        w = (c + 1) * HALF - q0
                        if k >= PRING or not flags[0]:
                            act.wait_ge(pv, s.n * Q + k - PRING + 1)
                        for pair in range(2):
                            act.wait_ge(scores, s.n * (2 * Q) + 2 * k + pair + 1)
                            act.activation(probs[k % PRING][:, 2 * pair:2 * pair + 2, 0:w],
                                           PS[:, 2 * pair:2 * pair + 2, 0:w], ACT.Exp).then_inc(exps, 1)
                        if k == AT_SECOND - 1 and not flags[0]:
                            emit_out(Step(s.n - 1, 0, 0), 1, base)
                        if k == AT_FIRST - 2:
                            emit_out(s, 0, None if flags[0] else base)
                run_steps(act, body)
                emit_out(Step(STEPS - 1, 0, 0), 1, base_of[STEPS])

            @block.vector
            def _(dve):
                for c in range(2):
                    last = dve.memset(B[OUT[c]], 0.0)
                last.then_inc(rows_done, 1)
                dve.wait_ge(masks, 3)
                dve.wait_ge(preset, 4)

                def emit_small(number, odd, s, what, order):
                    kind, ahead, u = what
                    bank = B[SMALL[odd]]
                    dve.wait_ge(small, number + 1)
                    if kind == "out":
                        v = bank.rearrange("p (t h e) -> p t h e", t=4, h=GH)
                        order.done(dve.reciprocal(recip[u][:], v[:, :, :, HD]))
                        n = s.n + ahead
                        dst = G.att_steps[:, bass.ds(n * 2 + u, 1)] if not isinstance(n, int) else G.att_steps[:, n * 2 + u:n * 2 + u + 1]
                        dve.tensor_tensor(dst.rearrange("p o t (h e) -> p (o t) h e", h=GH), v[:, :, :, 0:HD],
                                          recip[u][:, :, :, None].to_broadcast([P, 4, GH, HD]), ALU.mult).then_inc(small_read, 1)
                    elif u == "maxima":
                        n = s.n + ahead
                        order.done(dve.tensor_copy(max_parts[:, 0, :], bank[0:TB * GH, 0:P]))
                        order.done(dve.tensor_tensor(max_rest[:], bank[0:TB * GH, 0:P], max_parts[:, 0, :], ALU.subtract))
                        order.done(dve.tensor_copy(max_parts[:, 1, :], max_rest[:]))
                        dve.tensor_tensor(max_parts[:, 2, :], max_rest[:], max_parts[:, 1, :], ALU.subtract).then_inc(split, 1)
                        dve.wait_ge(split, n + 1)
                        dve.memset(mark[:], 0.0).then_inc(small_read, 1)
                    else:
                        qt, seg, h0, heads, width = u
                        dve.tensor_reduce(maxima[:, seg, h0:h0 + heads, qt],
                                          bank[:, 0:heads * width].rearrange("p (h k) -> p h k", h=heads),
                                          AX.X, ALU.max).then_inc(small_read, 1)
                        if u == MAX_UNITS[-2]:
                            t = s.next(ahead) if ahead else s
                            dve.wait_ge(small_read, number + 1)
                            order.done(dve.tensor_tensor(neg_max[:], maxima[:, 0].rearrange("p h t -> p (h t)"),
                                                         maxima[:, 1].rearrange("p h t -> p (h t)"), ALU.max))
                            dve.tensor_scalar(neg_max[:], neg_max[:], -1.0, None, ALU.mult).then_inc(neg_done, 1)
                            if not isinstance(t.n, int) or t.n:
                                b = (t.buf - 1) % BUFS
                                dve.wait_ge(max_here[b], (t.used + (0 if t.buf else -1)) * 48 + 48)

                number = 0
                order = Order(dve, order_sem)
                for s, units in ((Step(0, 0, 0), MAX_UNITS), (Step(1, 1, 0), MAX_UNITS[:EARLY])):
                    for u in units:
                        emit_small(number, number % 2, s, ("max", 0, u), order)
                        number += 1
                before = order.count
                PER = 6

                def body(s, base, odd, flags):
                    order = Order(dve, order_sem, before + 5 + (s.n - 1) * PER if not flags[0] else before)
                    n = 0
                    for slot in schedule(*flags):
                        for what in slot:
                            emit_small(base + n, (odd + n) % 2, s, what, order)
                            n += 1
                    assert order.count == (5 if flags[0] else PER if flags[1] else 2), order.count
                base = run_steps(dve, body)
                order = Order(dve, order_sem, before + 5 + (STEPS - 2) * PER + 2)
                emit_small(base, base % 2, Step(STEPS - 1, 0, 0), ("out", 0, 1), order)
                dve.wait_ge(small_read, base + 1)



def stage_projection(nc, G, I):
    GROUPS = HEADS // GH
    NORMED = 2 * BATCH
    with ExitStack() as ctx:
        M = Mem(nc, ctx)
        w_o, b_o = M.sb("wo_sb", [P, C]), M.sb("bo_sb", [P, C])
        w_r, b_r = M.sb("wr1_sb", [P, E1]), M.sb("br1_sb", [P, E1])
        att, attT = M.sb("p_att", [P, TB, GROUPS, GH * HD]), M.sb("p_attT", [P, SEQ])
        x_bias, y, x_new, xT = M.sb("p_bias", [P, TB, C]), M.sb("p_y", [P, TB, C]), M.sb("p_new", [P, TB, C]), M.sb("p_xT", [P, SEQ])
        stats, mv = M.sb("p_stats", [P, TB, 6]), M.sb("p_mv", [P, TB, 2])
        var_eps, rstd = M.sb("p_var_eps", [P, TB]), M.sb("p_rstd", [P, TB])
        weights = M.sem("weights")
        att_fixed, attT_psum, attT_done = M.sem("att_fixed"), M.sem("attT_psum"), M.sem("attT_done")
        y_psum, y_taken, xb_done = M.sem("y_psum"), M.sem("y_taken"), M.sem("xb_done")
        norm_done, x_kept, xT_psum, xT_done = M.sem("norm_done"), M.sem("x_kept"), M.sem("xT_psum"), M.sem("xT_done")
        logits_psum, logits_done, xT_kept, steps = M.sem("logits_psum"), M.sem("logits_done"), M.sem("xT_kept"), M.sem("steps")
        B = G.bank
        with nc.Block() as block:
            @block.sync
            def _(sp):
                sp.dma_start(w_o[:], I["Wo"]).then_inc(weights, 16)
                sp.dma_start(b_o[:], I["bo"].to_broadcast([P, C])).then_inc(weights, 16)
                sp.dma_start(w_r[:], I["Wr1"]).then_inc(weights, 16)
                sp.dma_start(b_r[:], I["br1"].to_broadcast([P, E1])).then_inc(weights, 16)
                @repeat(sp, BATCH)
                def _(i):
                    sp.wait_ge(norm_done, i + 1)
                    sp.dma_start(G.x_rows[:, tiles(i), :], x_new[:]).then_inc(x_kept, 16)
                    sp.wait_ge(xT_done, i * 2 + 2)
                    sp.dma_start(G.xT[:, bass.ds(i * SEQ, SEQ)], xT[:]).then_inc(xT_kept, 16)
                sp.wait_ge(x_kept, BATCH * 16)
                sp.wait_ge(xT_kept, BATCH * 16)

            @block.gpsimd
            def _(pool):
                pool.wait_ge(weights, 4 * 16)
                @repeat(pool, BATCH)
                def _(i):
                    wait_past(pool, y_taken, i * 2)
                    pool.tensor_tensor(x_bias[:], G.x_rows[:, tiles(i), :],
                                       b_o[:, None, :].to_broadcast([P, TB, C]), ALU.add).then_inc(xb_done, 1)
                    emit_norm_pool(pool, G, NORMED + i, var_eps, rstd)

            @block.tensor
            def _(pe):
                pe.wait_ge(weights, 4 * 16)
                @repeat(pe, BATCH)
                def _(i):
                    pe.wait_ge(att_fixed, i + 1)
                    wait_past(pe, xT_done, i * 2)
                    for t in range(TB):
                        mm = pe.transpose(B[t // 4][:, (t % 4) * P:(t % 4 + 1) * P], att[:, t].rearrange("p g e -> p (g e)"), G.ident[:])
                        if t % 4 == 3:
                            mm.then_inc(attT_psum, 1)
                    wait_past(pe, y_taken, i * 2)
                    for t in range(TB):
                        if t % 4 == 0:
                            pe.wait_ge(attT_done, i * 2 + t // 4 + 1)
                        mm = pe.matmul(B[2 + t // 4][:, (t % 4) * C:(t % 4 + 1) * C], attT[:, t * P:(t + 1) * P],
                                       w_o[:], start=(t % 4 == 0), stop=True, skip_group_check=True)
                        if t % 4 == 3:
                            mm.then_inc(y_psum, 1)
                    pe.wait_ge(norm_done, i + 1)
                    for t in range(TB):
                        mm = pe.transpose(B[t // 4][:, (t % 4) * P:(t % 4 + 1) * P], x_new[:, t, :], G.ident[:])
                        if t % 4 == 3:
                            mm.then_inc(xT_psum, 1)
                    pe.wait_ge(xT_done, i * 2 + 2)
                    wait_past(pe, logits_done, i)
                    for t in range(TB):
                        mm = pe.matmul(B[4][:, t * E1:(t + 1) * E1], xT[:, t * P:(t + 1) * P], w_r[:],
                                       start=(t == 0), stop=True, skip_group_check=True)
                    mm.then_inc(logits_psum, 1)

            @block.scalar
            def _(act):
                @repeat(act, BATCH)
                def _(i):
                    wait_past(act, attT_psum, i * 2)
                    act.activation(att[:].rearrange("p t g e -> p g t e"),
                                   G.att_steps[:, bass.ds(i * 2 * GROUPS, 2 * GROUPS)].rearrange("p (g c) t e -> p g (c t) e", c=2),
                                   ACT.Copy).then_inc(att_fixed, 1)
                    for c in range(2):
                        act.wait_ge(attT_psum, i * 2 + c + 1)
                        act.activation(attT[:, c * HALF:(c + 1) * HALF], B[c], ACT.Copy).then_inc(attT_done, 1)
                    wait_past(act, xT_kept, i * 16)
                    wait_past(act, logits_psum, i)
                    for c in range(2):
                        act.wait_ge(xT_psum, i * 2 + c + 1)
                        act.activation(xT[:, c * HALF:(c + 1) * HALF], B[c], ACT.Copy).then_inc(xT_done, 1)

            @block.vector
            def _(dve):
                dve.wait_ge(weights, 4 * 16)
                @repeat(dve, BATCH)
                def _(i):
                    order = Order(dve, steps, i * 2)
                    dve.wait_ge(xb_done, i + 1)
                    for c in range(2):
                        dve.wait_ge(y_psum, i * 2 + c + 1)
                        dve.tensor_tensor(y[:, 4 * c:4 * c + 4, :], B[2 + c].rearrange("p (t n) -> p t n", t=4),
                                          x_bias[:, 4 * c:4 * c + 4, :], ALU.add).then_inc(y_taken, 1)
                    dve.wait_ge(y_taken, i * 2 + 2)
                    wait_past(dve, x_kept, i * 16)
                    last = emit_norm_vector(dve, G, order, NORMED + i, lambda t: y[:, t, :], stats, mv, var_eps, rstd, lambda t: x_new[:, t, :])
                    last.then_inc(norm_done, 1)
                    dve.wait_ge(logits_psum, i + 1)
                    dve.tensor_tensor(G.logits1[:, tiles(i), :], B[4][:, 0:TB * E1].rearrange("p (t e) -> p t e", e=E1),
                                      b_r[:, None, :].to_broadcast([P, TB, E1]), ALU.add).then_inc(logits_done, 1)
                    assert order.count == 2


def stage_route1(nc, G, I):
    HC = HS // P
    HALVES = N // HALF
    with ExitStack() as ctx:
        M = Mem(nc, ctx)
        R = Router(M, G, E1, K1, "r1")
        w_g, w_u, w_d = M.sb("sg_sb", [P, HS]), M.sb("su_sb", [P, HS]), M.sb("sd_sb", [P, HC, C])
        silu, hT = [M.sb(f"s_silu{u}", [P, HALF]) for u in range(2)], M.sb("s_hT", [P, HC, HALF])
        tiles_i, tiles_f = M.sb("tiles_i", [P, E1], i32), M.sb("tiles_f", [P, E1])
        ends, starts = M.sb("ends", [P, E1]), M.sb("starts", [P, E1])
        compared, expert_f = M.sb("cmp", [P, E1]), M.sb("expert_f", [P, 2])
        loaded, placed, rows_ready, scattered = M.sem("loaded"), M.sem("placed"), M.sem("rows_ready"), M.sem("scattered")
        expert_done, expert_psum, experts_loaded = M.sem("expert_done"), M.sem("expert_psum"), M.sem("experts_loaded")
        gu_psum, silu_done, h_done, y_psum, acc_done = M.sem("gu_psum"), M.sem("silu_done"), M.sem("h_done"), M.sem("y_psum"), M.sem("acc_done")
        B = G.bank
        before_bank, total_bank = [B[0], B[1]], [B[2], B[3]]
        with nc.Block() as block:
            @block.sync
            def _(sp):
                sp.dma_start(R.goes_on[:].rearrange("p e t -> p (e t)"),
                             I["c_goes_on"].to_broadcast([P, E1 * TILES])).then_inc(loaded, 16)
                sp.dma_start(w_g[:], I["sg"]).then_inc(loaded, 16)
                sp.dma_start(w_u[:], I["su"]).then_inc(loaded, 16)
                sp.dma_start(w_d[:], I["sd"]).then_inc(loaded, 16)
                sp.dma_start(G.w_gu[:], I["gu"]).then_inc(experts_loaded, 16)
                sp.dma_start(G.w_down[:], I["down"]).then_inc(experts_loaded, 16)
                sp.wait_ge(experts_loaded, 32)

            @block.gpsimd
            def _(pool):
                pool.wait_ge(rows_ready, 1)
                emit_scatter(pool, G, G.to_row1, K1, G.sorted1, ROWS1 - 1, placed, scattered)

            @block.tensor
            def _(pe):
                emit_count_tensor(pe, R, 1, R.member, before_bank, total_bank)
                pe.wait_ge(expert_done, 1)
                for c in range(2):
                    mm = pe.matmul(B[0][0:1, c * P:(c + 1) * P], expert_f[:, c:c + 1], G.ident[:],
                                   start=(c == 0), stop=True, skip_group_check=True)
                mm.then_inc(expert_psum, 1)
                pe.wait_ge(loaded, 4 * 16)
                @repeat(pe, HALVES)
                def _(i):
                    for c in range(HC):
                        if c < 2:
                            wait_past(pe, h_done, i * HC)
                        else:
                            wait_past(pe, h_done, i * HC + c - 1)
                        for n, w in enumerate((w_g, w_u)):
                            mm = pe.matmul(B[4 + 2 * (c % 2) + n], w[:, c * P:(c + 1) * P],
                                           G.xT[:, bass.ds(i * HALF, HALF)], start=True, stop=True)
                        mm.then_inc(gu_psum, 1)
                    pe.wait_ge(h_done, i * HC + HC)
                    wait_past(pe, acc_done, i)
                    for t in range(4):
                        for c in range(HC):
                            mm = pe.matmul(B[1][:, t * C:(t + 1) * C], hT[:, c, t * P:(t + 1) * P], w_d[:, c, :],
                                           start=(t == 0 and c == 0), stop=(c == HC - 1), skip_group_check=True)
                    mm.then_inc(y_psum, 1)

            @block.scalar
            def _(act):
                emit_exp(act, R)
                @repeat(act, HALVES)
                def _(i):
                    for c in range(HC):
                        act.wait_ge(gu_psum, i * HC + c + 1)
                        if c < 2:
                            wait_past(act, h_done, i * HC)
                        else:
                            wait_past(act, h_done, i * HC + c - 1)
                        act.activation(silu[c % 2][:], B[4 + 2 * (c % 2)], ACT.Silu).then_inc(silu_done, 1)

            @block.vector
            def _(dve):
                order = Order(dve, R.vec)
                emit_softmax_topk(dve, order, R, G.logits1)
                dve.memset(tiles_f[:], 0.0).then_inc(R.to_count, 1)
                dve.wait_ge(loaded, 4 * 16)
                emit_positions(dve, order, R, 1, before_bank, total_bank)
                order.done(dve.tensor_scalar(tiles_i[:], R.scanned[:, :, TILES - 1], float(P - 1), None, ALU.add))
                order.done(dve.tensor_scalar(tiles_i[:], tiles_i[:], 7, None, ALU.arith_shift_right))
                order.done(dve.tensor_copy(tiles_f[:], tiles_i[:]))
                order.done(dve.tensor_tensor_scan(ends[:], G.ones[:, 0:E1], tiles_f[:], 0.0, ALU.mult, ALU.add))
                order.done(dve.tensor_tensor(starts[:], ends[:], tiles_f[:], ALU.subtract))
                order.done(dve.tensor_scalar(starts[:], starts[:], float(P), None, ALU.mult))
                order.done(dve.tensor_tensor(R.position[:], R.position[:], starts[:, None, :].to_broadcast([P, TILES, E1]), ALU.add))
                for k in range(K1):
                    emit_pick(dve, order, R, k, R.position, R.row[:])
                    order.done(dve.tensor_copy(G.to_row1[:, :, k], R.row[:]))
                dve.memset(compared[:], 0.0).then_inc(rows_ready, 1)
                dve.wait_ge(rows_ready, 1)
                for c in range(2):
                    order.done(dve.tensor_scalar(compared[:], ends[:], G.iota_p[:, c:c + 1], None, ALU.is_le, ALU.add,
                                                 accum_out=expert_f[:, c:c + 1]))
                dve.tensor_scalar(expert_f[:], expert_f[:], float(E1 - 1), None, ALU.min).then_inc(expert_done, 1)
                order.done(dve.tensor_reduce(R.total[:], R.top[:, :, 0:K1], AX.X, ALU.add))
                order.done(dve.tensor_scalar(R.total[:], R.total[:], 1e-12, None, ALU.max))
                order.done(dve.reciprocal(R.total[:], R.total[:]))
                order.done(dve.tensor_tensor(G.gate1[:], R.top[:, :, 0:K1], R.total[:, :, None].to_broadcast([P, TILES, K1]), ALU.mult))
                dve.wait_ge(expert_psum, 1)
                order.done(dve.tensor_copy(G.tile_expert[:], B[0][0:1, 0:2 * P]))
                @repeat(dve, HALVES)
                def _(i):
                    for c in range(HC):
                        dve.wait_ge(silu_done, i * HC + c + 1)
                        wait_past(dve, y_psum, i)
                        dve.tensor_tensor(hT[:, c, :], B[5 + 2 * (c % 2)], silu[c % 2][:], ALU.mult).then_inc(h_done, 1)
                    dve.wait_ge(y_psum, i + 1)
                    dve.tensor_tensor(G.acc[:, bass.ds(i * 4, 4), :], B[1].rearrange("p (t n) -> p t n", t=4),
                                      G.x_rows[:, bass.ds(i * 4, 4), :], ALU.add).then_inc(acc_done, 1)


def stage_experts1(nc, G, I):
    FT, RING = 4, 4
    GROUPS = TILES1 // FT
    with ExitStack() as ctx:
        M = Mem(nc, ctx)
        two = range(2)
        w_gu, w_d = G.w_gu, G.w_down
        rows = [M.sb(f"g_rows{v}", [P, FT, WIDE]) for v in range(RING)]
        place, place_done = M.sb("g_place", [P, TILES1], u32), M.sem("place_done")
        xT = [M.sb(f"g_xT{u}", [P, FT * P]) for u in two]
        silu, h = [M.sb(f"g_silu{u}", [P, FT, H1]) for u in two], [M.sb(f"g_h{u}", [P, FT, H1]) for u in two]
        hT, y = [M.sb(f"g_hT{u}", [P, FT * P]) for u in two], [M.sb(f"g_y{v}", [P, FT, C]) for v in range(RING)]
        here, kept = [M.sem(f"rows_here{v}") for v in range(RING)], [M.sem(f"y_kept{v}") for v in range(RING)]
        xT_psum, xT_done, gu_psum, silu_done, h_done = M.sem("xT_psum"), M.sem("xT_done"), M.sem("gu_psum"), M.sem("silu_done"), M.sem("h_done")
        hT_psum, hT_done, y_psum, y_done = M.sem("hT_psum"), M.sem("hT_done"), M.sem("y_psum"), M.sem("y_done")
        B = G.bank
        GU = lambda u: G.psum[:, 2 + 2 * u:4 + 2 * u, :].rearrange("p b (s x h) -> p (b s) x h", s=2, x=2)

        def rolled(engine, body, head, tail):
            assert (GROUPS - head - tail) % RING == 0
            for n in range(head):
                body(n, n % RING)
            with engine.Fori(0, (GROUPS - head - tail) // RING) as i:
                for r in range(RING):
                    body(i * RING + head + r, (head + r) % RING)
            for n in range(GROUPS - tail, GROUPS):
                body(n, n % RING)

        def uses(n, v, each):
            return n // RING * each if isinstance(n, int) else (n - v) * (each // RING)

        with nc.Block() as block:
            @block.sync
            def _(sp):
                def load(n, v):
                    if not isinstance(n, int) or n >= RING:
                        sp.wait_ge(xT_psum, n - RING + 1)
                        sp.wait_ge(place_done, n - RING + 1)
                    sp.dma_start(rows[v][:], G.sorted1[bass.ds(n * (FT * P), FT * P), :]
                                 .rearrange("(s p) c -> p s c", p=P)).then_inc(here[v], 16)
                rolled(sp, load, RING, 0)

            @block.tensor
            def _(pe):
                def load_experts(first, groups):
                    _, values = nc.values_load_multi_w_load_instructions(
                        G.tile_expert[0:1, bass.ds(first * FT, groups * FT)], engines=(mybir.EngineType.PE,),
                        min_val=0, max_val=E1 - 1, skip_runtime_bounds_check_because=
                        "stage_route1 counts experts up from 0 and takes the minimum with E1 - 1")
                    return values

                def emit_xT(n, v):
                    u = v % 2
                    pe.wait_ge(here[v], uses(n, v, 16) + 16)
                    if not isinstance(n, int) or n >= 2:
                        pe.wait_ge(xT_done, n - 1)
                    for s in range(FT):
                        mm = pe.transpose(B[u][:, s * P:(s + 1) * P], rows[v][:, s, 0:C], G.ident[:])
                    mm.then_inc(xT_psum, 1)

                def emit_gu(n, u, es):
                    pe.wait_ge(xT_done, n + 1)
                    if not isinstance(n, int) or n >= 2:
                        pe.wait_ge(h_done, n - 1)
                    for s in range(FT):
                        at = (s % 2) * 2 * H1
                        mm = pe.matmul(B[2 + 2 * u + s // 2][:, at:at + 2 * H1], xT[u][:, s * P:(s + 1) * P],
                                       w_gu[:, bass.ds(es[s] * (2 * H1), 2 * H1)], start=(s % 2 == 0), stop=True,
                                       skip_group_check=True)
                    mm.then_inc(gu_psum, 1)

                def emit_hT(n, u):
                    pe.wait_ge(h_done, n + 1)
                    if not isinstance(n, int) or n >= 1:
                        pe.wait_ge(hT_done, n)
                    for s in range(FT):
                        mm = pe.transpose(B[6][:, s * P:(s + 1) * P], h[u][:, s, :], G.ident[:])
                    mm.then_inc(hT_psum, 1)

                def emit_y(n, u, es):
                    pe.wait_ge(hT_done, n + 1)
                    if not isinstance(n, int) or n >= 1:
                        pe.wait_ge(y_done, n)
                    for s in range(FT):
                        mm = pe.matmul(B[7][:, s * C:(s + 1) * C], hT[u][:, s * P:(s + 1) * P],
                                       w_d[:, bass.ds(es[s] * C, C)], start=(s == 0), stop=True, skip_group_check=True)
                    mm.then_inc(y_psum, 1)

                def two_groups(n, v):
                    emit_xT(n + 1, v + 1)
                    es = load_experts(n - 2, 4)
                    emit_gu(n, 0, es[2 * FT:3 * FT])
                    emit_y(n - 2, 0, es[:FT])
                    emit_hT(n - 1, 1)
                    if not isinstance(n, int) or n + 2 < GROUPS:
                        emit_xT(n + 2, (v + 2) % RING)
                    emit_gu(n + 1, 1, es[3 * FT:])
                    emit_y(n - 1, 1, es[FT:2 * FT])
                    emit_hT(n, 0)
                    return es

                emit_xT(0, 0)
                es = load_experts(0, 2)
                emit_xT(1, 1)
                emit_gu(0, 0, es[:FT])
                emit_xT(2, 2)
                emit_gu(1, 1, es[FT:])
                emit_hT(0, 0)
                two_groups(2, 2)
                two_groups(4, 0)
                with pe.Fori(0, (GROUPS - 8) // RING) as i:
                    two_groups(i * RING + 6, 2)
                    two_groups(i * RING + 8, 0)
                es = two_groups(GROUPS - 2, 2)
                emit_y(GROUPS - 2, 0, es[2 * FT:3 * FT])
                emit_hT(GROUPS - 1, 1)
                emit_y(GROUPS - 1, 1, es[3 * FT:])

            @block.scalar
            def _(act):
                def copy_xT(n, u):
                    act.wait_ge(xT_psum, n + 1)
                    if not isinstance(n, int) or n >= 2:
                        act.wait_ge(gu_psum, n - 1)
                    act.activation(xT[u][:], B[u], ACT.Copy).then_inc(xT_done, 1)

                def body(n, v):
                    u = v % 2
                    if not isinstance(n, int) or n + 1 < GROUPS:
                        copy_xT(n + 1, 1 - u)
                    act.wait_ge(gu_psum, n + 1)
                    if not isinstance(n, int) or n >= 2:
                        act.wait_ge(h_done, n - 1)
                    act.activation(silu[u][:], GU(u)[:, :, 0, :], ACT.Silu).then_inc(silu_done, 1)
                copy_xT(0, 0)
                rolled(act, body, 2, 2)

            @block.vector
            def _(dve):
                def emit_hT(n, u):
                    dve.wait_ge(hT_psum, n + 1)
                    if not isinstance(n, int) or n >= 2:
                        dve.wait_ge(y_psum, n - 1)
                    dve.tensor_copy(hT[u][:], B[6]).then_inc(hT_done, 1)

                def emit_y(n, v):
                    dve.wait_ge(y_psum, n + 1)
                    if not isinstance(n, int) or n >= RING:
                        dve.wait_ge(kept[v], uses(n, v, 16 * FT))
                    dve.tensor_copy(y[v][:], B[7].rearrange("p (s c) -> p s c", c=C)).then_inc(y_done, 1)

                def take_place(n, v):
                    dve.wait_ge(here[v], uses(n, v, 16) + 16)
                    dve.tensor_copy(place[:, bass.ds(n * FT, FT)], rows[v][:, :, C]).then_inc(place_done, 1)

                def body(n, v):
                    u = v % 2
                    if not isinstance(n, int) or n + 1 < GROUPS:
                        take_place(n + 1, (v + 1) % RING)
                    if not isinstance(n, int) or n >= 2:
                        emit_y(n - 2, (v + 2) % RING)
                    dve.wait_ge(silu_done, n + 1)
                    if not isinstance(n, int) or n >= 2:
                        dve.wait_ge(hT_psum, n - 1)
                    dve.tensor_tensor(h[u][:], GU(u)[:, :, 1, :], silu[u][:], ALU.mult).then_inc(h_done, 1)
                    if not isinstance(n, int) or n >= 1:
                        emit_hT(n - 1, 1 - u)
                take_place(0, 0)
                rolled(dve, body, 6, 2)
                emit_y(GROUPS - 2, (GROUPS - 2) % RING)
                emit_hT(GROUPS - 1, 1)
                emit_y(GROUPS - 1, (GROUPS - 1) % RING)

            @block.gpsimd
            def _(pool):
                for n in range(GROUPS):
                    pool.wait_ge(y_done, n + 1)
                    for t in range(FT):
                        pool.indirect_dma_start(
                            out=G.expert_out1, out_offset=bass.IndirectOffsetOnAxis(ap=place[:, n * FT + t:n * FT + t + 1], axis=0),
                            in_=y[n % RING][:, t, :], in_offset=None, bounds_check=K1 * N - 1,
                            oob_is_err=False).then_inc(kept[n % RING], 16)
                for v in range(RING):
                    pool.wait_ge(kept[v], GROUPS // RING * FT * 16)


def stage_combine1(nc, G, I, out):
    NORMED = 3 * BATCH
    with ExitStack() as ctx:
        M = Mem(nc, ctx)
        two = range(2)
        got = [M.sb(f"f_got{u}", [P, K1, TB, C]) for u in two]
        y, x_new = M.sb("f_y", [P, TB, C]), [M.sb(f"f_new{u}", [P, TB, C]) for u in two]
        stats, mv = M.sb("f_stats", [P, TB, 6]), M.sb("f_mv", [P, TB, 2])
        var_eps, rstd = M.sb("f_var_eps", [P, TB]), M.sb("f_rstd", [P, TB])
        got_here, steps = [M.sem(f"f_got_here{u}") for u in two], M.sem("steps")
        norm_done, stored = M.sem("norm_done"), [M.sem(f"stored{u}") for u in two]
        with nc.Block() as block:
            @block.gpsimd
            def _(pool):
                for b in range(BATCH):
                    emit_norm_pool(pool, G, NORMED + b, var_eps, rstd)

            @block.vector
            def _(dve):
                order = Order(dve, steps)
                for b in range(BATCH):
                    dve.wait_ge(got_here[b % 2], (b // 2 + 1) * K1 * 16)
                    emit_combine(dve, order, b, got[b % 2], G.gate1, K1, G.acc[:, tiles(b), :], y[:])
                    if b >= 2:
                        dve.wait_ge(stored[b % 2], 16)
                    last = emit_norm_vector(dve, G, order, NORMED + b, lambda t: y[:, t, :], stats, mv, var_eps, rstd,
                                            lambda t: x_new[b % 2][:, t, :])
                    last.then_inc(norm_done, 1)

            @block.sync
            def _(sp):
                for b in two:
                    emit_combine_load(sp, b, got[b], got_here[b], G.expert_out1, K1)
                for b in range(BATCH):
                    sp.wait_ge(norm_done, b + 1)
                    sp.dma_start(out[b].rearrange("(t p) c -> p t c", p=P), x_new[b % 2][:]).then_inc(stored[b % 2], 16)
                    if b + 2 < BATCH:
                        emit_combine_load(sp, b + 2, got[b % 2], got_here[b % 2], G.expert_out1, K1)
                for u in two:
                    sp.wait_ge(stored[u], BATCH // 2 * 16)


class Shared:
    pass


def build(nc, I, out, upto=99):
    G = Shared()
    with ExitStack() as ctx:
        M = Mem(nc, ctx)
        G.psum = ctx.enter_context(nc.psum_tensor("psum", [P, 8, HALF], fp32))
        G.bank = [G.psum[:, b, :] for b in range(8)]
        G.x_wide = M.sb("x_rows", [P, TILES, WIDE])
        G.x_rows = G.x_wide[:, :, 0:C]
        G.blank = M.sb("blank", [P, WIDE])
        G.ident, G.ones, G.before = M.sb("ident", [P, P]), M.sb("ones_sb", [P, P]), M.sb("before", [P, P])
        G.place_of = M.sb("place_of", [P, K1, TILES])
        G.var_ready, G.rstd_ready = M.sem("var_ready"), M.sem("rstd_ready")
        G.cleared = M.sem("cleared")
        G.minus_half = M.sb("minus_half", [P, TILES])
        G.head_mask = M.sb("head_mask", [P, C])
        G.q_steps = nc.dram_tensor("q_steps", [STEPS, 3, GH * HD, SEQ], bf16, kind="Internal").ap()
        G.k_steps = nc.dram_tensor("k_steps", [STEPS, 3, GH * HD, SEQ], bf16, kind="Internal").ap()
        G.v_steps = nc.dram_tensor("v_steps", [STEPS, P, TB * GH * (HD + 1)], fp32, kind="Internal").ap()
        G.sorted0 = nc.dram_tensor("sorted0", [ROWS0, WIDE], fp32, kind="Internal").ap()
        G.sorted1 = nc.dram_tensor("sorted1", [ROWS1, WIDE], fp32, kind="Internal").ap()
        G.expert_out1 = nc.dram_tensor("expert_out1", [K1 * N, C], fp32, kind="Internal").ap()
        G.expert_out0 = nc.dram_tensor("expert_out0", [K0 * N, C], fp32, kind="Internal").ap()
        G.iota_e, G.iota_p = M.sb("iota_e", [P, E1]), M.sb("iota_p", [P, 2])
        G.logits0 = M.sb("logits0", [P, TILES, E0])
        stage_setup(nc, G, I)
        stage_linear_attention(nc, G, I)
        if upto < 2:
            return
        G.gate0 = M.sb("gate0", [P, TILES, K0])
        G.to_row0 = M.sb("to_row0", [P, TILES, K0], u32)
        stage_route0(nc, G, I)
        stage_experts0(nc, G, I)
        if upto < 3:
            return
        G.att_steps = M.sb("att_steps", [P, STEPS * 2, 4, GH * HD])
        stage_qkv(nc, G, I)
        stage_attention(nc, G, I)
        if upto < 4:
            return
        G.xT = M.sb("xT_all", [P, N])
        G.logits1 = M.sb("logits1", [P, TILES, E1])
        stage_projection(nc, G, I)
        G.gate1, G.to_row1 = M.sb("gate1", [P, TILES, K1]), M.sb("to_row1", [P, TILES, K1], u32)
        G.tile_expert = M.sb("tile_expert", [1, 2 * P], i32)
        G.acc = M.sb("acc", [P, TILES, C])
        G.w_gu, G.w_down = M.sb("w_gu", [P, E1 * 2 * H1]), M.sb("w_down", [P, E1 * C])
        stage_route1(nc, G, I)
        stage_experts1(nc, G, I)
        stage_combine1(nc, G, I, out)


def alibi_rows():
    bfloat = mybir.dt.np(bf16)
    dist = (SEQ - 1 - np.arange(SEQ)).astype(np.float32)
    value = -slopes()[:, None] * dist[None, :]
    parts = []
    for _ in range(3):
        parts.append(value.astype(bfloat))
        value = value - parts[-1].astype(np.float32)
    rows = np.stack(parts, 1).reshape(HEADS // GH, GH, 3, SEQ).transpose(0, 2, 1, 3).reshape(HEADS // GH, 3, GH * SEQ)
    rows = np.concatenate([rows, np.ones_like(rows)], 1)
    return np.tile(rows, (BATCH, 1, 1))


def layouts(a):
    f = {k: np.asarray(v) for k, v in a.items()}
    x = f["L0_attn_x"].reshape(N, C)
    head = np.arange(C) // HD
    gdh = np.arange(C).reshape(HEADS // GH, GH, HD).transpose(0, 2, 1).ravel()
    return {
        "x": x, "xT": x.T, "w_qkv": f["L0_attn_w_qkv"], "b_q_col": f["L0_attn_b_qkv"][:C, None],
        "b_kv": f["L0_attn_b_qkv"][None, C:], "w_proj": f["L0_attn_w_proj"], "b_proj": f["L0_attn_b_proj"][None],
        "Wr": f["L0_ffn_Wr"], "br": f["L0_ffn_br"][None],
        "W1": f["L0_ffn_W1"], "W2": f["L0_ffn_W2"].reshape(E0, H0 // P, P, C).transpose(0, 2, 1, 3),
        "b1": f["L0_ffn_b1"].reshape(E0, H0 // P, P).transpose(0, 2, 1), "b2": f["L0_ffn_b2"],
        "Wq": f["L1_attn_Wq"][:, gdh], "Wk": f["L1_attn_Wk"][:, gdh], "Wv": f["L1_attn_Wv"],
        "bq": f["L1_attn_bq"][gdh, None], "bk": f["L1_attn_bk"][gdh, None], "bv": f["L1_attn_bv"][None],
        "c_alibi": alibi_rows(),
        "Wo": f["L1_attn_Wo"], "bo": f["L1_attn_bo"][None],
        "Wr1": f["L1_ffn_router_w"].T, "br1": f["L1_ffn_router_bias"][None],
        "sg": f["L1_ffn_sgate_w"].T, "su": f["L1_ffn_sup_w"].T,
        "sd": f["L1_ffn_sdown_w"].T.reshape(HS // P, P, C).transpose(1, 0, 2),
        "gu": np.stack([f["L1_ffn_gate_w"], f["L1_ffn_up_w"]], 1).transpose(3, 0, 1, 2).reshape(C, E1 * 2 * H1),
        "down": f["L1_ffn_down_w"].transpose(2, 0, 1).reshape(H1, E1 * C),
        "c_same_expert": (np.arange(P)[:, None] % E0 == np.arange(P)[None, :] % E0).astype(np.float32),
        "c_first_of": (np.arange(P)[:, None] == np.arange(E0)[None, :]).astype(np.float32),
        "c_goes_on": (np.arange(E1 * TILES) % TILES > 0).astype(np.float32)[None],
        "c_head_mask": (head[:, None] == head[None, :]).astype(np.float32),
    }


def kernel(**inputs):
    import concourse.bacc as bacc
    from concourse.bass_utils import run_bass_kernel_spmd

    nc = bacc.Bacc("TRN2", target_bir_lowering=False, num_devices=1)
    arrays = {f"in_{k}": np.ascontiguousarray(v) for k, v in layouts(inputs).items()}
    I = {k[3:]: nc.dram_tensor(k, a.shape, mybir.dt.from_np(a.dtype), kind="ExternalInput").ap()
         for k, a in arrays.items()}
    out = nc.dram_tensor("out_x", (BATCH, SEQ, C), fp32, kind="ExternalOutput").ap()
    build(nc, I, out)
    result = run_bass_kernel_spmd(nc, [arrays], core_ids=[0])
    return result.results[0]["out_x"]
```

```python
import numpy as np
from contextlib import ExitStack

import concourse.bass as bass
from concourse import mybir

fp32 = mybir.dt.float32
bf16 = mybir.dt.bfloat16
i32 = mybir.dt.int32
u32 = mybir.dt.uint32
ALU = mybir.AluOpType
ACT = mybir.ActivationFunctionType
AX = mybir.AxisListType

P = 128
BATCH, SEQ, C = 4, 1024, 128
N = BATCH * SEQ
TILES = N // P
TB = SEQ // P
HALF = 512
HEADS, HD = 16, 8
EPS = 1e-5
STEPS_A, STEPS_QKV, STEPS_PROJECTION = 4, 5, 2

E0, H0, K0 = 8, 512, 2
CAP = int(np.ceil(1.2 * N / E0))
SLOTS0 = -(-CAP // P) * P
ROWS0 = E0 * SLOTS0

E1, H1, K1 = 32, 128, 4
TILES1 = N * K1 // P + E1
ROWS1 = TILES1 * P
CLEARS1 = 20
HS = H1 * K1
WIDE = C + 1
OUT_OF_RANGE = 1.0e6

GH = 4
STEPS = BATCH * HEADS // GH
PROD = 3 * 3 * HD
ALIBI_AT, MAX_AT = PROD, PROD + 3
ROWS_MAX, ROWS_ALL = PROD + 3, PROD + 6
MASKED = -1.0e30


def slopes():
    start = 2.0 ** (-2.0 ** (-(np.log2(HEADS) - 3)))
    return np.array([start * start ** i for i in range(HEADS)], np.float32)


class Order:

    def __init__(self, engine, sem, base=0):
        self.engine, self.sem, self.base, self.count = engine, sem, base, 0

    def done(self, instruction):
        self.count += 1
        instruction.then_inc(self.sem, 1)
        self.engine.wait_ge(self.sem, self.base + self.count)


def repeat(engine, times):
    def run(body):
        body(0)
        with engine.Fori(1, times) as i:
            body(i)
    return run


def one_ahead(engine, ahead, rest):
    ahead(0)
    rest(0, True)
    with engine.Fori(1, BATCH - 1) as i:
        rest(i, True)
    rest(BATCH - 1, False)


def wait_past(engine, sem, count):
    if not isinstance(count, int) or count > 0:
        engine.wait_ge(sem, count)


class Mem:

    def __init__(self, nc, ctx):
        self.nc, self.ctx = nc, ctx

    def sb(self, name, shape, dt=fp32):
        return self.ctx.enter_context(self.nc.sbuf_tensor(name, shape, dt))

    def sem(self, name):
        return self.ctx.enter_context(self.nc.semaphore(name))


def tiles(i, n=TB):
    return bass.ds(i * n, n)


def stage_setup(nc, G, I):
    with ExitStack() as ctx:
        M = Mem(nc, ctx)
        filled, shaped = M.sem("filled"), M.sem("shaped")
        with nc.Block() as block:
            @block.gpsimd
            def _(pool):
                pool.memset(G.ident[:], 0.0).then_inc(filled, 1)
                pool.memset(G.ones[:], 1.0).then_inc(filled, 1)
                pool.memset(G.ones_b[:], 1.0).then_inc(filled, 1)
                pool.memset(G.before_b[:], 1.0).then_inc(filled, 1)
                pool.memset(G.minus_half[:], -0.5).then_inc(filled, 1)
                pool.memset(G.blank[:, 0:C], 0.0).then_inc(filled, 1)
                pool.memset(G.blank[:, C:WIDE], OUT_OF_RANGE).then_inc(filled, 1)
                for place_of, K in ((G.place_of0, K0), (G.place_of1, K1)):
                    pool.iota(place_of[:], pattern=[[1, K], [P * K, TILES]], base=0, channel_multiplier=K,
                              allow_small_or_imprecise_dtypes=True).then_inc(filled, 1)
                pool.iota(G.iota_e[:], pattern=[[1, E1]], base=0, channel_multiplier=0,
                          allow_small_or_imprecise_dtypes=True).then_inc(filled, 1)
                pool.iota(G.iota_eb[:], pattern=[[1, E1]], base=0, channel_multiplier=0,
                          allow_small_or_imprecise_dtypes=True).then_inc(filled, 1)
                pool.iota(G.iota_p[:], pattern=[[P, 2]], base=0, channel_multiplier=1,
                          allow_small_or_imprecise_dtypes=True).then_inc(filled, 1)
                pool.wait_ge(filled, 12)
                pool.affine_select(out=G.ident[:], in_=G.ident[:], compare_op=ALU.not_equal, fill=1.0,
                                   base=0, pattern=[[-1, P]], channel_multiplier=1).then_inc(shaped, 1)
                pool.affine_select(out=G.before_b[:], in_=G.before_b[:], compare_op=ALU.is_gt, fill=0.0,
                                   base=0, pattern=[[1, P]], channel_multiplier=-1).then_inc(shaped, 1)
                pool.wait_ge(shaped, 2)


def emit_clear(engine, dst, value, cleared):
    rows, width = dst.shape
    each = rows // P
    return engine.dma_start(dst.rearrange("(p s) c -> p s c", s=each),
                            value[:, None, :].to_broadcast([P, each, width])).then_inc(cleared, 16)


def emit_norm_vector(dve, G, order, i, y, stats, mv, var_eps, rstd, out_tile):
    emit_norm_moments(dve, G, order, y, stats, mv, var_eps)
    return emit_norm_scale(dve, G, i, y, mv, rstd, out_tile)


def emit_norm_moments(dve, G, order, y, stats, mv, var_eps):
    for t in range(TB - 1):
        dve.bn_stats(stats[:, t, :], y(t))
    order.done(dve.bn_stats(stats[:, TB - 1, :], y(TB - 1)))
    dve.memset(var_eps[:, 0:1], 0.0)
    for t in range(TB - 1):
        dve.bn_aggr(mv[:, t, :], stats[:, t, :])
    order.done(dve.bn_aggr(mv[:, TB - 1, :], stats[:, TB - 1, :]))
    dve.tensor_scalar(var_eps[:], mv[:, :, 1], EPS, None, ALU.add).then_inc(G.var_ready, 1)


def emit_norm_scale(dve, G, i, y, mv, rstd, out_tile):
    dve.wait_ge(G.rstd_ready, i + 1)
    last = None
    for t in range(TB):
        last = dve.tensor_scalar(out_tile(t), y(t), mv[:, t, 0:1], rstd[:, t:t + 1],
                                 ALU.subtract, ALU.mult)
    return last


def emit_norm_pool(pool, G, i, var_eps, rstd):
    pool.wait_ge(G.var_ready, i + 1)
    pool.tensor_tensor(rstd[:], var_eps[:], G.minus_half[:, 0:TB], ALU.pow).then_inc(G.rstd_ready, 1)


def emit_scatter(pool, G, place_of, to_row, choices, sorted_rows, last_row, scattered, before, rows_ready=None):
    for k in range(choices):
        if rows_ready is not None:
            pool.wait_ge(rows_ready, k + 1)
        if k:
            pool.wait_ge(scattered, k * TILES * 16)
        pool.tensor_copy(G.x_wide[:, :, C], place_of[:, k, :]).then_inc(G.placed, 1)
        pool.wait_ge(G.placed, before + k + 1)
        for t in range(TILES):
            pool.indirect_dma_start(
                out=sorted_rows, out_offset=bass.IndirectOffsetOnAxis(ap=to_row[:, t, k:k + 1], axis=0),
                in_=G.x_wide[:, t, :], in_offset=None, bounds_check=last_row,
                oob_is_err=False).then_inc(scattered, 16)
    pool.wait_ge(scattered, choices * TILES * 16)


def stage_linear_attention(nc, G, I):
    NORMED = 0
    KV = 2 * C
    OUT = C + HEADS
    PER_BANK = HALF // OUT
    with ExitStack() as ctx:
        M = Mem(nc, ctx)
        w_qkv, w_proj = M.sb("wqkv_sb", [P, 3 * C]), M.sb("wproj_sb", [P, C])
        bq, bkv, bproj = M.sb("bq_sb", [P, 1]), M.sb("bkv_sb", [P, KV]), M.sb("bproj_sb", [P, C])
        w_r, b_r = M.sb("wr_sb", [P, E0]), M.sb("br_sb", [P, E0])
        head_mask = M.sb("head_mask", [P, OUT])
        xT = M.sb("xT_in", [P, SEQ])
        kv = M.sb("kv_rows", [P, TB, KV + 1])
        k_exp, k_relu = M.sb("k_exp", [P, TB, C]), M.sb("k_relu", [P, TB, C])
        qT, q_exp = M.sb("qT", [P, SEQ]), M.sb("q_exp", [P, SEQ])
        kv_heads = M.sb("kv_heads", [P, OUT])
        den, att, attT = M.sb("den", [P, TB, HEADS]), M.sb("att", [P, TB, C]), M.sb("attT", [P, SEQ])
        x_bias = M.sb("x_bias", [P, TB, C])
        y, x_new = M.sb("y_rows", [P, TB, C]), M.sb("x_new", [P, TB, C])
        xT_new = M.sb("xT_new", [P, SEQ])
        stats, mv = M.sb("stats", [P, TB, 6]), M.sb("mv", [P, TB, 2])
        var_eps, rstd = M.sb("var_eps", [P, TB]), M.sb("rstd", [P, TB])
        weights, xT_here = M.sem("weights"), M.sem("xT_here")
        x_here = M.sem("x_here")
        q_done, kv_done = M.sem("q_done"), M.sem("kv_done")
        kv_taken, q_relu = M.sem("kv_taken"), M.sem("q_relu")
        qexp_done, kexp_done, qT_done, k_done = M.sem("qexp_done"), M.sem("kexp_done"), M.sem("qT_done"), M.sem("k_done")
        sums_done, heads_done, out_done = M.sem("sums_done"), M.sem("heads_done"), M.sem("out_done")
        att_done, attT_psum, attT_done = M.sem("att_done"), M.sem("attT_psum"), M.sem("attT_done")
        y_done, y_taken = M.sem("y_done"), M.sem("y_taken")
        xb_done = M.sem("xb_done")
        norm_done, xT_psum, xT_copied = M.sem("norm_done"), M.sem("xT_psum"), M.sem("xT_copied")
        logits_psum, logits_done, x_kept = M.sem("logits_psum"), M.sem("logits_done"), M.sem("x_kept")
        front_steps, ones_set = M.sem("front_steps"), M.sem("ones_set")
        B = G.bank
        TURNED = (3, 0)

        def rounds(engine, first, back, last):
            first(0)
            back(0, False, True)
            with engine.Fori(1, BATCH - 1) as i:
                back(i, True, True)
            back(BATCH - 1, True, False)
            last(BATCH - 1)

        with nc.Block() as block:
            @block.sync
            def _(sp):
                sp.dma_start(w_qkv[:], I["w_qkv"]).then_inc(weights, 16)
                sp.dma_start(xT[:], I["xT"][:, 0:SEQ]).then_inc(xT_here, 16)
                sp.dma_start(bq[:], I["b_q_col"]).then_inc(weights, 16)
                sp.dma_start(bkv[:], I["b_kv"].to_broadcast([P, KV])).then_inc(weights, 16)
                sp.dma_start(head_mask[:], I["c_head_mask"]).then_inc(weights, 16)
                sp.dma_start(w_proj[:], I["w_proj"]).then_inc(weights, 16)
                sp.dma_start(bproj[:], I["b_proj"].to_broadcast([P, C])).then_inc(weights, 16)
                sp.dma_start(w_r[:], I["Wr"]).then_inc(weights, 16)
                sp.dma_start(b_r[:], I["br"].to_broadcast([P, E0])).then_inc(weights, 16)
                for b in range(BATCH):
                    sp.dma_start(G.x_rows[:, b * TB:(b + 1) * TB, :],
                                 I["x"][b * SEQ:(b + 1) * SEQ, :].rearrange("(t p) c -> p t c", p=P)).then_inc(x_here, 16)

                def load_xT(i):
                    sp.wait_ge(kv_done, i * 4)
                    sp.dma_start(xT[:], I["xT"][:, bass.ds(i * SEQ, SEQ)]).then_inc(xT_here, 16)

                def keep(i):
                    sp.wait_ge(norm_done, i + 1)
                    sp.dma_start(G.x_rows[:, tiles(i), :], x_new[:]).then_inc(x_kept, 16)
                load_xT(1)
                with sp.Fori(0, BATCH - 2) as i:
                    load_xT(i + 2)
                    keep(i)
                for i in (BATCH - 2, BATCH - 1):
                    keep(i)
                sp.wait_ge(x_kept, BATCH * 16)

            @block.tensor
            def _(pe):
                pe.wait_ge(weights, 8 * 16)

                def front(i):
                    pe.wait_ge(xT_here, i * 16 + 16)
                    for c in range(2):
                        wait_past(pe, qexp_done, i * 2)
                        wait_past(pe, q_relu, i * 2)
                        pe.matmul(B[4 + c][:], w_qkv[:, 0:C], xT[:, c * HALF:(c + 1) * HALF],
                                  start=True, stop=True).then_inc(q_done, 1)
                    for t in range(TB):
                        if t % 2 == 0:
                            b = t // 2
                            if b < 2:
                                wait_past(pe, kv_taken, i * 4)
                                wait_past(pe, heads_done, i * 2)
                            else:
                                pe.wait_ge(kv_taken, i * 4 + b - 1)
                        mm = pe.matmul(B[6 + b % 2][:, (t % 2) * KV:(t % 2 + 1) * KV], xT[:, t * P:(t + 1) * P],
                                       w_qkv[:, C:3 * C], start=(t % 2 == 0), stop=True, skip_group_check=True)
                        if t % 2:
                            mm.then_inc(kv_done, 1)

                def sums(i):
                    pe.wait_ge(k_done, i + 1)
                    for t in range(TB):
                        mm = pe.matmul(B[6][:, 0:C + 1], kv[:, t, 0:C], kv[:, t, C:KV + 1],
                                       start=(t == 0), stop=(t == TB - 1))
                    mm.then_inc(sums_done, 1)

                def turn(rows, psum_done):
                    for t in range(TB):
                        mm = pe.transpose(B[TURNED[t // 4]][:, (t % 4) * P:(t % 4 + 1) * P], rows[:, t, :], G.ident[:])
                        if t % 4 == 3:
                            mm.then_inc(psum_done, 1)

                def logits(i):
                    for t in range(TB):
                        if t % 4 == 0:
                            pe.wait_ge(xT_copied, i * 2 + t // 4 + 1)
                        mm = pe.matmul(B[7][:, t * E0:(t + 1) * E0], xT_new[:, t * P:(t + 1) * P], w_r[:],
                                       start=(t == 0), stop=True, skip_group_check=True)
                    mm.then_inc(logits_psum, 1)

                def back(i, before, more):
                    pe.wait_ge(heads_done, i * 2 + 2)
                    pe.wait_ge(qT_done, i * 2 + 2)
                    for t in range(TB):
                        at = (t % PER_BANK) * OUT
                        mm = pe.matmul(B[t // PER_BANK][:, at:at + OUT], qT[:, t * P:(t + 1) * P], kv_heads[:],
                                       start=(at == 0), stop=True, skip_group_check=True)
                    mm.then_inc(out_done, 1)
                    if more:
                        front(i + 1)
                    pe.wait_ge(att_done, i + 1)
                    turn(att, attT_psum)
                    for t in range(TB):
                        if t % 4 == 0:
                            pe.wait_ge(attT_done, i * 2 + t // 4 + 1)
                        mm = pe.matmul(B[1 + t // 4][:, (t % 4) * C:(t % 4 + 1) * C], attT[:, t * P:(t + 1) * P],
                                       w_proj[:], start=(t % 4 == 0), stop=True, skip_group_check=True)
                        if t % 4 == 3:
                            mm.then_inc(y_done, 1)
                    if before:
                        pe.wait_ge(norm_done, i)
                        turn(x_new, xT_psum)
                    if more:
                        if before:
                            pe.wait_ge(kv_taken, i * 4 + 8)
                            logits(i - 1)
                        sums(i + 1)
                    else:
                        logits(i - 1)

                def first(i):
                    front(i)
                    sums(i)

                def last(i):
                    pe.wait_ge(norm_done, i + 1)
                    pe.wait_ge(logits_done, i)
                    turn(x_new, xT_psum)
                    logits(i)
                rounds(pe, first, back, last)

            @block.scalar
            def _(act):
                act.wait_ge(weights, 8 * 16)

                def front(i):
                    for c in range(2):
                        act.wait_ge(q_relu, i * 2 + c + 1)
                        wait_past(act, qT_done, i * 2)
                        act.activation(q_exp[:, c * HALF:(c + 1) * HALF], B[4 + c][:], ACT.Exp,
                                       bias=bq[:]).then_inc(qexp_done, 1)
                    act.wait_ge(kv_taken, i * 4 + 4)
                    wait_past(act, k_done, i)
                    act.activation(k_exp[:], kv[:, :, 0:C], ACT.Exp).then_inc(kexp_done, 1)

                def back(i, before, more):
                    if more:
                        front(i + 1)
                    for c in range(2):
                        act.wait_ge(attT_psum, i * 2 + c + 1)
                        wait_past(act, y_done, i * 2)
                        act.activation(attT[:, c * HALF:(c + 1) * HALF], B[TURNED[c]][:], ACT.Copy).then_inc(attT_done, 1)
                    if before:
                        last(i - 1)

                def last(i):
                    for c in range(2):
                        act.wait_ge(xT_psum, i * 2 + c + 1)
                        act.activation(xT_new[:, c * HALF:(c + 1) * HALF], B[TURNED[c]][:], ACT.Copy).then_inc(xT_copied, 1)
                rounds(act, front, back, last)

            @block.gpsimd
            def _(pool):
                pool.memset(kv[:, :, KV:KV + 1], 1.0).then_inc(ones_set, 1)
                pool.wait_ge(weights, 8 * 16)
                pool.wait_ge(x_here, BATCH * 16)

                @repeat(pool, BATCH)
                def _(i):
                    wait_past(pool, y_taken, i * 2)
                    pool.tensor_tensor(x_bias[:], G.x_rows[:, tiles(i), :],
                                       bproj[:, None, :].to_broadcast([P, TB, C]), ALU.add).then_inc(xb_done, 1)
                    emit_norm_pool(pool, G, NORMED + i, var_eps, rstd)

            @block.vector
            def _(dve):
                dve.wait_ge(weights, 8 * 16)
                dve.wait_ge(ones_set, 1)

                def front(i):
                    order = Order(dve, front_steps, i)
                    for c in range(2):
                        dve.wait_ge(q_done, i * 2 + c + 1)
                        dve.tensor_scalar(qT[:, c * HALF:(c + 1) * HALF], B[4 + c][:], bq[:], 0.0,
                                          ALU.add, ALU.max).then_inc(q_relu, 1)
                    for b in range(4):
                        dve.wait_ge(kv_done, i * 4 + b + 1)
                        dve.tensor_tensor(kv[:, 2 * b:2 * b + 2, 0:KV],
                                          B[6 + b % 2][:].rearrange("p (t n) -> p t n", t=2),
                                          bkv[:, None, :].to_broadcast([P, 2, KV]), ALU.add).then_inc(kv_taken, 1)
                    dve.wait_ge(kv_taken, i * 4 + 4)
                    order.done(dve.tensor_scalar(k_relu[:], kv[:, :, 0:C], 0.0, None, ALU.max))
                    for c in range(2):
                        dve.wait_ge(qexp_done, i * 2 + c + 1)
                        dve.wait_ge(q_relu, i * 2 + c + 1)
                        s = slice(c * HALF, (c + 1) * HALF)
                        dve.scalar_tensor_tensor(out=qT[:, s], in0=q_exp[:, s], scalar=1.0, in1=qT[:, s],
                                                 op0=ALU.min, op1=ALU.add).then_inc(qT_done, 1)
                    dve.wait_ge(kexp_done, i + 1)
                    dve.scalar_tensor_tensor(out=kv[:, :, 0:C], in0=k_exp[:], scalar=1.0, in1=k_relu[:],
                                             op0=ALU.min, op1=ALU.add).then_inc(k_done, 1)
                    assert order.count == 1

                def heads(i):
                    dve.wait_ge(sums_done, i + 1)
                    dve.tensor_tensor(kv_heads[:, 0:C], B[6][:, 0:C], head_mask[:, 0:C], ALU.mult).then_inc(heads_done, 1)
                    dve.tensor_scalar(kv_heads[:, C:OUT], head_mask[:, C:OUT], B[6][:, C:C + 1], None,
                                      ALU.mult).then_inc(heads_done, 1)

                def last(i):
                    dve.wait_ge(logits_psum, i + 1)
                    dve.tensor_tensor(G.logits0[:, tiles(i), :],
                                      B[7][:, 0:TB * E0].rearrange("p (t e) -> p t e", e=E0),
                                      b_r[:, None, :].to_broadcast([P, TB, E0]), ALU.add).then_inc(logits_done, 1)

                def back(i, before, more):
                    order = Order(dve, G.steps, i * STEPS_A)
                    dve.wait_ge(out_done, i + 1)
                    outs = [(b, b * PER_BANK, min(PER_BANK, TB - b * PER_BANK)) for b in range(3)]
                    view = lambda b, n: B[b][:, 0:n * OUT].rearrange("p (t o) -> p t o", o=OUT)
                    for b, t, n in outs:
                        done = dve.tensor_scalar(den[:, t:t + n, :], view(b, n)[:, :, C:OUT], 1e-8, None, ALU.add)
                    order.done(done)
                    order.done(dve.reciprocal(den[:], den[:]))
                    wait_past(dve, attT_psum, i * 2)
                    for b, t, n in outs:
                        done = dve.tensor_tensor(att[:, t:t + n, :].rearrange("p t (h e) -> p t h e", h=HEADS),
                                                 view(b, n)[:, :, 0:C].rearrange("p t (h e) -> p t h e", h=HEADS),
                                                 den[:, t:t + n, :, None].to_broadcast([P, n, HEADS, HD]), ALU.mult)
                    done.then_inc(att_done, 1)
                    if more:
                        front(i + 1)
                    dve.wait_ge(xb_done, i + 1)
                    for c in range(2):
                        dve.wait_ge(y_done, i * 2 + c + 1)
                        dve.tensor_tensor(y[:, 4 * c:4 * c + 4, :], B[1 + c][:].rearrange("p (t n) -> p t n", t=4),
                                          x_bias[:, 4 * c:4 * c + 4, :], ALU.add).then_inc(y_taken, 1)
                    dve.wait_ge(y_taken, i * 2 + 2)
                    wait_past(dve, x_kept, i * 16)
                    wait_past(dve, xT_psum, i * 2)
                    emit_norm_moments(dve, G, order, lambda t: y[:, t, :], stats, mv, var_eps)
                    if before:
                        last(i - 1)
                    if more:
                        heads(i + 1)
                    emit_norm_scale(dve, G, NORMED + i, lambda t: y[:, t, :], mv, rstd,
                                    lambda t: x_new[:, t, :]).then_inc(norm_done, 1)
                    assert order.count == STEPS_A

                def first(i):
                    front(i)
                    heads(i)
                rounds(dve, first, back, last)



class Router:

    def __init__(self, M, G, experts, chosen, name):
        self.E, self.K, self.G = experts, chosen, G
        self.cols = TILES * experts
        self.prob = M.sb(name + "_prob", [P, TILES, experts])
        self.top = M.sb(name + "_top", [P, TILES, 8])
        self.top_at = M.sb(name + "_top_at", [P, TILES, 8], u32)
        self.top_at_f = M.sb(name + "_top_at_f", [P, TILES, chosen], bf16)
        self.total = M.sb(name + "_total", [P, TILES])
        self.onehot = M.sb(name + "_onehot", [P, chosen, TILES, experts], bf16)
        self.member = M.sb(name + "_member", [P, TILES, experts], bf16)
        self.mask = M.sb(name + "_mask", [P, TILES, experts], bf16)
        self.position = M.sb(name + "_position", [P, TILES, experts])
        self.by_expert = M.sb(name + "_by_expert", [P, experts, TILES])
        self.scanned = M.sb(name + "_scanned", [P, experts, TILES])
        self.goes_on = M.sb(name + "_goes_on", [P, experts, TILES])
        self.picked = M.sb(name + "_picked", [P, TILES, experts])
        self.row = M.sb(name + "_row", [P, TILES])
        self.vec, self.exp_in, self.exp_out = M.sem(name + "_vec"), M.sem(name + "_exp_in"), M.sem(name + "_exp_out")
        self.to_count, self.counted = M.sem(name + "_to_count"), M.sem(name + "_counted")

    def across(self, per_tile):
        return per_tile[:, :, None].to_broadcast([P, TILES, self.E])


def emit_softmax_topk(dve, order, R, logits):
    order.done(dve.tensor_reduce(R.total[:], logits[:], AX.X, ALU.max))
    dve.tensor_tensor(R.prob[:], logits[:], R.across(R.total), ALU.subtract).then_inc(R.exp_in, 1)
    dve.wait_ge(R.exp_out, 1)
    order.done(dve.tensor_reduce(R.total[:], R.prob[:], AX.X, ALU.add))
    order.done(dve.reciprocal(R.total[:], R.total[:]))
    order.done(dve.tensor_tensor(R.prob[:], R.prob[:], R.across(R.total), ALU.mult))
    for t in range(TILES - 1):
        dve.max(R.top[:, t, :], R.prob[:, t, :])
    order.done(dve.max(R.top[:, TILES - 1, :], R.prob[:, TILES - 1, :]))
    for t in range(TILES - 1):
        dve.max_index(R.top_at[:, t, :], R.top[:, t, :], R.prob[:, t, :])
    order.done(dve.max_index(R.top_at[:, TILES - 1, :], R.top[:, TILES - 1, :], R.prob[:, TILES - 1, :]))
    order.done(dve.tensor_copy(R.top_at_f[:], R.top_at[:, :, 0:R.K]))
    for k in range(R.K):
        last = dve.tensor_tensor(R.onehot[:, k], R.G.iota_eb[:, None, 0:R.E].to_broadcast([P, TILES, R.E]),
                                 R.across(R.top_at_f[:, :, k]), ALU.is_equal)
    order.done(last)
    for k in range(1, R.K):
        order.done(dve.tensor_tensor(R.mask[:] if k == R.K - 1 else R.member[:],
                                     R.onehot[:, 0] if k == 1 else R.member[:], R.onehot[:, k], ALU.add))


def emit_exp(act, R):
    act.wait_ge(R.exp_in, 1)
    act.activation(R.prob[:], R.prob[:], ACT.Exp).then_inc(R.exp_out, 1)


def emit_count_tensor(pe, R, n, mask, before_bank, total_bank):
    pe.wait_ge(R.to_count, n)
    flat = mask[:].rearrange("p t e -> p (t e)")
    for banks, lhsT in ((before_bank, R.G.before_b), (total_bank, R.G.ones_b)):
        for c in range(-(-R.cols // HALF)):
            w = min(HALF, R.cols - c * HALF)
            mm = pe.matmul(banks[c][:, 0:w], lhsT[:], flat[:, c * HALF:c * HALF + w], start=True, stop=True)
    mm.then_inc(R.counted, 1)


def emit_positions(dve, order, R, n, before_bank, total_bank):
    dve.wait_ge(R.counted, n)
    per = HALF // R.E
    for c in range(-(-R.cols // HALF)):
        w = min(per, TILES - c * per)
        last = dve.tensor_copy(R.by_expert[:, :, c * per:c * per + w],
                               total_bank[c][:, 0:w * R.E].rearrange("p (t e) -> p e t", e=R.E))
    order.done(last)
    flat = lambda x: x[:].rearrange("p e t -> p (e t)")
    order.done(dve.tensor_tensor_scan(flat(R.scanned), flat(R.goes_on), flat(R.by_expert), 0.0, ALU.mult, ALU.add))
    order.done(dve.tensor_tensor(R.by_expert[:], R.scanned[:], R.by_expert[:], ALU.subtract))
    for c in range(-(-R.cols // HALF)):
        w = min(per, TILES - c * per)
        last = dve.tensor_tensor(R.position[:, c * per:c * per + w, :],
                                 before_bank[c][:, 0:w * R.E].rearrange("p (t e) -> p t e", e=R.E),
                                 R.by_expert[:, :, c * per:c * per + w].rearrange("p e t -> p t e"), ALU.add)
    order.done(last)


def emit_pick(dve, order, R, k, values, out):
    order.done(dve.tensor_tensor(R.picked[:], R.onehot[:, k], values[:], ALU.mult))
    order.done(dve.tensor_reduce(out, R.picked[:], AX.X, ALU.add))


def stage_route0(nc, G, I):
    BITS = 30
    with ExitStack() as ctx:
        M = Mem(nc, ctx)
        R = Router(M, G, E0, K0, "r0")
        gate = M.sb("gate_of", [P, TILES, E0])
        gateT = M.sb("gateT", [P, 2 * P])
        compared = M.sb("compared", [P, 3, 2 * P])
        same_expert = M.sb("same_expert", [P, P])
        first_of = M.sb("first_of", [P, E0])
        count, tried, spread = M.sb("count", [P, 3]), M.sb("tried", [P, 3]), M.sb("spread", [P, E0])
        found, reached = M.sb("found", [P, 1]), M.sb("reached", [P, 4])
        bits = M.sb("bits", [P, 3], u32)
        above, equal, taken = [M.sb(name, [P, TILES, E0], bf16) for name in ("above", "equal", "taken")]
        limit, room = M.sb("limit", [P, E0]), M.sb("room", [P, E0])
        loaded, gateT_psum, cnt_in, cnt_out = M.sem("loaded"), M.sem("gateT_psum"), M.sem("cnt_in"), M.sem("cnt_out")
        gate_done, found_done, limit_psum, vec_loop = M.sem("gate_done"), M.sem("found_done"), M.sem("limit_psum"), M.sem("vec_loop")
        above_done, above_psum = M.sem("above_done"), M.sem("above_psum")
        B = G.bank
        over = lambda v: v[:, None, :].to_broadcast([P, TILES, E0])
        with nc.Block() as block:
            @block.sync
            def _(sp):
                sp.dma_start(same_expert[:], I["c_same_expert"]).then_inc(loaded, 16)
                sp.dma_start(first_of[:], I["c_first_of"]).then_inc(loaded, 16)
                sp.dma_start(R.goes_on[:].rearrange("p e t -> p (e t)"),
                             I["c_goes_on"][:, 0:E0 * TILES].to_broadcast([P, E0 * TILES])).then_inc(loaded, 16)

            @block.gpsimd
            def _(pool):
                emit_clear(pool, G.sorted0, G.blank[:], G.cleared)
                emit_clear(pool, G.expert_out0, G.blank[:, 0:C], G.cleared)

            @block.scalar
            def _(act):
                emit_exp(act, R)

            @block.tensor
            def _(pe):
                pe.wait_ge(loaded, 48)
                pe.wait_ge(gate_done, 1)
                flat = gate[:].rearrange("p t e -> p (t e)")
                for c in range(2):
                    mm = pe.transpose(B[0][:, c * P:(c + 1) * P], flat[:, c * P:(c + 1) * P], G.ident[:])
                mm.then_inc(gateT_psum, 1)
                with pe.Fori(0, BITS // 2) as i:
                    pe.wait_ge(cnt_in, i + 1)
                    pe.matmul(B[1][:, 0:3], same_expert[:], count[:], start=True, stop=True).then_inc(cnt_out, 1)
                pe.wait_ge(found_done, 1)
                pe.matmul(B[1][:, 0:E0], G.ones[:], spread[:], start=True, stop=True).then_inc(limit_psum, 1)
                emit_count_tensor(pe, R, 1, equal, [B[2]], [B[3]])
                pe.matmul(B[4][:, 0:R.cols], G.ones_b[:], above[:].rearrange("p t e -> p (t e)"),
                          start=True, stop=True).then_inc(above_psum, 1)
                emit_count_tensor(pe, R, 2, taken, [B[5]], [B[6]])

            @block.vector
            def _(dve):
                order = Order(dve, R.vec)
                emit_softmax_topk(dve, order, R, G.logits0)
                order.done(dve.tensor_tensor(gate[:], R.prob[:], R.mask[:], ALU.mult))
                order.done(dve.tensor_tensor(gate[:], gate[:], R.mask[:], ALU.add))
                dve.tensor_scalar(gate[:], gate[:], 1.0, None, ALU.subtract).then_inc(gate_done, 1)
                dve.memset(reached[:], 0.0)
                for j in range(3):
                    dve.memset(bits[:, j:j + 1], (j + 1) << (BITS - 2))
                    last = dve.memset(tried[:, j:j + 1].bitcast(u32), (j + 1) << (BITS - 2))
                order.done(last)
                dve.wait_ge(loaded, 48)
                dve.wait_ge(gateT_psum, 1)
                order.done(dve.tensor_copy(gateT[:], B[0][:, 0:2 * P]))
                with dve.Fori(0, BITS // 2) as i:
                    inner = Order(dve, vec_loop, i * 4)
                    for j in range(3):
                        last = dve.tensor_scalar(compared[:, j], gateT[:], tried[:, j:j + 1], None, ALU.is_ge, ALU.add,
                                                 accum_out=count[:, j:j + 1])
                    last.then_inc(cnt_in, 1)
                    inner.done(dve.tensor_scalar(bits[:], bits[:], 2, None, ALU.logical_shift_right))
                    dve.wait_ge(cnt_out, i + 1)
                    inner.done(dve.scalar_tensor_tensor(out=reached[:, 1:4], in0=B[1][:, 0:3], scalar=float(CAP),
                                                        in1=tried[:], op0=ALU.is_ge, op1=ALU.mult))
                    inner.done(dve.tensor_reduce(found[:], reached[:], AX.X, ALU.max))
                    dve.tensor_copy(reached[:, 0:1], found[:])
                    inner.done(dve.tensor_tensor(tried[:].bitcast(u32), found[:].bitcast(u32).to_broadcast([P, 3]), bits[:],
                                                 ALU.bitwise_or))
                    assert inner.count == 4
                dve.tensor_scalar(spread[:], first_of[:], found[:], None, ALU.mult).then_inc(found_done, 1)
                dve.wait_ge(limit_psum, 1)
                order.done(dve.tensor_copy(limit[:], B[1][:, 0:E0]))
                dve.tensor_tensor(above[:], gate[:], over(limit), ALU.is_gt).then_inc(above_done, 1)
                dve.tensor_tensor(equal[:], gate[:], over(limit), ALU.is_equal).then_inc(R.to_count, 1)
                emit_positions(dve, order, R, 1, [B[2]], [B[3]])
                dve.wait_ge(above_psum, 1)
                order.done(dve.tensor_reduce(room[:], B[4][:, 0:R.cols].rearrange("p (t e) -> p e t", e=E0), AX.X, ALU.add))
                order.done(dve.tensor_scalar(room[:], room[:], -1.0, float(CAP), ALU.mult, ALU.add))
                order.done(dve.tensor_tensor(taken[:], R.position[:], over(room), ALU.is_lt))
                order.done(dve.tensor_tensor(taken[:], taken[:], equal[:], ALU.mult))
                dve.tensor_tensor(taken[:], taken[:], above[:], ALU.add).then_inc(R.to_count, 1)
                emit_positions(dve, order, R, 2, [B[5]], [B[6]])
                order.done(dve.tensor_scalar(limit[:], G.iota_e[:, 0:E0], float(SLOTS0), OUT_OF_RANGE, ALU.mult, ALU.add))
                order.done(dve.tensor_tensor(R.position[:], R.position[:], over(limit), ALU.add))
                order.done(dve.scalar_tensor_tensor(out=R.position[:], in0=taken[:], scalar=-OUT_OF_RANGE,
                                                    in1=R.position[:], op0=ALU.mult, op1=ALU.add))
                for k in range(K0):
                    emit_pick(dve, order, R, k, taken, R.row[:])
                    order.done(dve.tensor_tensor(G.gate0[:, :, k], R.row[:], R.top[:, :, k], ALU.mult))
                    emit_pick(dve, order, R, k, R.position, R.row[:])
                    order.done(dve.tensor_copy(G.to_row0[:, :, k], R.row[:]))


def stage_experts0(nc, G, I):
    HC = H0 // P
    ST = SLOTS0 // P
    FIRST = min(SLOTS0, HALF)
    PARTS = ((0, FIRST), (FIRST, SLOTS0))
    with ExitStack() as ctx:
        M = Mem(nc, ctx)
        two = range(2)
        w1 = [M.sb(f"w1_{u}", [P, H0]) for u in two]
        w2 = [M.sb(f"w2_{u}", [P, HC, C]) for u in two]
        b1 = [M.sb(f"b1_{u}", [P, HC]) for u in two]
        b2 = [M.sb(f"b2_{u}", [P, C]) for u in two]
        rows = [M.sb(f"rows_{u}", [P, ST, WIDE]) for u in two]
        place = [M.sb(f"place_{u}", [P, ST], u32) for u in two]
        place_done = M.sem("place_done")
        xT = [M.sb(f"exT_{u}", [P, SLOTS0]) for u in two]
        hT = M.sb("hT", [P, HC, SLOTS0])
        y = [M.sb(f"ey_{u}", [P, ST, C]) for u in two]
        scattered, w_here = M.sem("scattered"), [M.sem(f"w_here{u}") for u in two]
        rows_here, y_kept = [M.sem(f"rows_here{u}") for u in two], [M.sem(f"y_kept{u}") for u in two]
        xT_psum, xT_done, h_psum, h_done = M.sem("xT_psum"), M.sem("xT_done"), M.sem("h_psum"), M.sem("h_done")
        y_psum, y_done = M.sem("y_psum"), M.sem("y_done")
        B = G.bank

        def pairs(engine, expert):
            for e in range(2):
                expert(e, e, 0, True)
            with engine.Fori(1, E0 // 2 - 1) as i:
                for u in two:
                    expert(i * 2 + u, u, i, True)
            for e in range(E0 - 2, E0):
                expert(e, e % 2, e // 2, e + 1 < E0)

        with nc.Block() as block:
            @block.gpsimd
            def _(pool):
                pool.wait_ge(G.cleared, 2 * 16)
                emit_scatter(pool, G, G.place_of0, G.to_row0, K0, G.sorted0, ROWS0 - 1, scattered, 0)
                for e in range(E0):
                    pool.wait_ge(y_done, e + 1)
                    for t in range(ST):
                        pool.indirect_dma_start(
                            out=G.expert_out0, out_offset=bass.IndirectOffsetOnAxis(ap=place[e % 2][:, t:t + 1], axis=0),
                            in_=y[e % 2][:, t, :], in_offset=None, bounds_check=K0 * N - 1,
                            oob_is_err=False).then_inc(y_kept[e % 2], 16)
                for u in two:
                    pool.wait_ge(y_kept[u], E0 // 2 * ST * 16)

            @block.sync
            def _(sp):
                @repeat(sp, E0 // 2)
                def _(i):
                    for u in two:
                        e = i * 2 + u
                        wait_past(sp, y_psum, i * 2 + u - 1)
                        sp.dma_start(w1[u][:], I["W1"][bass.ds(e, 1)].rearrange("o d h -> (o d) h")).then_inc(w_here[u], 16)
                        sp.dma_start(w2[u][:], I["W2"][bass.ds(e, 1)].rearrange("o p c d -> (o p) c d")).then_inc(w_here[u], 16)
                        sp.dma_start(b1[u][:], I["b1"][bass.ds(e, 1)].rearrange("o p c -> (o p) c")).then_inc(w_here[u], 16)
                        wait_past(sp, y_done, i * 2 + u - 1)
                        sp.dma_start(b2[u][:], I["b2"][bass.ds(e, 1), :].to_broadcast([P, C])).then_inc(w_here[u], 16)
                        sp.wait_ge(scattered, TILES * K0 * 16)
                        sp.dma_start(rows[u][:], G.sorted0[bass.ds(e * SLOTS0, SLOTS0), :]
                                     .rearrange("(s p) c -> p s c", p=P)).then_inc(rows_here[u], 16)

            @block.tensor
            def _(pe):
                def turn(e, u, used):
                    pe.wait_ge(rows_here[u], used * 16 + 16)
                    wait_past(pe, xT_done, e)
                    for s in range(ST):
                        c, at = divmod(s * P, HALF)
                        mm = pe.transpose(B[c][:, at:at + P], rows[u][:, s, 0:C], G.ident[:])
                    mm.then_inc(xT_psum, 1)

                def expert(e, u, used, more):
                    pe.wait_ge(xT_done, e + 1)
                    pe.wait_ge(w_here[u], used * 64 + 64)
                    for c in range(HC):
                        if c < 2:
                            wait_past(pe, h_done, e * HC)
                        else:
                            pe.wait_ge(h_done, e * HC + c - 1)
                        for n, (a, b) in enumerate(PARTS):
                            mm = pe.matmul(B[2 + 2 * (c % 2) + n][:, 0:b - a], w1[u][:, c * P:(c + 1) * P],
                                           xT[u][:, a:b], start=True, stop=True)
                        mm.then_inc(h_psum, 1)
                    if more:
                        turn(e + 1, 1 - u, used + u)
                    wait_past(pe, y_done, e)
                    for s in range(ST):
                        n, at = divmod(s * C, HALF)
                        for c in range(HC):
                            if s == 0:
                                pe.wait_ge(h_done, e * HC + c + 1)
                            mm = pe.matmul(B[6 + n][:, at:at + C], hT[:, c, s * P:(s + 1) * P], w2[u][:, c, :],
                                           start=(c == 0 and at == 0), stop=(c == HC - 1), skip_group_check=True)
                    mm.then_inc(y_psum, 1)
                turn(0, 0, 0)
                pairs(pe, expert)

            @block.scalar
            def _(act):
                def copy(e, u):
                    act.wait_ge(xT_psum, e + 1)
                    for n, (a, b) in enumerate(PARTS):
                        last = act.activation(xT[u][:, a:b], B[n][:, 0:b - a], ACT.Copy)
                    last.then_inc(xT_done, 1)

                def expert(e, u, used, more):
                    act.wait_ge(w_here[u], used * 64 + 64)
                    wait_past(act, y_psum, e)
                    for c in range(HC):
                        act.wait_ge(h_psum, e * HC + c + 1)
                        for n, (a, b) in enumerate(PARTS):
                            last = act.activation(hT[:, c, a:b], B[2 + 2 * (c % 2) + n][:, 0:b - a], ACT.Silu,
                                                  bias=b1[u][:, c:c + 1])
                        last.then_inc(h_done, 1)
                    if more:
                        copy(e + 1, 1 - u)
                copy(0, 0)
                pairs(act, expert)

            @block.vector
            def _(dve):
                @repeat(dve, E0 // 2)
                def _(i):
                    for u in two:
                        dve.wait_ge(y_psum, i * 2 + u + 1)
                        wait_past(dve, y_kept[u], i * (ST * 16))
                        dve.wait_ge(rows_here[u], i * 16 + 16)
                        dve.tensor_copy(place[u][:], rows[u][:, :, C]).then_inc(place_done, 1)
                        for n, (a, b) in enumerate(PARTS):
                            k = (b - a) // P
                            last = dve.tensor_tensor(y[u][:, a // P:b // P, :], B[6 + n][:, 0:b - a].rearrange("p (s c) -> p s c", c=C),
                                                     b2[u][:, None, :].to_broadcast([P, k, C]), ALU.add)
                        last.then_inc(y_done, 1)


LOAD_PARTS = 4


def emit_combine_load(sp, b, got, here, expert_out, choices):
    rows, part = SEQ * choices, SEQ * choices // LOAD_PARTS
    for q in range(LOAD_PARTS):
        t = slice(q * TB // LOAD_PARTS, (q + 1) * TB // LOAD_PARTS)
        sp.dma_start(got[:, t].rearrange("p t k c -> p t (k c)"),
                     expert_out[bass.ds(b * rows + q * part, part), :]
                     .rearrange("(t p k) c -> p t (k c)", p=P, k=choices)).then_inc(here, 16)


def emit_product(engine, b, got, gate, k):
    return engine.tensor_tensor(got[:, :, k, :], got[:, :, k, :], gate[:, tiles(b), k:k + 1].to_broadcast([P, TB, C]), ALU.mult)


def emit_combine(dve, order, b, got, gate, choices, x, y, others):
    for k in range(choices - choices // 2):
        last = emit_product(dve, b, got, gate, k)
    order.done(last)
    order.done(dve.tensor_tensor(y, got[:, :, 0, :], x, ALU.add))
    for k in range(1, choices):
        if k == choices - choices // 2:
            others()
        last = dve.tensor_tensor(y, y, got[:, :, k, :], ALU.add)
        order.done(last)


def stage_qkv(nc, G, I):
    GROUPS = HEADS // GH
    NORMED = 1 * BATCH
    with ExitStack() as ctx:
        M = Mem(nc, ctx)
        w_q, w_k, w_v = M.sb("wq_sb", [P, C]), M.sb("wk_sb", [P, C]), M.sb("wv_sb", [P, C])
        b_q, b_k, b_v = M.sb("bq1_sb", [P, 1]), M.sb("bk1_sb", [P, 1]), M.sb("bv1_sb", [P, C])
        x_new, xT = M.sb("qx_new", [P, TB, C]), M.sb("qxT", [P, SEQ])
        got, y = M.sb("got", [P, TB, K0, C]), M.sb("combined", [P, TB, C])
        got_here = M.sem("got_here")
        stats, mv = M.sb("qstats", [P, TB, 6]), M.sb("qmv", [P, TB, 2])
        var_eps, rstd = M.sb("qvar_eps", [P, TB]), M.sb("qrstd", [P, TB])
        qk = [M.sb("q_full", [P, SEQ]), M.sb("k_full", [P, SEQ])]
        rest_of = [M.sb("q_rest", [P, SEQ]), M.sb("k_rest", [P, SEQ])]
        parts = [M.sb("q_parts", [P, 3, SEQ], bf16), M.sb("k_parts", [P, 3, SEQ], bf16)]
        v_rows = M.sb("v_rows", [P, GROUPS, TB, GH, HD + 1])
        weights, ones_set = M.sem("weights"), M.sem("ones_set")
        norm_done, xT_psum, xT_done, x_kept = M.sem("norm_done"), M.sem("xT_psum"), M.sem("xT_done"), M.sem("x_kept")
        proj, qk_full = [M.sem("q_psum"), M.sem("k_psum")], [M.sem("q_full_done"), M.sem("k_full_done")]
        v_psum, v_done, v_kept = M.sem("v_psum"), M.sem("v_done"), M.sem("v_kept")
        part_done, rest_done, parts_kept = [M.sem("q_part"), M.sem("k_part")], [M.sem("q_rest_s"), M.sem("k_rest_s")], M.sem("parts_kept")
        B = G.bank
        with nc.Block() as block:
            @block.sync
            def _(sp):
                def load(i):
                    if i:
                        sp.wait_ge(G.var_ready, NORMED + i)
                    emit_combine_load(sp, i, got, got_here, G.expert_out0, K0)

                load(0)
                for dst, name in ((w_q, "Wq"), (w_k, "Wk"), (w_v, "Wv"), (b_q, "bq"), (b_k, "bk")):
                    sp.dma_start(dst[:], I[name]).then_inc(weights, 16)
                sp.dma_start(b_v[:], I["bv"].to_broadcast([P, C])).then_inc(weights, 16)
                def keep(i):
                    sp.wait_ge(norm_done, i + 1)
                    sp.dma_start(G.x_rows[:, tiles(i), :], x_new[:]).then_inc(x_kept, 16)

                load(1)
                keep(0)
                for i in range(BATCH):
                    if i + 2 < BATCH:
                        load(i + 2)
                    sp.wait_ge(v_done, i * TB + TB)
                    sp.dma_start(G.v_steps[bass.ds(i * GROUPS, GROUPS)].rearrange("g p n -> p g n"),
                                 v_rows[:].rearrange("p g t h e -> p g (t h e)")).then_inc(v_kept, 16)
                    for j in range(3):
                        for s, store in enumerate((G.q_steps, G.k_steps)):
                            sp.wait_ge(part_done[s], i * 3 + j + 1)
                            sp.dma_start(store[bass.ds(i * GROUPS, GROUPS), j], parts[s][:, j, :])\
                              .then_inc(parts_kept, 16)
                        if j == 0 and i + 1 < BATCH:
                            keep(i + 1)
                    if i == 0:
                        for b in range(BUFS):
                            sp.dma_start(G.qa[b][ALIBI_AT:ALIBI_AT + 3].rearrange("r h n -> r (h n)"),
                                         I["c_alibi"][0, 3:6, :]).then_inc(G.ones_here, 16)
                    elif i < 3:
                        if i == 1:
                            sp.wait_ge(parts_kept, 2 * 6 * 16)
                            sp.wait_ge(v_kept, 2 * 16)
                        emit_load(sp, G, I, Step(i - 1, i - 1, 0))
                sp.wait_ge(x_kept, BATCH * 16)
                sp.wait_ge(v_kept, BATCH * 16)
                sp.wait_ge(parts_kept, BATCH * 6 * 16)

            @block.gpsimd
            def _(pool):
                pool.memset(v_rows[:], 1.0).then_inc(ones_set, 1)

                def product(i):
                    pool.wait_ge(got_here, i * (LOAD_PARTS * 16) + LOAD_PARTS * 16)
                    emit_product(pool, i, got, G.gate0, 1).then_inc(G.product_done, 1)
                product(0)
                emit_norm_pool(pool, G, NORMED, var_eps, rstd)
                product(1)
                for i in range(BATCH):
                    if i + 1 < BATCH:
                        emit_norm_pool(pool, G, NORMED + i + 1, var_eps, rstd)
                    pool.wait_ge(part_done[1], i * 3 + 1)
                    pool.tensor_tensor(rest_of[1][:], qk[1][:], parts[1][:, 0, :], ALU.subtract).then_inc(rest_done[1], 1)
                    if i + 2 < BATCH:
                        product(i + 2)
                    pool.wait_ge(part_done[1], i * 3 + 2)
                    pool.tensor_tensor(parts[1][:, 2, :], rest_of[1][:], parts[1][:, 1, :], ALU.subtract).then_inc(part_done[1], 1)

            @block.tensor
            def _(pe):
                pe.wait_ge(weights, 6 * 16)
                @repeat(pe, BATCH)
                def _(i):
                    pe.wait_ge(norm_done, i + 1)
                    for t in range(TB):
                        mm = pe.transpose(B[t // 4][:, (t % 4) * P:(t % 4 + 1) * P], x_new[:, t, :], G.ident[:])
                        if t % 4 == 3:
                            mm.then_inc(xT_psum, 1)
                    for s, w in enumerate((w_q, w_k)):
                        for c in range(2):
                            if s == 0:
                                pe.wait_ge(xT_done, i * 2 + c + 1)
                            wait_past(pe, qk_full[s], i * 2)
                            pe.matmul(B[2 + 2 * s + c][:], w[:], xT[:, c * HALF:(c + 1) * HALF],
                                      start=True, stop=True).then_inc(proj[s], 1)
                    wait_past(pe, v_done, i * TB)
                    for t in range(TB):
                        mm = pe.matmul(B[6 + t // 4][:, (t % 4) * P:(t % 4 + 1) * P], xT[:, t * P:(t + 1) * P], w_v[:],
                                       start=(t % 4 == 0), stop=True, skip_group_check=True)
                        if t % 4 == 3:
                            mm.then_inc(v_psum, 1)

            @block.scalar
            def _(act):
                act.wait_ge(weights, 6 * 16)

                def ahead(i):
                    wait_past(act, v_psum, i * 2)
                    for c in range(2):
                        act.wait_ge(xT_psum, i * 2 + c + 1)
                        act.activation(xT[:, c * HALF:(c + 1) * HALF], B[c][:], ACT.Copy).then_inc(xT_done, 1)

                def rest(i, more):
                    wait_past(act, part_done[1], i * 3)
                    for c in range(2):
                        act.wait_ge(proj[1], i * 2 + c + 1)
                        act.activation(qk[1][:, c * HALF:(c + 1) * HALF], B[4 + c][:], ACT.Identity,
                                       bias=b_k[:]).then_inc(qk_full[1], 1)
                    for s in range(2):
                        act.wait_ge(qk_full[s], i * 2 + 2)
                        wait_past(act, parts_kept, i * 96)
                        act.activation(parts[s][:, 0, :], qk[s][:], ACT.Copy).then_inc(part_done[s], 1)
                    if more:
                        ahead(i + 1)
                    for s in range(2):
                        act.wait_ge(rest_done[s], i + 1)
                        act.activation(parts[s][:, 1, :], rest_of[s][:], ACT.Copy).then_inc(part_done[s], 1)
                one_ahead(act, ahead, rest)

            @block.vector
            def _(dve):
                dve.wait_ge(weights, 6 * 16)
                dve.wait_ge(ones_set, 1)

                row = lambda t: y[:, t, :]

                def moments(i):
                    order = Order(dve, G.steps, BATCH * STEPS_A + i * STEPS_QKV)
                    dve.wait_ge(got_here, i * (LOAD_PARTS * 16) + LOAD_PARTS * 16)
                    emit_combine(dve, order, i, got, G.gate0, K0, G.x_rows[:, tiles(i), :], y[:],
                                 lambda: dve.wait_ge(G.product_done, i + 1))
                    emit_norm_moments(dve, G, order, row, stats, mv, var_eps)
                    assert order.count == STEPS_QKV

                def scale(i):
                    wait_past(dve, x_kept, i * 16)
                    wait_past(dve, xT_psum, i * 2)
                    emit_norm_scale(dve, G, NORMED + i, row, mv, rstd, lambda t: x_new[:, t, :]).then_inc(norm_done, 1)

                def ahead(i):
                    moments(i)
                    scale(i)

                def rest(i, more):
                    if more:
                        moments(i + 1)
                    for c in range(2):
                        dve.wait_ge(proj[0], i * 2 + c + 1)
                        dve.tensor_scalar(qk[0][:, c * HALF:(c + 1) * HALF], B[2 + c][:], b_q[:],
                                          float(1 / np.sqrt(np.float32(HD))), ALU.add, ALU.mult).then_inc(qk_full[0], 1)
                    wait_past(dve, v_kept, i * 16)
                    for t in range(TB):
                        if t % 4 == 0:
                            dve.wait_ge(v_psum, i * 2 + t // 4 + 1)
                        dve.tensor_tensor(v_rows[:, :, t, :, 0:HD],
                                          B[6 + t // 4][:, (t % 4) * P:(t % 4 + 1) * P].rearrange("p (g h e) -> p g h e", g=GROUPS, h=GH),
                                          b_v[:].rearrange("p (g h e) -> p g h e", g=GROUPS, h=GH), ALU.add).then_inc(v_done, 1)
                    if more:
                        scale(i + 1)
                    dve.wait_ge(part_done[0], i * 3 + 1)
                    dve.tensor_tensor(rest_of[0][:], qk[0][:], parts[0][:, 0, :], ALU.subtract).then_inc(rest_done[0], 1)
                    dve.wait_ge(part_done[0], i * 3 + 2)
                    dve.tensor_tensor(parts[0][:, 2, :], rest_of[0][:], parts[0][:, 1, :], ALU.subtract).then_inc(part_done[0], 1)
                one_ahead(dve, ahead, rest)


def max_units():
    units = []
    for qt in range(TB):
        for seg in range(qt // 4 + 1):
            width = min(HALF, (qt + 1) * P - seg * HALF)
            heads = max(1, min(GH, HALF // width))
            if qt == 0:
                heads = 2
            units += [(qt, seg, h, heads, width) for h in range(0, GH, heads)]
    return units + ["maxima"]


EXP_UNITS = [(c, j) for c in range(2) for j in range(4 * c + 4)]
MAX_UNITS = max_units()
EARLY = 8
AT_SECOND, AT_FIRST = 2, 9
BUFS = 3
EVEN = 1.0
PRING = 3


class Step:

    def __init__(self, n, buf, used):
        self.n, self.buf, self.used = n, buf, used

    def next(self, by=1):
        b = self.buf + by
        return Step(self.n + by, b % BUFS, self.used + b // BUFS)


LOADS = 6 * 16


def emit_load(sp, G, I, s):
    def sl(store):
        return store[bass.ds(s.n, 1)] if not isinstance(s.n, int) else store[s.n:s.n + 1]
    q = sl(G.q_steps)
    k = sl(G.k_steps)
    for j in range(3):
        sp.dma_start(G.qa[s.buf][j * HD * 3:(j + 1) * HD * 3].rearrange("r h n -> r (h n)"),
                     q.rearrange("o i (d h) n -> (o d) i (h n)", d=HD)).then_inc(G.here[s.buf], 16)
    sp.dma_start(G.ka[s.buf][0:PROD].rearrange("r h n -> r (h n)"),
                 k.rearrange("o j (d h) n -> (o j d) (h n)", d=HD)[:, None, :].to_broadcast([3 * HD, 3, GH * SEQ])
                 ).then_inc(G.here[s.buf], 16)
    sp.dma_start(G.va[s.buf][:].rearrange("p t h e -> p (t h e)"),
                 sl(G.v_steps).rearrange("o p n -> (o p) n")).then_inc(G.here[s.buf], 16)
    al = I["c_alibi"]
    al = al[bass.ds(s.n, 1)] if not isinstance(s.n, int) else al[s.n:s.n + 1]
    sp.dma_start(G.ka[s.buf][ALIBI_AT:ALIBI_AT + 6].rearrange("r h n -> r (h n)"),
                 al.rearrange("o r n -> (o r) n")).then_inc(G.here[s.buf], 16)


class Operands:

    def __init__(self, M, G):
        G.qa = [M.sb(f"qa{b}", [P, GH, SEQ], bf16) for b in range(BUFS)]
        G.ka = [M.sb(f"ka{b}", [P, GH, SEQ], bf16) for b in range(BUFS)]
        G.va = [M.sb(f"va{b}", [P, TB, GH, HD + 1]) for b in range(BUFS)]
        G.here = [M.sem(f"operands_here{b}") for b in range(BUFS)]
        G.ones_here = M.sem("ones_here")


def schedule(first, more, more2):
    work = [("max", 1, u) for u in MAX_UNITS[EARLY:]] if more else []
    work2 = [("max", 2, u) for u in MAX_UNITS[:EARLY]] if more2 else []
    slots = []
    K = len(EXP_UNITS)
    share = [EVEN + min(HALF, (c + 1) * HALF - j * P) / HALF for c, j in EXP_UNITS[:K - 2]]
    upto = [round(len(work) * sum(share[:k]) / sum(share)) for k in range(K - 1)]
    for k in range(K):
        if k < K - 2:
            slot = work[upto[k]:upto[k + 1]]
        else:
            a, b = len(work2) * (k - K + 2) // 2, len(work2) * (k - K + 3) // 2
            slot = work2[a:b]
        if k == AT_SECOND and not first:
            slot = slot + [("out", -1, 1)]
        if k == AT_FIRST:
            slot = slot + [("out", 0, 0)]
        slots.append(slot)
    return slots


def step_plan():
    def flags(n):
        return n == 0, n + 1 < STEPS, n + 2 < STEPS
    count = lambda n: sum(map(len, schedule(*flags(n))))
    base = [len(MAX_UNITS) + EARLY]
    for n in range(STEPS):
        base.append(base[-1] + count(n))
    assert all(base[n] == base[1] + (n - 1) * (base[2] - base[1]) for n in range(1, STEPS - 1)), base
    assert (base[2] - base[1]) % 2 == 0
    return flags, base


def run_steps(engine, body):
    flags, base = step_plan()
    per = base[2] - base[1]
    body(Step(0, 0, 0), base[0], base[0] % 2, flags(0))
    rounds = (STEPS - 1 - 2) // BUFS
    with engine.Fori(0, rounds) as i:
        for r in range(BUFS):
            n = 1 + r
            body(Step(i * BUFS + n, n % BUFS, i + n // BUFS), i * (BUFS * per) + base[n], base[n] % 2, flags(n))
    for n in range(1 + rounds * BUFS, STEPS):
        body(Step(n, n % BUFS, n // BUFS), base[n], base[n] % 2, flags(n))
    return base[STEPS]


def stage_attention(nc, G, I):
    with ExitStack() as ctx:
        M = Mem(nc, ctx)
        qa, ka, va, here, ones_here = G.qa, G.ka, G.va, G.here, G.ones_here
        probs = [M.sb(f"probs{b}", [P, GH, HALF]) for b in range(PRING)]
        outT = [M.sb(f"outT{c}", [P, HALF]) for c in range(2)]
        maxima, neg_max = M.sb("maxima", [P, 2, GH, TB]), M.sb("neg_max", [P, TB * GH])
        max_parts, max_rest = M.sb("max_parts", [TB * GH, 3, P], bf16), M.sb("max_rest", [TB * GH, P])
        recip = [M.sb(f"recip{c}", [P, 4, GH]) for c in range(2)]
        ident_b, mask_q, mask_k = M.sb("ident_b", [P, P], bf16), M.sb("mask_q", [P, P], bf16), M.sb("mask_k", [P, P], bf16)
        max_here = [M.sem(f"max_rows_here{b}") for b in range(BUFS)]
        preset, masks = M.sem("preset"), M.sem("masks")
        scores, exps, pv = M.sem("scores"), M.sem("exps"), M.sem("pv")
        small, small_read, out_read, split = M.sem("small"), M.sem("small_read"), M.sem("out_read"), M.sem("split")
        order_sem, rows_done, neg_done = M.sem("order"), M.sem("rows_done"), M.sem("neg_done")
        PS, B = G.psum, G.bank
        SMALL, OUT = (4, 5), (6, 7)
        Q = len(EXP_UNITS)
        _, base_of = step_plan()


        def emit_max_rows(sp, s):
            sp.wait_ge(split, s.n + 1)
            for r in range(3):
                sp.dma_start(qa[s.buf][MAX_AT + r:MAX_AT + r + 1].rearrange("o h (t q) -> o (h t) q", q=P),
                             max_parts[:, r, :]).then_inc(max_here[s.buf], 16)

        with nc.Block() as block:
            @block.gpsimd
            def _(pool):
                pool.memset(ident_b[:], 0.0).then_inc(preset, 1)
                pool.memset(mask_q[:], 0.0).then_inc(preset, 1)
                pool.memset(mask_k[:], 0.0).then_inc(preset, 1)
                pool.memset(maxima[:], -3.0e38).then_inc(preset, 1)
                pool.wait_ge(preset, 4)
                pool.affine_select(out=ident_b[:], in_=ident_b[:], compare_op=ALU.not_equal, fill=1.0,
                                   base=0, pattern=[[-1, P]], channel_multiplier=1).then_inc(masks, 1)
                pool.affine_select(out=mask_q[:], in_=mask_q[:], compare_op=ALU.is_ge, fill=MASKED,
                                   base=0, pattern=[[-1, P]], channel_multiplier=1).then_inc(masks, 1)
                pool.affine_select(out=mask_k[:], in_=mask_k[:], compare_op=ALU.is_ge, fill=MASKED,
                                   base=0, pattern=[[1, P]], channel_multiplier=-1).then_inc(masks, 1)
                for q in range(CLEARS1):
                    pool.wait_ge(exps, (q // 2 + 1) * (2 * Q))
                    emit_clear(pool, G.sorted1[q * (ROWS1 // CLEARS1):(q + 1) * (ROWS1 // CLEARS1)], G.blank[:], G.cleared)

            @block.sync
            def _(sp):
                emit_max_rows(sp, Step(0, 0, 0))

                def body(s, base, odd, flags):
                    first, more, more2 = flags
                    if more2:
                        if not first:
                            sp.wait_ge(pv, s.n * Q)
                            sp.wait_ge(ones_here, BUFS * 16)
                        emit_load(sp, G, I, s.next(2))
                    if more:
                        emit_max_rows(sp, s.next())
                run_steps(sp, body)

            @block.tensor
            def _(pe):
                pe.wait_ge(masks, 3)
                pe.wait_ge(ones_here, BUFS * 16)
                pe.wait_ge(rows_done, 1)

                def emit_small(number, odd, s, what):
                    kind, ahead, u = what
                    bank = B[SMALL[odd]]
                    if not isinstance(number, int) or number >= 2:
                        pe.wait_ge(small_read, number - 1)
                    if kind == "out":
                        pe.wait_ge(out_read, (s.n + ahead) * 2 + u + 1)
                        for t in range(4):
                            mm = pe.transpose(bank[:, t * P:(t + 1) * P], outT[u][:, t * P:(t + 1) * P], G.ident[:])
                    elif u == "maxima":
                        pe.wait_ge(small_read, number)
                        pe.wait_ge(neg_done, s.n + ahead + 1)
                        mm = pe.transpose(bank[0:TB * GH, 0:P], neg_max[:], G.ident[:])
                    else:
                        b = (s.buf + ahead) % BUFS
                        qt, seg, h0, heads, width = u
                        if u == MAX_UNITS[0]:
                            t = s.next(ahead) if ahead else s
                            pe.wait_ge(here[b], t.used * LOADS + LOADS)
                        for h in range(heads):
                            mm = pe.matmul(bank[:, h * width:(h + 1) * width], qa[b][0:ROWS_MAX, h0 + h, qt * P:(qt + 1) * P],
                                           ka[b][0:ROWS_MAX, h0 + h, seg * HALF:seg * HALF + width],
                                           start=(h == 0), stop=True, skip_group_check=True)
                        if seg * HALF + width == (qt + 1) * P:
                            for h in range(heads):
                                mm = pe.matmul(bank[:, (h + 1) * width - P:(h + 1) * width], ident_b[:], mask_q[:],
                                               start=False, stop=True, skip_group_check=True)
                    mm.then_inc(small, 1)

                def emit_scores(s, k, pair):
                    c, j = EXP_UNITS[k]
                    q0 = max(c * HALF, j * P)
                    if k or not isinstance(s.n, int) or s.n:
                        pe.wait_ge(exps, s.n * (2 * Q) + 2 * k + pair - 1)
                    for h in (2 * pair, 2 * pair + 1):
                        out = B[h][:, 0:(c + 1) * HALF - q0]
                        mm = pe.matmul(out, ka[s.buf][0:ROWS_ALL, h, j * P:(j + 1) * P],
                                       qa[s.buf][0:ROWS_ALL, h, q0:(c + 1) * HALF], start=True, stop=True,
                                       skip_group_check=True)
                        if q0 == j * P:
                            mm = pe.matmul(out[:, 0:P], ident_b[:], mask_k[:], start=False, stop=True,
                                           skip_group_check=True)
                    mm.then_inc(scores, 1)

                def emit_pv(s, k):
                    c, j = EXP_UNITS[k]
                    q0 = max(c * HALF, j * P)
                    pe.wait_ge(exps, s.n * (2 * Q) + 2 * k + 2)
                    if j == 0 and (not isinstance(s.n, int) or s.n):
                        pe.wait_ge(out_read, s.n * 2 - 1 + c)
                    for h in range(GH):
                        mm = pe.matmul(B[OUT[c]][32 * h:32 * h + HD + 1, q0 - c * HALF:HALF],
                                       va[s.buf][:, j, h, :], probs[k % PRING][:, h, 0:(c + 1) * HALF - q0],
                                       start=(j == 0), stop=(j == 4 * c + 3), skip_group_check=True)
                    mm.then_inc(pv, 1)

                number = 0
                for s, units in ((Step(0, 0, 0), MAX_UNITS), (Step(1, 1, 0), MAX_UNITS[:EARLY])):
                    for u in units:
                        emit_small(number, number % 2, s, ("max", 0, u))
                        number += 1

                def body(s, base, odd, flags):
                    pe.wait_ge(max_here[s.buf], s.used * 48 + 48)
                    n = 0
                    for k, slot in enumerate(schedule(*flags)):
                        behind = []
                        if slot and slot[-1][2] == "maxima":
                            slot, behind = slot[:-1], slot[-1:]
                        apart = [slot[:len(slot) // 3], slot[len(slot) // 3:2 * len(slot) // 3], slot[2 * len(slot) // 3:]]
                        for part, pair in zip(apart, (0, 1, None)):
                            for what in part:
                                emit_small(base + n, (odd + n) % 2, s, what)
                                n += 1
                            if pair is not None:
                                emit_scores(s, k, pair)
                        if k:
                            emit_pv(s, k - 1)
                        elif not flags[0]:
                            before = Step(s.n - 1, (s.buf - 1) % BUFS, 0)
                            emit_pv(before, Q - 1)
                        for what in behind:
                            emit_small(base + n, (odd + n) % 2, s, what)
                            n += 1
                base = run_steps(pe, body)
                last = Step(STEPS - 1, (STEPS - 1) % BUFS, 0)
                emit_pv(last, Q - 1)
                emit_small(base, base % 2, last, ("out", 0, 1))

            @block.scalar
            def _(act):
                def emit_out(s, c, before):
                    act.wait_ge(pv, s.n * Q + (4 if c == 0 else Q))
                    if before is not None:
                        act.wait_ge(small, before)
                    act.activation(outT[c][:], B[OUT[c]], ACT.Copy).then_inc(out_read, 1)

                def at_out(flags, c):
                    n = 0
                    for slot in schedule(*flags):
                        for what in slot:
                            n += 1
                            if what[0] == "out" and what[2] == c:
                                return n

                def body(s, base, odd, flags):
                    for k in range(Q):
                        c, j = EXP_UNITS[k]
                        q0 = max(c * HALF, j * P)
                        w = (c + 1) * HALF - q0
                        if k >= PRING or not flags[0]:
                            act.wait_ge(pv, s.n * Q + k - PRING + 1)
                        for pair in range(2):
                            act.wait_ge(scores, s.n * (2 * Q) + 2 * k + pair + 1)
                            act.activation(probs[k % PRING][:, 2 * pair:2 * pair + 2, 0:w],
                                           PS[:, 2 * pair:2 * pair + 2, 0:w], ACT.Exp).then_inc(exps, 1)
                        if k == AT_SECOND - 1 and not flags[0]:
                            emit_out(Step(s.n - 1, 0, 0), 1, base)
                        if k == AT_FIRST - 2:
                            emit_out(s, 0, None if flags[0] else base)
                run_steps(act, body)
                emit_out(Step(STEPS - 1, 0, 0), 1, base_of[STEPS])

            @block.vector
            def _(dve):
                for c in range(2):
                    last = dve.memset(B[OUT[c]], 0.0)
                last.then_inc(rows_done, 1)
                dve.wait_ge(masks, 3)
                dve.wait_ge(preset, 4)

                def emit_small(number, odd, s, what, order):
                    kind, ahead, u = what
                    bank = B[SMALL[odd]]
                    dve.wait_ge(small, number + 1)
                    if kind == "out":
                        v = bank.rearrange("p (t h e) -> p t h e", t=4, h=GH)
                        order.done(dve.reciprocal(recip[u][:], v[:, :, :, HD]))
                        n = s.n + ahead
                        dst = G.att_steps[:, bass.ds(n * 2 + u, 1)] if not isinstance(n, int) else G.att_steps[:, n * 2 + u:n * 2 + u + 1]
                        dve.tensor_tensor(dst.rearrange("p o t (h e) -> p (o t) h e", h=GH), v[:, :, :, 0:HD],
                                          recip[u][:, :, :, None].to_broadcast([P, 4, GH, HD]), ALU.mult).then_inc(small_read, 1)
                    elif u == "maxima":
                        order.done(dve.tensor_copy(max_parts[:, 0, :], bank[0:TB * GH, 0:P]))
                        dve.tensor_tensor(max_rest[:], bank[0:TB * GH, 0:P], max_parts[:, 0, :], ALU.subtract).then_inc(small_read, 1)
                        dve.wait_ge(small_read, number + 1)
                        order.done(dve.tensor_copy(max_parts[:, 1, :], max_rest[:]))
                        dve.tensor_tensor(max_parts[:, 2, :], max_rest[:], max_parts[:, 1, :], ALU.subtract).then_inc(split, 1)
                    else:
                        qt, seg, h0, heads, width = u
                        dve.tensor_reduce(maxima[:, seg, h0:h0 + heads, qt],
                                          bank[:, 0:heads * width].rearrange("p (h k) -> p h k", h=heads),
                                          AX.X, ALU.max).then_inc(small_read, 1)
                        if u == MAX_UNITS[-2]:
                            t = s.next(ahead) if ahead else s
                            dve.wait_ge(small_read, number + 1)
                            order.done(dve.tensor_tensor(neg_max[:], maxima[:, 0].rearrange("p h t -> p (h t)"),
                                                         maxima[:, 1].rearrange("p h t -> p (h t)"), ALU.max))
                            dve.tensor_scalar(neg_max[:], neg_max[:], -1.0, None, ALU.mult).then_inc(neg_done, 1)
                            if not isinstance(t.n, int) or t.n:
                                b = (t.buf - 1) % BUFS
                                dve.wait_ge(max_here[b], (t.used + (0 if t.buf else -1)) * 48 + 48)

                number = 0
                order = Order(dve, order_sem)
                for s, units in ((Step(0, 0, 0), MAX_UNITS), (Step(1, 1, 0), MAX_UNITS[:EARLY])):
                    for u in units:
                        emit_small(number, number % 2, s, ("max", 0, u), order)
                        number += 1
                before = order.count
                PER = 5

                def body(s, base, odd, flags):
                    order = Order(dve, order_sem, before + 4 + (s.n - 1) * PER if not flags[0] else before)
                    n = 0
                    for slot in schedule(*flags):
                        for what in slot:
                            emit_small(base + n, (odd + n) % 2, s, what, order)
                            n += 1
                    assert order.count == (4 if flags[0] else PER if flags[1] else 2), order.count
                base = run_steps(dve, body)
                order = Order(dve, order_sem, before + 4 + (STEPS - 2) * PER + 2)
                emit_small(base, base % 2, Step(STEPS - 1, 0, 0), ("out", 0, 1), order)
                dve.wait_ge(small_read, base + 1)



def stage_projection(nc, G, I):
    GROUPS = HEADS // GH
    NORMED = 2 * BATCH
    with ExitStack() as ctx:
        M = Mem(nc, ctx)
        w_o, b_o = M.sb("wo_sb", [P, C]), M.sb("bo_sb", [P, C])
        w_r, b_r = M.sb("wr1_sb", [P, E1]), M.sb("br1_sb", [P, E1])
        att, attT = M.sb("p_att", [P, TB, GROUPS, GH * HD]), M.sb("p_attT", [P, SEQ])
        x_bias, y, x_new, xT = M.sb("p_bias", [P, TB, C]), M.sb("p_y", [P, TB, C]), M.sb("p_new", [P, TB, C]), M.sb("p_xT", [P, SEQ])
        stats, mv = M.sb("p_stats", [P, TB, 6]), M.sb("p_mv", [P, TB, 2])
        var_eps, rstd = M.sb("p_var_eps", [P, TB]), M.sb("p_rstd", [P, TB])
        weights = M.sem("weights")
        att_fixed, attT_psum, attT_done = M.sem("att_fixed"), M.sem("attT_psum"), M.sem("attT_done")
        y_psum, y_taken, xb_done = M.sem("y_psum"), M.sem("y_taken"), M.sem("xb_done")
        norm_done, x_kept, xT_psum, xT_done = M.sem("norm_done"), M.sem("x_kept"), M.sem("xT_psum"), M.sem("xT_done")
        logits_psum, logits_done, xT_kept = M.sem("logits_psum"), M.sem("logits_done"), M.sem("xT_kept")
        B = G.bank
        with nc.Block() as block:
            @block.sync
            def _(sp):
                sp.dma_start(w_o[:], I["Wo"]).then_inc(weights, 16)
                sp.dma_start(b_o[:], I["bo"].to_broadcast([P, C])).then_inc(weights, 16)
                sp.dma_start(w_r[:], I["Wr1"]).then_inc(weights, 16)
                sp.dma_start(b_r[:], I["br1"].to_broadcast([P, E1])).then_inc(weights, 16)

                @repeat(sp, BATCH)
                def _(i):
                    sp.wait_ge(norm_done, i + 1)
                    sp.dma_start(G.x_rows[:, tiles(i), :], x_new[:]).then_inc(x_kept, 16)
                    sp.wait_ge(xT_done, i * 2 + 2)
                    sp.dma_start(G.xT[:, bass.ds(i * SEQ, SEQ)], xT[:]).then_inc(xT_kept, 16)
                sp.wait_ge(x_kept, BATCH * 16)
                sp.wait_ge(xT_kept, BATCH * 16)

            @block.gpsimd
            def _(pool):
                pool.wait_ge(weights, 4 * 16)
                @repeat(pool, BATCH)
                def _(i):
                    wait_past(pool, y_taken, i * 2)
                    pool.tensor_tensor(x_bias[:], G.x_rows[:, tiles(i), :],
                                       b_o[:, None, :].to_broadcast([P, TB, C]), ALU.add).then_inc(xb_done, 1)
                    emit_norm_pool(pool, G, NORMED + i, var_eps, rstd)

            @block.tensor
            def _(pe):
                pe.wait_ge(weights, 4 * 16)

                def ahead(i):
                    pe.wait_ge(att_fixed, i + 1)
                    for t in range(TB):
                        if t % 4 == 0:
                            wait_past(pe, attT_done, i * 2)
                        mm = pe.transpose(B[t // 4][:, (t % 4) * P:(t % 4 + 1) * P], att[:, t].rearrange("p g e -> p (g e)"), G.ident[:])
                        if t % 4 == 3:
                            mm.then_inc(attT_psum, 1)
                    wait_past(pe, y_taken, i * 2)
                    for t in range(TB):
                        if t % 4 == 0:
                            pe.wait_ge(attT_done, i * 2 + t // 4 + 1)
                        mm = pe.matmul(B[2 + t // 4][:, (t % 4) * C:(t % 4 + 1) * C], attT[:, t * P:(t + 1) * P],
                                       w_o[:], start=(t % 4 == 0), stop=True, skip_group_check=True)
                        if t % 4 == 3:
                            mm.then_inc(y_psum, 1)

                def rest(i, more):
                    if more:
                        ahead(i + 1)
                    pe.wait_ge(norm_done, i + 1)
                    wait_past(pe, xT_done, i * 2)
                    for t in range(TB):
                        mm = pe.transpose(B[6 + t // 4][:, (t % 4) * P:(t % 4 + 1) * P], x_new[:, t, :], G.ident[:])
                        if t % 4 == 3:
                            mm.then_inc(xT_psum, 1)
                    wait_past(pe, logits_done, i)
                    for t in range(TB):
                        if t % 4 == 0:
                            pe.wait_ge(xT_done, i * 2 + t // 4 + 1)
                        mm = pe.matmul(B[4][:, t * E1:(t + 1) * E1], xT[:, t * P:(t + 1) * P], w_r[:],
                                       start=(t == 0), stop=True, skip_group_check=True)
                    mm.then_inc(logits_psum, 1)
                one_ahead(pe, ahead, rest)

            @block.scalar
            def _(act):
                def ahead(i):
                    wait_past(act, attT_psum, i * 2)
                    act.activation(att[:].rearrange("p t g e -> p g t e"),
                                   G.att_steps[:, bass.ds(i * 2 * GROUPS, 2 * GROUPS)].rearrange("p (g c) t e -> p g (c t) e", c=2),
                                   ACT.Copy).then_inc(att_fixed, 1)
                    wait_past(act, y_psum, i * 2)
                    for c in range(2):
                        act.wait_ge(attT_psum, i * 2 + c + 1)
                        act.activation(attT[:, c * HALF:(c + 1) * HALF], B[c], ACT.Copy).then_inc(attT_done, 1)

                def rest(i, more):
                    if more:
                        ahead(i + 1)
                    wait_past(act, xT_kept, i * 16)
                    wait_past(act, logits_psum, i)
                    for c in range(2):
                        act.wait_ge(xT_psum, i * 2 + c + 1)
                        act.activation(xT[:, c * HALF:(c + 1) * HALF], B[6 + c], ACT.Copy).then_inc(xT_done, 1)
                one_ahead(act, ahead, rest)

            @block.vector
            def _(dve):
                dve.wait_ge(weights, 4 * 16)
                row = lambda t: y[:, t, :]

                def moments(i):
                    order = Order(dve, G.steps, BATCH * (STEPS_A + STEPS_QKV) + i * STEPS_PROJECTION)
                    wait_past(dve, norm_done, i)
                    dve.wait_ge(xb_done, i + 1)
                    for c in range(2):
                        dve.wait_ge(y_psum, i * 2 + c + 1)
                        dve.tensor_tensor(y[:, 4 * c:4 * c + 4, :], B[2 + c].rearrange("p (t n) -> p t n", t=4),
                                          x_bias[:, 4 * c:4 * c + 4, :], ALU.add).then_inc(y_taken, 1)
                    dve.wait_ge(y_taken, i * 2 + 2)
                    emit_norm_moments(dve, G, order, row, stats, mv, var_eps)
                    assert order.count == STEPS_PROJECTION

                def scale(i):
                    wait_past(dve, x_kept, i * 16)
                    wait_past(dve, xT_psum, i * 2)
                    emit_norm_scale(dve, G, NORMED + i, row, mv, rstd, lambda t: x_new[:, t, :]).then_inc(norm_done, 1)

                def ahead(i):
                    moments(i)
                    scale(i)

                def rest(i, more):
                    if more:
                        moments(i + 1)
                    dve.wait_ge(logits_psum, i + 1)
                    dve.tensor_tensor(G.logits1[:, tiles(i), :], B[4][:, 0:TB * E1].rearrange("p (t e) -> p t e", e=E1),
                                      b_r[:, None, :].to_broadcast([P, TB, E1]), ALU.add).then_inc(logits_done, 1)
                    if more:
                        scale(i + 1)
                one_ahead(dve, ahead, rest)


def stage_route1(nc, G, I):
    HC = HS // P
    HALVES = N // HALF
    with ExitStack() as ctx:
        M = Mem(nc, ctx)
        R = Router(M, G, E1, K1, "r1")
        w_g, w_u, w_d = M.sb("sg_sb", [P, HS]), M.sb("su_sb", [P, HS]), M.sb("sd_sb", [P, HC, C])
        silu, hT = [M.sb(f"s_silu{u}", [P, HALF]) for u in range(2)], M.sb("s_hT", [P, HC, HALF])
        tiles_i, tiles_f = M.sb("tiles_i", [P, E1], i32), M.sb("tiles_f", [P, E1])
        ends, starts = M.sb("ends", [P, E1]), M.sb("starts", [P, E1])
        compared, expert_f = M.sb("cmp", [P, E1]), M.sb("expert_f", [P, 2])
        loaded, rows_ready, scattered = M.sem("loaded"), M.sem("rows_ready"), M.sem("scattered")
        expert_done, expert_psum, experts_loaded = M.sem("expert_done"), M.sem("expert_psum"), M.sem("experts_loaded")
        gu_psum, silu_done, h_done, y_psum, acc_done = M.sem("gu_psum"), M.sem("silu_done"), M.sem("h_done"), M.sem("y_psum"), M.sem("acc_done")
        B = G.bank
        before_bank, total_bank = [B[0], B[1]], [B[2], B[3]]
        with nc.Block() as block:
            @block.sync
            def _(sp):
                sp.dma_start(R.goes_on[:].rearrange("p e t -> p (e t)"),
                             I["c_goes_on"].to_broadcast([P, E1 * TILES])).then_inc(loaded, 16)
                sp.dma_start(w_g[:], I["sg"]).then_inc(loaded, 16)
                sp.dma_start(w_u[:], I["su"]).then_inc(loaded, 16)
                sp.dma_start(w_d[:], I["sd"]).then_inc(loaded, 16)
                sp.dma_start(G.w_gu[:], I["gu"]).then_inc(experts_loaded, 16)
                sp.dma_start(G.w_down[:], I["down"]).then_inc(experts_loaded, 16)
                sp.wait_ge(experts_loaded, 32)

            @block.gpsimd
            def _(pool):
                pool.wait_ge(G.cleared, (2 + CLEARS1) * 16)
                emit_scatter(pool, G, G.place_of1, G.to_row1, K1, G.sorted1, ROWS1 - 1, scattered, K0, rows_ready)

            @block.tensor
            def _(pe):
                emit_count_tensor(pe, R, 1, R.mask, before_bank, total_bank)
                pe.wait_ge(expert_done, 1)
                for c in range(2):
                    mm = pe.matmul(B[0][0:1, c * P:(c + 1) * P], expert_f[:, c:c + 1], G.ident[:],
                                   start=(c == 0), stop=True, skip_group_check=True)
                mm.then_inc(expert_psum, 1)
                pe.wait_ge(loaded, 4 * 16)
                @repeat(pe, HALVES)
                def _(i):
                    for c in range(HC):
                        if c < 2:
                            wait_past(pe, h_done, i * HC)
                        else:
                            wait_past(pe, h_done, i * HC + c - 1)
                        for n, w in enumerate((w_g, w_u)):
                            mm = pe.matmul(B[4 + 2 * (c % 2) + n], w[:, c * P:(c + 1) * P],
                                           G.xT[:, bass.ds(i * HALF, HALF)], start=True, stop=True)
                        mm.then_inc(gu_psum, 1)
                    pe.wait_ge(h_done, i * HC + HC)
                    wait_past(pe, acc_done, i)
                    for t in range(4):
                        for c in range(HC):
                            mm = pe.matmul(B[1][:, t * C:(t + 1) * C], hT[:, c, t * P:(t + 1) * P], w_d[:, c, :],
                                           start=(t == 0 and c == 0), stop=(c == HC - 1), skip_group_check=True)
                    mm.then_inc(y_psum, 1)

            @block.scalar
            def _(act):
                emit_exp(act, R)
                @repeat(act, HALVES)
                def _(i):
                    for c in range(HC):
                        act.wait_ge(gu_psum, i * HC + c + 1)
                        if c < 2:
                            wait_past(act, h_done, i * HC)
                        else:
                            wait_past(act, h_done, i * HC + c - 1)
                        act.activation(silu[c % 2][:], B[4 + 2 * (c % 2)], ACT.Silu).then_inc(silu_done, 1)

            @block.vector
            def _(dve):
                order = Order(dve, R.vec)
                emit_softmax_topk(dve, order, R, G.logits1)
                dve.memset(tiles_f[:], 0.0).then_inc(R.to_count, 1)
                dve.wait_ge(loaded, 4 * 16)
                emit_positions(dve, order, R, 1, before_bank, total_bank)
                order.done(dve.tensor_scalar(tiles_i[:], R.scanned[:, :, TILES - 1], float(P - 1), None, ALU.add))
                order.done(dve.tensor_scalar(tiles_i[:], tiles_i[:], 7, None, ALU.arith_shift_right))
                order.done(dve.tensor_copy(tiles_f[:], tiles_i[:]))
                order.done(dve.tensor_tensor_scan(ends[:], G.ones[:, 0:E1], tiles_f[:], 0.0, ALU.mult, ALU.add))
                order.done(dve.tensor_tensor(starts[:], ends[:], tiles_f[:], ALU.subtract))
                order.done(dve.tensor_scalar(starts[:], starts[:], float(P), None, ALU.mult))
                order.done(dve.tensor_tensor(R.position[:], R.position[:], starts[:, None, :].to_broadcast([P, TILES, E1]), ALU.add))
                for k in range(K1):
                    emit_pick(dve, order, R, k, R.position, R.row[:])
                    dve.tensor_copy(G.to_row1[:, :, k], R.row[:]).then_inc(rows_ready, 1)
                    dve.wait_ge(rows_ready, k + 1)
                for c in range(2):
                    order.done(dve.tensor_scalar(compared[:], ends[:], G.iota_p[:, c:c + 1], None, ALU.is_le, ALU.add,
                                                 accum_out=expert_f[:, c:c + 1]))
                dve.tensor_scalar(expert_f[:], expert_f[:], float(E1 - 1), None, ALU.min).then_inc(expert_done, 1)
                order.done(dve.tensor_reduce(R.total[:], R.top[:, :, 0:K1], AX.X, ALU.add))
                order.done(dve.tensor_scalar(R.total[:], R.total[:], 1e-12, None, ALU.max))
                order.done(dve.reciprocal(R.total[:], R.total[:]))
                order.done(dve.tensor_tensor(G.gate1[:], R.top[:, :, 0:K1], R.total[:, :, None].to_broadcast([P, TILES, K1]), ALU.mult))
                dve.wait_ge(expert_psum, 1)
                order.done(dve.tensor_copy(G.tile_expert[:], B[0][0:1, 0:2 * P]))
                @repeat(dve, HALVES)
                def _(i):
                    for c in range(HC):
                        dve.wait_ge(silu_done, i * HC + c + 1)
                        wait_past(dve, y_psum, i)
                        dve.tensor_tensor(hT[:, c, :], B[5 + 2 * (c % 2)], silu[c % 2][:], ALU.mult).then_inc(h_done, 1)
                    dve.wait_ge(y_psum, i + 1)
                    dve.tensor_tensor(G.acc[:, bass.ds(i * 4, 4), :], B[1].rearrange("p (t n) -> p t n", t=4),
                                      G.x_rows[:, bass.ds(i * 4, 4), :], ALU.add).then_inc(acc_done, 1)


def stage_experts1(nc, G, I):
    FT, RING = 4, 4
    GROUPS = TILES1 // FT
    with ExitStack() as ctx:
        M = Mem(nc, ctx)
        two = range(2)
        w_gu, w_d = G.w_gu, G.w_down
        rows = [M.sb(f"g_rows{v}", [P, FT, WIDE]) for v in range(RING)]
        place, place_done = M.sb("g_place", [P, TILES1], u32), M.sem("place_done")
        xT = [M.sb(f"g_xT{u}", [P, FT * P]) for u in two]
        silu, h = [M.sb(f"g_silu{u}", [P, FT, H1]) for u in two], [M.sb(f"g_h{u}", [P, FT, H1]) for u in two]
        hT, y = [M.sb(f"g_hT{u}", [P, FT * P]) for u in two], [M.sb(f"g_y{v}", [P, FT, C]) for v in range(RING)]
        here, kept = [M.sem(f"rows_here{v}") for v in range(RING)], [M.sem(f"y_kept{v}") for v in range(RING)]
        xT_psum, xT_done, gu_psum, silu_done, h_done = M.sem("xT_psum"), M.sem("xT_done"), M.sem("gu_psum"), M.sem("silu_done"), M.sem("h_done")
        hT_psum, hT_done, y_psum, y_done = M.sem("hT_psum"), M.sem("hT_done"), M.sem("y_psum"), M.sem("y_done")
        B = G.bank
        GU = lambda u: G.psum[:, 2 + 2 * u:4 + 2 * u, :].rearrange("p b (s x h) -> p (b s) x h", s=2, x=2)

        def rolled(engine, body, head, tail):
            assert (GROUPS - head - tail) % RING == 0
            for n in range(head):
                body(n, n % RING)
            with engine.Fori(0, (GROUPS - head - tail) // RING) as i:
                for r in range(RING):
                    body(i * RING + head + r, (head + r) % RING)
            for n in range(GROUPS - tail, GROUPS):
                body(n, n % RING)

        def uses(n, v, each):
            return n // RING * each if isinstance(n, int) else (n - v) * (each // RING)

        with nc.Block() as block:
            @block.sync
            def _(sp):
                def load(n, v):
                    if not isinstance(n, int) or n >= RING:
                        sp.wait_ge(xT_psum, n - RING + 1)
                        sp.wait_ge(place_done, n - RING + 1)
                    sp.dma_start(rows[v][:], G.sorted1[bass.ds(n * (FT * P), FT * P), :]
                                 .rearrange("(s p) c -> p s c", p=P)).then_inc(here[v], 16)
                rolled(sp, load, RING, 0)

            @block.tensor
            def _(pe):
                def load_experts(first, groups):
                    _, values = nc.values_load_multi_w_load_instructions(
                        G.tile_expert[0:1, bass.ds(first * FT, groups * FT)], engines=(mybir.EngineType.PE,),
                        min_val=0, max_val=E1 - 1, skip_runtime_bounds_check_because=
                        "stage_route1 counts experts up from 0 and takes the minimum with E1 - 1")
                    return values

                def emit_xT(n, v):
                    u = v % 2
                    pe.wait_ge(here[v], uses(n, v, 16) + 16)
                    if not isinstance(n, int) or n >= 2:
                        pe.wait_ge(xT_done, n - 1)
                    for s in range(FT):
                        mm = pe.transpose(B[u][:, s * P:(s + 1) * P], rows[v][:, s, 0:C], G.ident[:])
                    mm.then_inc(xT_psum, 1)

                def emit_gu(n, u, es):
                    pe.wait_ge(xT_done, n + 1)
                    if not isinstance(n, int) or n >= 2:
                        pe.wait_ge(h_done, n - 1)
                    for s in range(FT):
                        at = (s % 2) * 2 * H1
                        mm = pe.matmul(B[2 + 2 * u + s // 2][:, at:at + 2 * H1], xT[u][:, s * P:(s + 1) * P],
                                       w_gu[:, bass.ds(es[s] * (2 * H1), 2 * H1)], start=(s % 2 == 0), stop=True,
                                       skip_group_check=True)
                    mm.then_inc(gu_psum, 1)

                def emit_hT(n, u):
                    pe.wait_ge(h_done, n + 1)
                    if not isinstance(n, int) or n >= 1:
                        pe.wait_ge(hT_done, n)
                    for s in range(FT):
                        mm = pe.transpose(B[6][:, s * P:(s + 1) * P], h[u][:, s, :], G.ident[:])
                    mm.then_inc(hT_psum, 1)

                def emit_y(n, u, es):
                    pe.wait_ge(hT_done, n + 1)
                    if not isinstance(n, int) or n >= 1:
                        pe.wait_ge(y_done, n)
                    for s in range(FT):
                        mm = pe.matmul(B[7][:, s * C:(s + 1) * C], hT[u][:, s * P:(s + 1) * P],
                                       w_d[:, bass.ds(es[s] * C, C)], start=(s == 0), stop=True, skip_group_check=True)
                    mm.then_inc(y_psum, 1)

                def two_groups(n, v):
                    emit_xT(n + 1, v + 1)
                    es = load_experts(n - 2, 4)
                    emit_gu(n, 0, es[2 * FT:3 * FT])
                    emit_y(n - 2, 0, es[:FT])
                    emit_hT(n - 1, 1)
                    if not isinstance(n, int) or n + 2 < GROUPS:
                        emit_xT(n + 2, (v + 2) % RING)
                    emit_gu(n + 1, 1, es[3 * FT:])
                    emit_y(n - 1, 1, es[FT:2 * FT])
                    emit_hT(n, 0)
                    return es

                emit_xT(0, 0)
                es = load_experts(0, 2)
                emit_xT(1, 1)
                emit_gu(0, 0, es[:FT])
                emit_xT(2, 2)
                emit_gu(1, 1, es[FT:])
                emit_hT(0, 0)
                two_groups(2, 2)
                two_groups(4, 0)
                with pe.Fori(0, (GROUPS - 8) // RING) as i:
                    two_groups(i * RING + 6, 2)
                    two_groups(i * RING + 8, 0)
                es = two_groups(GROUPS - 2, 2)
                emit_y(GROUPS - 2, 0, es[2 * FT:3 * FT])
                emit_hT(GROUPS - 1, 1)
                emit_y(GROUPS - 1, 1, es[3 * FT:])

            @block.scalar
            def _(act):
                def copy_xT(n, u):
                    act.wait_ge(xT_psum, n + 1)
                    if not isinstance(n, int) or n >= 2:
                        act.wait_ge(gu_psum, n - 1)
                    act.activation(xT[u][:], B[u], ACT.Copy).then_inc(xT_done, 1)

                def body(n, v):
                    u = v % 2
                    if not isinstance(n, int) or n + 1 < GROUPS:
                        copy_xT(n + 1, 1 - u)
                    act.wait_ge(gu_psum, n + 1)
                    if not isinstance(n, int) or n >= 2:
                        act.wait_ge(h_done, n - 1)
                    act.activation(silu[u][:], GU(u)[:, :, 0, :], ACT.Silu).then_inc(silu_done, 1)
                copy_xT(0, 0)
                rolled(act, body, 2, 2)

            @block.vector
            def _(dve):
                def emit_hT(n, u):
                    dve.wait_ge(hT_psum, n + 1)
                    if not isinstance(n, int) or n >= 2:
                        dve.wait_ge(y_psum, n - 1)
                    dve.tensor_copy(hT[u][:], B[6]).then_inc(hT_done, 1)

                def emit_y(n, v):
                    dve.wait_ge(y_psum, n + 1)
                    if not isinstance(n, int) or n >= RING:
                        dve.wait_ge(kept[v], uses(n, v, 16 * FT))
                    dve.tensor_copy(y[v][:], B[7].rearrange("p (s c) -> p s c", c=C)).then_inc(y_done, 1)

                def take_place(n, v):
                    dve.wait_ge(here[v], uses(n, v, 16) + 16)
                    dve.tensor_copy(place[:, bass.ds(n * FT, FT)], rows[v][:, :, C]).then_inc(place_done, 1)

                def body(n, v):
                    u = v % 2
                    if not isinstance(n, int) or n + 1 < GROUPS:
                        take_place(n + 1, (v + 1) % RING)
                    if not isinstance(n, int) or n >= 2:
                        emit_y(n - 2, (v + 2) % RING)
                    dve.wait_ge(silu_done, n + 1)
                    if not isinstance(n, int) or n >= 2:
                        dve.wait_ge(hT_psum, n - 1)
                    dve.tensor_tensor(h[u][:], GU(u)[:, :, 1, :], silu[u][:], ALU.mult).then_inc(h_done, 1)
                    if not isinstance(n, int) or n >= 1:
                        emit_hT(n - 1, 1 - u)
                take_place(0, 0)
                rolled(dve, body, 6, 2)
                emit_y(GROUPS - 2, (GROUPS - 2) % RING)
                emit_hT(GROUPS - 1, 1)
                emit_y(GROUPS - 1, (GROUPS - 1) % RING)

            @block.gpsimd
            def _(pool):
                for n in range(GROUPS):
                    pool.wait_ge(y_done, n + 1)
                    for t in range(FT):
                        pool.indirect_dma_start(
                            out=G.expert_out1, out_offset=bass.IndirectOffsetOnAxis(ap=place[:, n * FT + t:n * FT + t + 1], axis=0),
                            in_=y[n % RING][:, t, :], in_offset=None, bounds_check=K1 * N - 1,
                            oob_is_err=False).then_inc(kept[n % RING], 16)
                for v in range(RING):
                    pool.wait_ge(kept[v], GROUPS // RING * FT * 16)


def stage_combine1(nc, G, I, out):
    NORMED = 3 * BATCH
    with ExitStack() as ctx:
        M = Mem(nc, ctx)
        two = range(2)
        got = [M.sb(f"f_got{u}", [P, TB, K1, C]) for u in two]
        y, x_new = M.sb("f_y", [P, TB, C]), [M.sb(f"f_new{u}", [P, TB, C]) for u in two]
        stats, mv = M.sb("f_stats", [P, TB, 6]), M.sb("f_mv", [P, TB, 2])
        var_eps, rstd = M.sb("f_var_eps", [P, TB]), M.sb("f_rstd", [P, TB])
        got_here = [M.sem(f"f_got_here{u}") for u in two]
        norm_done, stored = M.sem("norm_done"), [M.sem(f"stored{u}") for u in two]
        with nc.Block() as block:
            @block.gpsimd
            def _(pool):
                for b in range(BATCH):
                    pool.wait_ge(got_here[b % 2], (b // 2 + 1) * LOAD_PARTS * 16)
                    for k in range(K1 // 2, K1):
                        emit_product(pool, b, got[b % 2], G.gate1, k).then_inc(G.product_done, 1)
                    emit_norm_pool(pool, G, NORMED + b, var_eps, rstd)

            @block.vector
            def _(dve):
                order = Order(dve, G.steps, BATCH * (STEPS_A + STEPS_QKV + STEPS_PROJECTION))
                for b in range(BATCH):
                    dve.wait_ge(got_here[b % 2], (b // 2 + 1) * LOAD_PARTS * 16)
                    emit_combine(dve, order, b, got[b % 2], G.gate1, K1, G.acc[:, tiles(b), :], y[:],
                                 lambda: dve.wait_ge(G.product_done, BATCH + (b + 1) * (K1 // 2)))
                    if b >= 2:
                        dve.wait_ge(stored[b % 2], 16)
                    last = emit_norm_vector(dve, G, order, NORMED + b, lambda t: y[:, t, :], stats, mv, var_eps, rstd,
                                            lambda t: x_new[b % 2][:, t, :])
                    last.then_inc(norm_done, 1)

            @block.sync
            def _(sp):
                for b in two:
                    emit_combine_load(sp, b, got[b], got_here[b], G.expert_out1, K1)
                for b in range(BATCH):
                    sp.wait_ge(norm_done, b + 1)
                    sp.dma_start(out[b].rearrange("(t p) c -> p t c", p=P), x_new[b % 2][:]).then_inc(stored[b % 2], 16)
                    if b + 2 < BATCH:
                        emit_combine_load(sp, b + 2, got[b % 2], got_here[b % 2], G.expert_out1, K1)
                for u in two:
                    sp.wait_ge(stored[u], BATCH // 2 * 16)


class Shared:
    pass


def build(nc, I, out):
    G = Shared()
    with ExitStack() as ctx:
        M = Mem(nc, ctx)
        G.psum = ctx.enter_context(nc.psum_tensor("psum", [P, 8, HALF], fp32))
        G.bank = [G.psum[:, b, :] for b in range(8)]
        G.x_wide = M.sb("x_rows", [P, TILES, WIDE])
        G.x_rows = G.x_wide[:, :, 0:C]
        G.blank = M.sb("blank", [P, WIDE])
        G.ident, G.ones = M.sb("ident", [P, P]), M.sb("ones_sb", [P, P])
        G.ones_b, G.before_b = M.sb("ones_b", [P, P], bf16), M.sb("before_b", [P, P], bf16)
        G.place_of0, G.place_of1 = M.sb("place_of0", [P, K0, TILES]), M.sb("place_of1", [P, K1, TILES])
        G.var_ready, G.rstd_ready = M.sem("var_ready"), M.sem("rstd_ready")
        G.steps, G.placed, G.product_done = M.sem("steps"), M.sem("placed"), M.sem("product_done")
        G.cleared = M.sem("cleared")
        G.minus_half = M.sb("minus_half", [P, TILES])
        G.q_steps = nc.dram_tensor("q_steps", [STEPS, 3, GH * HD, SEQ], bf16, kind="Internal").ap()
        G.k_steps = nc.dram_tensor("k_steps", [STEPS, 3, GH * HD, SEQ], bf16, kind="Internal").ap()
        G.v_steps = nc.dram_tensor("v_steps", [STEPS, P, TB * GH * (HD + 1)], fp32, kind="Internal").ap()
        G.sorted0 = nc.dram_tensor("sorted0", [ROWS0, WIDE], fp32, kind="Internal").ap()
        G.sorted1 = nc.dram_tensor("sorted1", [ROWS1, WIDE], fp32, kind="Internal").ap()
        G.expert_out1 = nc.dram_tensor("expert_out1", [K1 * N, C], fp32, kind="Internal").ap()
        G.expert_out0 = nc.dram_tensor("expert_out0", [K0 * N, C], fp32, kind="Internal").ap()
        G.iota_e, G.iota_p = M.sb("iota_e", [P, E1]), M.sb("iota_p", [P, 2])
        G.iota_eb = M.sb("iota_eb", [P, E1], bf16)
        G.logits0 = M.sb("logits0", [P, TILES, E0])
        stage_setup(nc, G, I)
        stage_linear_attention(nc, G, I)
        G.gate0 = M.sb("gate0", [P, TILES, K0])
        G.to_row0 = M.sb("to_row0", [P, TILES, K0], u32)
        stage_route0(nc, G, I)
        stage_experts0(nc, G, I)
        G.att_steps = M.sb("att_steps", [P, STEPS * 2, 4, GH * HD])
        with ExitStack() as both:
            Operands(Mem(nc, both), G)
            stage_qkv(nc, G, I)
            stage_attention(nc, G, I)
        G.xT = M.sb("xT_all", [P, N])
        G.logits1 = M.sb("logits1", [P, TILES, E1])
        stage_projection(nc, G, I)
        G.gate1, G.to_row1 = M.sb("gate1", [P, TILES, K1]), M.sb("to_row1", [P, TILES, K1], u32)
        G.tile_expert = M.sb("tile_expert", [1, 2 * P], i32)
        G.acc = M.sb("acc", [P, TILES, C])
        G.w_gu, G.w_down = M.sb("w_gu", [P, E1 * 2 * H1]), M.sb("w_down", [P, E1 * C])
        stage_route1(nc, G, I)
        stage_experts1(nc, G, I)
        stage_combine1(nc, G, I, out)


def alibi_rows():
    bfloat = mybir.dt.np(bf16)
    dist = (SEQ - 1 - np.arange(SEQ)).astype(np.float32)
    value = -slopes()[:, None] * dist[None, :]
    parts = []
    for _ in range(3):
        parts.append(value.astype(bfloat))
        value = value - parts[-1].astype(np.float32)
    rows = np.stack(parts, 1).reshape(HEADS // GH, GH, 3, SEQ).transpose(0, 2, 1, 3).reshape(HEADS // GH, 3, GH * SEQ)
    rows = np.concatenate([rows, np.ones_like(rows)], 1)
    return np.tile(rows, (BATCH, 1, 1))


def layouts(a):
    f = {k: np.asarray(v) for k, v in a.items()}
    x = f["L0_attn_x"].reshape(N, C)
    head = np.arange(C) // HD
    gdh = np.arange(C).reshape(HEADS // GH, GH, HD).transpose(0, 2, 1).ravel()
    return {
        "x": x, "xT": x.T, "w_qkv": f["L0_attn_w_qkv"], "b_q_col": f["L0_attn_b_qkv"][:C, None],
        "b_kv": f["L0_attn_b_qkv"][None, C:], "w_proj": f["L0_attn_w_proj"], "b_proj": f["L0_attn_b_proj"][None],
        "Wr": f["L0_ffn_Wr"], "br": f["L0_ffn_br"][None],
        "W1": f["L0_ffn_W1"], "W2": f["L0_ffn_W2"].reshape(E0, H0 // P, P, C).transpose(0, 2, 1, 3),
        "b1": f["L0_ffn_b1"].reshape(E0, H0 // P, P).transpose(0, 2, 1), "b2": f["L0_ffn_b2"],
        "Wq": f["L1_attn_Wq"][:, gdh], "Wk": f["L1_attn_Wk"][:, gdh], "Wv": f["L1_attn_Wv"],
        "bq": f["L1_attn_bq"][gdh, None], "bk": f["L1_attn_bk"][gdh, None], "bv": f["L1_attn_bv"][None],
        "c_alibi": alibi_rows(),
        "Wo": f["L1_attn_Wo"], "bo": f["L1_attn_bo"][None],
        "Wr1": f["L1_ffn_router_w"].T, "br1": f["L1_ffn_router_bias"][None],
        "sg": f["L1_ffn_sgate_w"].T, "su": f["L1_ffn_sup_w"].T,
        "sd": f["L1_ffn_sdown_w"].T.reshape(HS // P, P, C).transpose(1, 0, 2),
        "gu": np.stack([f["L1_ffn_gate_w"], f["L1_ffn_up_w"]], 1).transpose(3, 0, 1, 2).reshape(C, E1 * 2 * H1),
        "down": f["L1_ffn_down_w"].transpose(2, 0, 1).reshape(H1, E1 * C),
        "c_same_expert": (np.arange(P)[:, None] % E0 == np.arange(P)[None, :] % E0).astype(np.float32),
        "c_first_of": (np.arange(P)[:, None] == np.arange(E0)[None, :]).astype(np.float32),
        "c_goes_on": (np.arange(E1 * TILES) % TILES > 0).astype(np.float32)[None],
        "c_head_mask": np.concatenate([head[:, None] == head[None, :], head[:, None] == np.arange(HEADS)[None, :]],
                                      1).astype(np.float32),
    }


def kernel(**inputs):
    import concourse.bacc as bacc
    from concourse.bass_utils import run_bass_kernel_spmd

    nc = bacc.Bacc("TRN2", target_bir_lowering=False, num_devices=1)
    arrays = {f"in_{k}": np.ascontiguousarray(v) for k, v in layouts(inputs).items()}
    I = {k[3:]: nc.dram_tensor(k, a.shape, mybir.dt.from_np(a.dtype), kind="ExternalInput").ap()
         for k, a in arrays.items()}
    out = nc.dram_tensor("out_x", (BATCH, SEQ, C), fp32, kind="ExternalOutput").ap()
    build(nc, I, out)
    result = run_bass_kernel_spmd(nc, [arrays], core_ids=[0])
    return result.results[0]["out_x"]
```
